# Optimizing a Trainium2 kernel written in Bass

```python
import numpy as np
import jax
import jax.numpy as jnp

def _softmax(x, axis=-1):
    return jax.nn.softmax(x, axis=axis)

def _gelu(x):
    return jax.nn.gelu(x, approximate=True)

def _silu(x):
    return jax.nn.silu(x)

def _sigmoid(x):
    return jax.nn.sigmoid(x)

def _layernorm(x, axis=-1, eps=1e-05):
    m = jnp.mean(x, axis=axis, keepdims=True)
    v = jnp.var(x, axis=axis, keepdims=True)
    return (x - m) / jnp.sqrt(v + eps)

def _scatter_add(tgt, idx, src, axis=0):
    return tgt.at[idx].add(src)

def _segment_sum(src, seg, n):
    return jax.ops.segment_sum(src, seg, n)
kernel_name = 'mk_gnn_resnorm_d4_gnn_r8_d182bb'

def setup_inputs(seed: int=0):
    np.random.seed(seed)
    _w = jnp.asarray

    def _rec_inputs():
        import jax
        import jax.numpy as jnp
        _gk = jax.random.key(seed)
        x = -0.0003713 + 1 * jax.random.normal(jax.random.fold_in(_gk, 1), (12500, 128), jnp.float32)
        _s = jax.random.randint(jax.random.fold_in(_gk, 2), (100000,), 0, 12500, jnp.int32)
        _d = jax.random.randint(jax.random.fold_in(_gk, 3), (100000,), 0, 12500, jnp.int32)
        _loop = jnp.arange(12500, dtype=jnp.int32)
        src = jnp.concatenate([_s, _d, _loop])
        dst = jnp.concatenate([_d, _s, _loop])
        _o = jnp.argsort(dst, stable=True)
        src = src[_o]
        dst = dst[_o]
        edge_attr_50 = 0.000154925 + 1.00009 * jax.random.normal(jax.random.fold_in(_gk, 13), (212500, 50), jnp.float32)
        edge_weight = jax.random.uniform(jax.random.fold_in(_gk, 15), (212500,), jnp.float32, 0.0, 0.999998)
        return (x, src, dst, edge_attr_50, edge_weight)
    x, src, dst, edge_attr_50, edge_weight = _rec_inputs()

    def _L0_gnn_setup():
        import jax, jax.numpy as jnp
        import numpy as np
        N_NODES = 12500
        N_EDGES = 200000
        D_IN = 128
        D_OUT = 128
        key = jax.random.key(seed)
        k1, k2, k3, k4, k5 = jax.random.split(key, 5)
        feature = jax.random.normal(k1, (N_NODES, D_IN), dtype=jnp.float32)
        src = jax.random.randint(k2, (N_EDGES,), 0, N_NODES, dtype=jnp.int32)
        dst = jax.random.randint(k3, (N_EDGES,), 0, N_NODES, dtype=jnp.int32)
        bound = float(np.sqrt(6.0 / (D_IN + D_OUT)))
        W_self = jax.random.uniform(k4, (D_IN, D_OUT), jnp.float32, -bound, bound)
        W_inter = jax.random.uniform(k5, (D_IN, D_OUT), jnp.float32, -bound, bound)
        return {'feature': feature, 'src': src, 'dst': dst, 'W_self': W_self, 'W_inter': W_inter}
    _L0_gnn_all = _L0_gnn_setup()
    _L0_gnn_in = {k: v for k, v in _L0_gnn_all.items() if k in ('W_self', 'W_inter')}
    del _L0_gnn_all

    def _L1_gnn_setup():
        import jax, jax.numpy as jnp
        import numpy as np
        NUM_NODES = 6250
        NUM_EDGES = 75000
        IN_DIM = 128
        OUT_DIM = 128
        key = jax.random.key(seed)
        k1, k2, k3, k4, k5 = jax.random.split(key, 5)
        x = jax.random.normal(k1, (NUM_NODES, IN_DIM), dtype=jnp.float32)
        edge_index = jax.random.randint(k2, (2, NUM_EDGES), 0, NUM_NODES, dtype=jnp.int64)
        edge_weight = jax.random.uniform(k3, (NUM_EDGES,), dtype=jnp.float32)
        W = jax.random.normal(k4, (OUT_DIM, IN_DIM), dtype=jnp.float32) * (1.0 / np.sqrt(IN_DIM))
        b = jax.random.normal(k5, (OUT_DIM,), dtype=jnp.float32) * 0.01
        return {'x': x, 'edge_index': edge_index, 'edge_weight': edge_weight, 'W': W, 'b': b}
    _L1_gnn_all = _L1_gnn_setup()
    _L1_gnn_in = {k: v for k, v in _L1_gnn_all.items() if k in ('W', 'b')}
    del _L1_gnn_all

    def _L2_gnn_setup():
        import jax, jax.numpy as jnp
        import numpy as np
        NEG_SLOPE = 0.2
        EPS = 1e-16
        key = jax.random.key(seed)
        k1, k2, k3, k4, k5 = jax.random.split(key, 5)
        N, E, D_in, H, C = (12500, 200000, 128, 4, 32)
        x = jax.random.normal(k1, (N, D_in), dtype=jnp.float32)
        edge_index = jax.random.randint(k2, (2, E), 0, N, dtype=jnp.int64)
        W = jax.random.normal(k3, (D_in, H * C), dtype=jnp.float32) * 0.05
        att_src = jax.random.normal(k4, (H, C), dtype=jnp.float32) * 0.05
        att_dst = jax.random.normal(k5, (H, C), dtype=jnp.float32) * 0.05
        bias = jnp.zeros((H * C,), dtype=jnp.float32)
        return {'x': x, 'edge_index': edge_index, 'W': W, 'att_src': att_src, 'att_dst': att_dst, 'bias': bias}
    _L2_gnn_all = _L2_gnn_setup()
    _L2_gnn_in = {k: v for k, v in _L2_gnn_all.items() if k in ('W', 'att_src', 'att_dst', 'bias')}
    del _L2_gnn_all

    def _L3_gnn_setup():
        import jax, jax.numpy as jnp
        import numpy as np
        from math import pi as PI
        HIDDEN = 128
        NUM_GAUSS = 50
        NUM_FILT = 128
        CUTOFF = 10.0
        N_CONV = 2
        NUM_STATE = 2
        N_NODES = 6250
        N_EDGES = 100000
        N_GRAPHS = 256

        def ssp(x):
            return jax.nn.softplus(x) - jnp.log(2.0).astype(x.dtype)

        def _xavier(key, shape):
            fan_in, fan_out = (shape[-2], shape[-1])
            lim = np.sqrt(6.0 / (fan_in + fan_out))
            return jax.random.uniform(key, shape, jnp.float32, -lim, lim)
        key = jax.random.key(seed)
        ks = jax.random.split(key, 20)
        h = jax.random.normal(ks[0], (N_NODES, HIDDEN), jnp.float32)
        edge_index = jax.random.randint(ks[1], (2, N_EDGES), 0, N_NODES, jnp.int32)
        edge_weight = jax.random.uniform(ks[2], (N_EDGES,), jnp.float32) * CUTOFF
        edge_attr = jax.random.normal(ks[3], (N_EDGES, NUM_GAUSS), jnp.float32)
        state_attr = jax.random.normal(ks[4], (N_GRAPHS, NUM_STATE), jnp.float32)
        batch = jnp.sort(jax.random.randint(ks[5], (N_NODES,), 0, N_GRAPHS, jnp.int32))
        L = N_CONV
        params = {'lin1_w': _xavier(ks[6], (L, HIDDEN + NUM_STATE, HIDDEN)), 'lin1_b': jnp.zeros((L, HIDDEN), jnp.float32), 'mlp1_w': _xavier(ks[7], (L, NUM_GAUSS, NUM_FILT)), 'mlp1_b': jnp.zeros((L, NUM_FILT), jnp.float32), 'mlp2_w': _xavier(ks[8], (L, NUM_FILT, NUM_FILT)), 'mlp2_b': jnp.zeros((L, NUM_FILT), jnp.float32), 'conv1_w': _xavier(ks[9], (L, HIDDEN, NUM_FILT)), 'conv2_w': _xavier(ks[10], (L, NUM_FILT, HIDDEN)), 'conv2_b': jnp.zeros((L, HIDDEN), jnp.float32), 'blin_w': _xavier(ks[11], (L, HIDDEN, HIDDEN)), 'blin_b': jnp.zeros((L, HIDDEN), jnp.float32), 'out_w': _xavier(ks[12], (HIDDEN, NUM_FILT)), 'out_b': jnp.zeros((NUM_FILT,), jnp.float32)}
        return dict(h=h, edge_index=edge_index, edge_weight=edge_weight, edge_attr=edge_attr, state_attr=state_attr, batch=batch, **params)
    _L3_gnn_all = _L3_gnn_setup()
    _L3_gnn_in = {k: v for k, v in _L3_gnn_all.items() if k in ('state_attr', 'lin1_w', 'lin1_b', 'mlp1_w', 'mlp1_b', 'mlp2_w', 'mlp2_b', 'conv1_w', 'conv2_w', 'conv2_b', 'blin_w', 'blin_b', 'out_w', 'out_b')}
    del _L3_gnn_all
    return {'x': x, 'src': src, 'dst': dst, 'edge_attr_50': edge_attr_50, 'edge_weight': edge_weight, 'L0_gnn_W_self': _L0_gnn_in['W_self'], 'L0_gnn_W_inter': _L0_gnn_in['W_inter'], 'L1_gnn_W': _L1_gnn_in['W'], 'L1_gnn_b': _L1_gnn_in['b'], 'L2_gnn_W': _L2_gnn_in['W'], 'L2_gnn_att_src': _L2_gnn_in['att_src'], 'L2_gnn_att_dst': _L2_gnn_in['att_dst'], 'L2_gnn_bias': _L2_gnn_in['bias'], 'L3_gnn_state_attr': _L3_gnn_in['state_attr'], 'L3_gnn_lin1_w': _L3_gnn_in['lin1_w'], 'L3_gnn_lin1_b': _L3_gnn_in['lin1_b'], 'L3_gnn_mlp1_w': _L3_gnn_in['mlp1_w'], 'L3_gnn_mlp1_b': _L3_gnn_in['mlp1_b'], 'L3_gnn_mlp2_w': _L3_gnn_in['mlp2_w'], 'L3_gnn_mlp2_b': _L3_gnn_in['mlp2_b'], 'L3_gnn_conv1_w': _L3_gnn_in['conv1_w'], 'L3_gnn_conv2_w': _L3_gnn_in['conv2_w'], 'L3_gnn_conv2_b': _L3_gnn_in['conv2_b'], 'L3_gnn_blin_w': _L3_gnn_in['blin_w'], 'L3_gnn_blin_b': _L3_gnn_in['blin_b'], 'L3_gnn_out_w': _L3_gnn_in['out_w'], 'L3_gnn_out_b': _L3_gnn_in['out_b']}

def reference(x, src, dst, edge_attr_50, edge_weight, L0_gnn_W_self, L0_gnn_W_inter, L1_gnn_W, L1_gnn_b, L2_gnn_W, L2_gnn_att_src, L2_gnn_att_dst, L2_gnn_bias, L3_gnn_state_attr, L3_gnn_lin1_w, L3_gnn_lin1_b, L3_gnn_mlp1_w, L3_gnn_mlp1_b, L3_gnn_mlp2_w, L3_gnn_mlp2_b, L3_gnn_conv1_w, L3_gnn_conv2_w, L3_gnn_conv2_b, L3_gnn_blin_w, L3_gnn_blin_b, L3_gnn_out_w, L3_gnn_out_b):
    import jax
    import jax.numpy as jnp

    def _L0_gnn_ref(feature, src, dst, W_self, W_inter):
        import jax, jax.numpy as jnp
        import numpy as np
        N_NODES = 12500
        N_EDGES = 200000
        D_IN = 128
        D_OUT = 128
        n = feature.shape[0]
        ones = jnp.ones_like(src, dtype=jnp.float32)
        out_deg = jnp.clip(jax.ops.segment_sum(ones, src, num_segments=n), 1.0)
        in_deg = jnp.clip(jax.ops.segment_sum(ones, dst, num_segments=n), 1.0)
        h = feature * (out_deg ** (-0.5))[:, None]
        h_self = jax.ops.segment_sum(h[src], dst, num_segments=n)
        m_inter = h[src] * feature[dst]
        h_inter = jax.ops.segment_sum(m_inter, dst, num_segments=n)
        rst = h_self @ W_self + h_inter @ W_inter
        rst = rst * (in_deg ** (-0.5))[:, None]
        rst = rst + feature @ W_self
        return rst

    def _L1_gnn_ref(x, edge_index, edge_weight, W, b):
        import jax, jax.numpy as jnp
        import numpy as np
        NUM_NODES = 6250
        NUM_EDGES = 75000
        IN_DIM = 128
        OUT_DIM = 128
        num_nodes = x.shape[0]
        loop = jnp.arange(num_nodes, dtype=edge_index.dtype)
        src = jnp.concatenate([edge_index[0], loop])
        tgt = jnp.concatenate([edge_index[1], loop])
        w = jnp.concatenate([edge_weight, jnp.ones((num_nodes,), dtype=edge_weight.dtype)])
        deg = jax.ops.segment_sum(w, src, num_segments=num_nodes)
        dinv = 1.0 / jnp.sqrt(deg)
        w_norm = w * dinv[src] * dinv[tgt]
        msg = x[src] * w_norm[:, None]
        agg = jax.ops.segment_sum(msg, tgt, num_segments=num_nodes)
        return agg @ W.T + b

    def _L2_gnn_ref(x, edge_index, W, att_src, att_dst, bias):
        import jax, jax.numpy as jnp
        import numpy as np
        NEG_SLOPE = 0.2
        EPS = 1e-16
        N = x.shape[0]
        H, C = att_src.shape
        loop = jnp.arange(N, dtype=edge_index.dtype)
        src = jnp.concatenate([edge_index[0], loop])
        dst = jnp.concatenate([edge_index[1], loop])
        h = (x @ W).reshape(N, H, C)
        a_src = jnp.einsum('nhc,hc->nh', h, att_src)
        a_dst = jnp.einsum('nhc,hc->nh', h, att_dst)
        e = jax.nn.leaky_relu(a_src[src] + a_dst[dst], NEG_SLOPE)
        m = jax.ops.segment_max(e, dst, num_segments=N)
        m = jnp.where(jnp.isfinite(m), m, 0.0)
        ex = jnp.exp(e - m[dst])
        s = jax.ops.segment_sum(ex, dst, num_segments=N)
        alpha = ex / (s[dst] + EPS)
        msgs = h[src] * alpha[:, :, None]
        out = jax.ops.segment_sum(msgs, dst, num_segments=N)
        return out.reshape(N, H * C) + bias

    def _L3_gnn_ref(h, edge_index, edge_weight, edge_attr, state_attr, batch, lin1_w, lin1_b, mlp1_w, mlp1_b, mlp2_w, mlp2_b, conv1_w, conv2_w, conv2_b, blin_w, blin_b, out_w, out_b):
        import jax, jax.numpy as jnp
        import numpy as np
        from math import pi as PI
        HIDDEN = 128
        NUM_GAUSS = 50
        NUM_FILT = 128
        CUTOFF = 10.0
        N_CONV = 2
        NUM_STATE = 2
        N_NODES = 6250
        N_EDGES = 100000
        N_GRAPHS = 256

        def ssp(x):
            return jax.nn.softplus(x) - jnp.log(2.0).astype(x.dtype)

        def _xavier(key, shape):
            fan_in, fan_out = (shape[-2], shape[-1])
            lim = np.sqrt(6.0 / (fan_in + fan_out))
            return jax.random.uniform(key, shape, jnp.float32, -lim, lim)
        src, dst = (edge_index[0], edge_index[1])
        N = h.shape[0]
        G = state_attr.shape[0]
        C = 0.5 * (jnp.cos(edge_weight * (PI / CUTOFF)) + 1.0)
        counts = jax.ops.segment_sum(jnp.ones((N,), h.dtype), batch, num_segments=G)
        counts = jnp.maximum(counts, 1.0)[:, None]
        sa = state_attr
        for l in range(N_CONV):
            hcat = jnp.concatenate([sa[batch], h], axis=1)
            h = hcat @ lin1_w[l] + lin1_b[l]
            W = ssp(edge_attr @ mlp1_w[l] + mlp1_b[l]) @ mlp2_w[l] + mlp2_b[l]
            W = W * C[:, None]
            xm = h @ conv1_w[l]
            msg = xm[src] * W
            agg = jax.ops.segment_sum(msg, dst, num_segments=N)
            xc = agg @ conv2_w[l] + conv2_b[l]
            xc = ssp(xc) @ blin_w[l] + blin_b[l]
            h = h + xc
            mean = jax.ops.segment_sum(h, batch, num_segments=G) / counts
            s = jnp.sum(mean, axis=1, keepdims=True)
            sa = jnp.broadcast_to(s, (G, NUM_STATE))
        return jax.nn.relu(h @ out_w + out_b)
    edge_index = jnp.stack([src, dst])
    batch0 = jnp.zeros((12500,), jnp.int32)
    x = _layernorm(x + _L0_gnn_ref(x, src, dst, L0_gnn_W_self, L0_gnn_W_inter), axis=-1)
    x = _layernorm(x + _L1_gnn_ref(x, edge_index, edge_weight, L1_gnn_W, L1_gnn_b), axis=-1)
    x = _layernorm(x + _L2_gnn_ref(x, edge_index, L2_gnn_W, L2_gnn_att_src, L2_gnn_att_dst, L2_gnn_bias), axis=-1)
    x = _layernorm(x + _L3_gnn_ref(x, edge_index, edge_weight, edge_attr_50, L3_gnn_state_attr, batch0, L3_gnn_lin1_w, L3_gnn_lin1_b, L3_gnn_mlp1_w, L3_gnn_mlp1_b, L3_gnn_mlp2_w, L3_gnn_mlp2_b, L3_gnn_conv1_w, L3_gnn_conv2_w, L3_gnn_conv2_b, L3_gnn_blin_w, L3_gnn_blin_b, L3_gnn_out_w, L3_gnn_out_b), axis=-1)
    return x

_drawn_inputs = setup_inputs


def setup_inputs(seed=0):
    import zlib

    import numpy as np

    out = dict(_drawn_inputs(seed))
    spreads = {'L2_gnn_bias': (0.0, 0.1),
     'L3_gnn_lin1_b': (0.0, 0.1),
     'L3_gnn_mlp1_b': (0.0, 0.1),
     'L3_gnn_mlp2_b': (0.0, 0.1),
     'L3_gnn_conv2_b': (0.0, 0.1),
     'L3_gnn_blin_b': (0.0, 0.1),
     'L3_gnn_out_b': (0.0, 0.1)}
    factors = {'L1_gnn_b': 3.47, 'L2_gnn_att_dst': 8.0}
    for name, (base, spread) in spreads.items():
        noise = np.random.default_rng([zlib.crc32(name.encode()), seed]).standard_normal(out[name].shape)
        drawn = base * np.exp(spread * noise) if base else spread * noise
        out[name] = jnp.asarray(drawn.astype(out[name].dtype))
    for name, factor in factors.items():
        out[name] = (out[name] * factor).astype(out[name].dtype)
    return out
```

```python
from contextlib import ExitStack

import numpy as np
import concourse.bass as bass
from concourse import mybir

F32 = mybir.dt.float32
BF16 = mybir.dt.bfloat16
I32 = mybir.dt.int32
ALU = mybir.AluOpType
ACT = mybir.ActivationFunctionType
AX = mybir.AxisListType.X

P = 128
D = 128
G = 8
GE = G * P
CT = 4
CH = CT * P
HEADS = 4
HD = D // HEADS
EPS = 1e-5
ROW2 = D + HEADS
RESET = -1.0e30
PI = float(np.pi)
LN2 = float(np.log(2.0))


def ceil_to(n, k):
    return -(-n // k) * k


class Sizes:

    def __init__(self, nodes, edges, gauss):
        self.nodes, self.edges, self.gauss = nodes, edges, gauss
        self.groups = ceil_to(-(-edges // GE), 2)
        self.half = self.groups // 2
        self.tiles = self.groups * G
        self.padded = ceil_to(nodes + 1, CH)
        self.chunks = self.padded // CH
        self.node_tiles = self.padded // P
        self.cols = self.padded + P


class Chain:

    def __init__(self, eng, sem, base, per=None):
        self.eng, self.sem, self.base, self.per, self.n = eng, sem, base, per, 0

    def go(self, ins):
        self.n += 1
        ins.then_inc(self.sem, 1)

    def wait(self):
        self.eng.wait_ge(self.sem, self.base + self.n)

    def __call__(self, ins):
        self.go(ins)
        self.wait()

    def done(self):
        assert self.per is None or self.n == self.per, self.n


class Phase(ExitStack):

    def __init__(self, nc):
        super().__init__()
        self.nc, self.sems = nc, []

    def semaphore(self, name):
        self.sems.append(self.nc.alloc_semaphore(name))
        return self.sems[-1]

    def __exit__(self, *what):
        super().__exit__(*what)
        if what[0] is None:
            self.nc.clear_and_free_semaphores(self.sems)
            self.nc.all_engine_barrier()


def bc(ap, n):
    return ap.unsqueeze(2).to_broadcast([ap.shape[0], ap.shape[1], n])


def cols(t, start, size):
    return t[:, bass.ds(start, size)]



def prepare(nc, z, m, ins):
    E, HG, NT = z.edges, z.half, z.tiles
    full = E // GE - HG
    rest = E % GE
    with Phase(nc) as ctx:
        def sb(name, shape, dt=F32):
            return ctx.enter_context(nc.sbuf_tensor(name, shape, dt))

        src_i = sb("src_i", [HG, 2 * GE], I32)
        dst_i = sb("dst_i", [HG, 2 * GE], I32)
        src_f = sb("src_f", [HG, 2 * GE])
        dst_f = sb("dst_f", [HG, 2 * GE])
        w_e = sb("w_e", [HG, 2 * GE])
        loc = sb("loc_e", [HG, 2 * GE])
        last = sb("last_e", [HG, 2 * GE])
        change = sb("change_e", [HG, 2 * GE])
        lane_i = sb("lane_i", [P, P], I32)
        lo = sb("lo_t", [HG, 16])
        hi = sb("hi_t", [HG, 16])
        bad = sb("bad_t", [HG, 16])
        tmp = sb("tmp_t", [HG, 16])
        badg = sb("bad_g", [HG, 2])
        base_i = sb("base_i", [HG, 16], I32)
        lohi_i = sb("lohi_i", [P, NT], I32)
        zeros = sb("zeros", [P, D])
        ps = [ctx.enter_context(nc.psum_tensor(f"prep_ps{i}", [P, 4, P], F32)) for i in range(4)]

        sem = {n: ctx.semaphore(n) for n in (
            "edges_in", "padded", "consts", "ident_zero", "prep_step", "moved", "copied", "spilled",
            "rows_padded", "tables", "weights_in", "lanes")}

        def whole(t):
            return t[:, :].rearrange("p (h n) -> p h n", h=2)

        tile3 = lambda t: t[:, :].rearrange("p (t e) -> p t e", e=P)
        block = ctx.enter_context(nc.Block())
        moves = [(src_f, m.src_idx), (dst_f, m.dst_idx), (loc, m.loc), (last, m.last), (w_e, m.w)]
        n_edge_dmas = 3 * (1 + (full > 0) + (rest > 0))

        @block.sync
        def _(sp):
            sp.wait_ge(sem["padded"], 4)
            for name, t in (("src", src_i), ("dst", dst_i), ("edge_weight", w_e)):
                a = ins[name]
                sp.dma_start(t[:, 0:GE], a[0:HG * GE].rearrange("(p n) -> p n", n=GE)).then_inc(sem["edges_in"], 16)
                if full:
                    sp.dma_start(t[0:full, GE:2 * GE], a[HG * GE:(HG + full) * GE].rearrange("(p n) -> p n", n=GE)).then_inc(sem["edges_in"], 16)
                if rest:
                    at = (HG + full) * GE
                    sp.dma_start(t[full:full + 1, GE:GE + rest], a[at:E].rearrange("(p n) -> p n", p=1)).then_inc(sem["edges_in"], 16)
            n = 0
            sp.dma_start(m.x0[0:z.nodes, :], ins["x"]).then_inc(sem["rows_padded"], 16)
            n += 1
            for at in range(z.nodes, z.padded, P):
                k = min(P, z.padded - at)
                sp.dma_start(m.x0[at:at + k, :], zeros[0:k, :]).then_inc(sem["rows_padded"], 16)
                n += 1
            sp.wait_ge(sem["edges_in"], 16 * n_edge_dmas)
            for h in range(2):
                sp.dma_start(m.dst_pad[h * HG:(h + 1) * HG, :], dst_i[:, h * GE:(h + 1) * GE]).then_inc(sem["spilled"], 16)
            sp.wait_ge(sem["tables"], 2)
            for h in range(2):
                for r_ in range(HEADS):
                    sp.dma_start(m.resets4[h * HG:(h + 1) * HG, :].rearrange("g (k r e) -> g k r e", r=HEADS, e=P)[:, :, r_, :],
                                 change[:, h * GE:(h + 1) * GE].rearrange("g (k e) -> g k e", e=P)).then_inc(sem["spilled"], 16)
                sp.dma_start(m.bases[h * HG:(h + 1) * HG, :], base_i[:, h * G:(h + 1) * G]).then_inc(sem["spilled"], 16)
            n_spilled = 2 * (1 + HEADS + 1)
            sp.wait_ge(sem["spilled"], 16 * n_spilled)
            sp.dma_start(m.base_row[:, :], m.bases[:, :].rearrange("g k -> (g k)").rearrange("(o n) -> o n", o=1)).then_inc(sem["spilled"], 16)
            sp.wait_ge(sem["spilled"], 16 * (n_spilled + 1))
            sp.wait_ge(sem["rows_padded"], 16 * n)

        @block.gpsimd
        def _(pool):
            nc.gpsimd.memset(m.ident[:, :], 0.0).then_inc(sem["ident_zero"], 1)
            pool.wait_ge(sem["ident_zero"], 1)
            nc.gpsimd.affine_select(out=m.ident[:, :], in_=m.ident[:, :], compare_op=ALU.not_equal, fill=1.0,
                                    base=0, pattern=[[-1, P]], channel_multiplier=1).then_inc(sem["consts"], 1)
            nc.gpsimd.iota(lane_i[:, :], pattern=[[1, P]], base=0, channel_multiplier=0).then_inc(sem["consts"], 1)

        @block.tensor
        def _(pe):
            pe.wait_ge(sem["consts"], 1)
            pe.wait_ge(sem["tables"], 2)
            i = 0
            for src, _ in moves:
                for h in range(2):
                    for q in range(2):
                        if i >= 4:
                            pe.wait_ge(sem["copied"], i - 3)
                        for k in range(4):
                            at = h * GE + (q * 4 + k) * P
                            last_one = nc.tensor.transpose(ps[i % 4][:, k, 0:HG], src[:, at:at + P], m.ident[0:HG, 0:HG])
                        last_one.then_inc(sem["moved"], 1)
                        i += 1

        @block.vector
        def _(v):
            step = Chain(v, sem["prep_step"], 0)
            nc.vector.memset(src_i[:, :], z.nodes).then_inc(sem["padded"], 1)
            nc.vector.memset(dst_i[:, :], z.nodes).then_inc(sem["padded"], 1)
            nc.vector.memset(w_e[:, :], 0.0).then_inc(sem["padded"], 1)
            nc.vector.memset(zeros[:, :], 0.0).then_inc(sem["padded"], 1)
            step(nc.vector.memset(m.ones[:, :], 1.0))
            v.wait_ge(sem["consts"], 2)
            step(nc.vector.tensor_copy(m.lane[:, :], lane_i[:, :]))
            step(nc.vector.tensor_copy(m.lane_bf[:, :], lane_i[:, :]))
            v.wait_ge(sem["edges_in"], 16 * n_edge_dmas)
            step(nc.vector.tensor_copy(src_f[:, :], src_i[:, :]))
            step(nc.vector.tensor_copy(dst_f[:, :], dst_i[:, :]))
            d3, l3, c3, e3 = tile3(dst_f), tile3(loc), tile3(change), tile3(last)
            step(nc.vector.tensor_reduce(lo[:, :], d3, AX, ALU.min))
            step(nc.vector.tensor_reduce(hi[:, :], d3, AX, ALU.max))
            step(nc.vector.tensor_tensor(c3[:, :, 1:P], d3[:, :, 1:P], d3[:, :, 0:P - 1], ALU.subtract))
            step(nc.vector.tensor_reduce(tmp[:, :], c3[:, :, 1:P], AX, ALU.min))
            step(nc.vector.tensor_scalar(tmp[:, :], tmp[:, :], 0.0, None, ALU.is_lt))
            step(nc.vector.tensor_tensor(hi[:, :], hi[:, :], lo[:, :], ALU.subtract))
            step(nc.vector.tensor_scalar(hi[:, :], hi[:, :], float(P), None, ALU.is_ge))
            step(nc.vector.tensor_tensor(hi[:, :], hi[:, :], tmp[:, :], ALU.max))
            step(nc.vector.tensor_reduce(badg[:, :], hi[:, :].rearrange("p (h k) -> p h k", h=2), AX, ALU.max))
            step(nc.vector.tensor_copy(bad[:, :].rearrange("p (h k) -> p h k", h=2), bc(badg[:, :], G)))
            step(nc.vector.tensor_tensor(l3, d3, bc(lo[:, :], P), ALU.subtract))
            step(nc.vector.tensor_tensor(c3, m.lane[0:HG, :].unsqueeze(1).to_broadcast([HG, 16, P]), l3, ALU.subtract))
            step(nc.vector.tensor_tensor(c3, c3, bc(bad[:, :], P), ALU.mult))
            step(nc.vector.tensor_tensor(l3, l3, c3, ALU.add))
            step(nc.vector.tensor_scalar(tmp[:, :], lo[:, :], 1.0, None, ALU.add))
            step(nc.vector.tensor_tensor(tmp[:, :], tmp[:, :], bad[:, :], ALU.mult))
            step(nc.vector.tensor_tensor(tmp[:, :], lo[:, :], tmp[:, :], ALU.subtract))
            step(nc.vector.tensor_copy(base_i[:, :], tmp[:, :]))
            step(nc.vector.tensor_tensor(c3[:, :, 1:P], l3[:, :, 1:P], l3[:, :, 0:P - 1], ALU.not_equal))
            step(nc.vector.memset(c3[:, :, 0:1], 1.0))
            step(nc.vector.tensor_scalar(e3[:, :, 0:P - 1], l3[:, :, 0:P - 1], 1.0, None, ALU.add))
            step(nc.vector.tensor_tensor(e3[:, :, 0:P - 1], e3[:, :, 0:P - 1], c3[:, :, 1:P], ALU.mult))
            step(nc.vector.tensor_scalar(e3[:, :, 0:P - 1], e3[:, :, 0:P - 1], -1.0, None, ALU.add))
            step(nc.vector.tensor_copy(e3[:, :, P - 1:P], l3[:, :, P - 1:P]))
            nc.vector.tensor_scalar(change[:, :], change[:, :], RESET, None, ALU.mult).then_inc(sem["tables"], 1)
            v.wait_ge(sem["tables"], 1)
            nc.vector.memset(m.edge_zero[:, :], 0.0).then_inc(sem["tables"], 1)
            i = 0
            for _, table in moves:
                for h in range(2):
                    for q in range(2):
                        v.wait_ge(sem["moved"], i + 1)
                        out = table[:, 0:NT].rearrange("p (h g k) -> p h k g", h=2, k=G)[:, h, q * 4:q * 4 + 4, :]
                        nc.vector.tensor_copy(out, ps[i % 4][:, :, 0:HG]).then_inc(sem["copied"], 1)
                        i += 1
            v.wait_ge(sem["copied"], i)
            for idx, low, high in ((m.src_idx, m.src_lo, m.src_hi), (m.dst_idx, m.dst_lo, m.dst_hi)):
                step(nc.vector.tensor_scalar(lohi_i[:, :], idx[:, 0:NT], P - 1, None, ALU.bitwise_and))
                step(nc.vector.tensor_copy(low[:, :], lohi_i[:, :]))
                step(nc.vector.tensor_scalar(lohi_i[:, :], idx[:, 0:NT], 7, None, ALU.logical_shift_right))
                step(nc.vector.tensor_copy(high[:, :], lohi_i[:, :]))



def degrees(nc, z, m):
    NPT, B = z.node_tiles, z.groups // 2
    with Phase(nc) as ctx:
        def sb(name, shape, dt=F32):
            return ctx.enter_context(nc.sbuf_tensor(name, shape, dt))

        src_low = sb("src_low1", [P, 2, G, P])
        src_high = sb("src_high1", [P, 2, G, 2, NPT])
        dst_low = sb("dst_low1", [P, 2, G, P], BF16)
        dst_high = sb("dst_high1", [P, 2, G, NPT], BF16)
        ps_src = [ctx.enter_context(nc.psum_tensor(f"ps_src{i}", [P, 2, NPT], F32)) for i in range(2)]
        ps_dst = [ctx.enter_context(nc.psum_tensor(f"ps_dst{i}", [P, NPT], F32)) for i in range(2)]
        hot_ready = [ctx.semaphore(f"hot_ready{i}") for i in range(2)]
        summed = [ctx.semaphore(f"summed{i}") for i in range(2)]
        added = ctx.semaphore("hist_added")
        block = ctx.enter_context(nc.Block())

        def hot(b, par):
            for k in range(G):
                t = (b * 2 + par) * G + k
                one = lambda table: table[:, bass.ds(t, 1)]
                nc.vector.tensor_scalar(src_low[:, par, k, :], m.lane[:, :], one(m.src_lo), None, ALU.is_equal)
                nc.vector.tensor_scalar(src_high[:, par, k, 0, :], m.lane[:, 0:NPT], one(m.src_hi), None, ALU.is_equal)
                nc.vector.tensor_scalar(src_high[:, par, k, 1, :], m.lane[:, 0:NPT], one(m.src_hi), one(m.w), ALU.is_equal, ALU.mult)
                nc.vector.tensor_scalar(dst_low[:, par, k, :], m.lane_bf[:, :], one(m.dst_lo), None, ALU.is_equal)
                last = nc.vector.tensor_scalar(dst_high[:, par, k, :], m.lane_bf[:, 0:NPT], one(m.dst_hi), None, ALU.is_equal)
            last.then_inc(hot_ready[par], 1)

        @block.vector
        def _(v):
            nc.vector.memset(m.deg[:, :, :], 0.0).then_inc(added, 1)
            with v.Fori(0, B) as b:
                for par in range(2):
                    hot(b, par)
                for par in range(2):
                    v.wait_ge(summed[par], b + 1)
                    v.wait_ge(added, b * 4 + 2 * par + 1)
                    nc.vector.tensor_tensor(m.deg[:, 0:2, :], m.deg[:, 0:2, :], ps_src[par][:, :, :], ALU.add).then_inc(added, 1)
                    nc.vector.tensor_tensor(m.deg[:, 2, :], m.deg[:, 2, :], ps_dst[par][:, :], ALU.add).then_inc(added, 1)

        @block.tensor
        def _(pe):
            with pe.Fori(0, B) as b:
                for par in range(2):
                    pe.wait_ge(hot_ready[par], b + 1)
                    pe.wait_ge(added, b * 4 + 1)
                    for k in range(G):
                        nc.tensor.matmul(ps_src[par][:, :, :], src_low[:, par, k, :], src_high[:, par, k, :, :], start=(k == 0), stop=(k == G - 1))
                        last = nc.tensor.matmul(ps_dst[par][:, :], dst_low[:, par, k, :], dst_high[:, par, k, :], start=(k == 0), stop=(k == G - 1))
                    last.then_inc(summed[par], 1)


def inverse_roots(nc, z, m):
    NPT = z.node_tiles
    with Phase(nc) as ctx:
        sb = lambda name: ctx.enter_context(nc.sbuf_tensor(name, [P, 3, NPT], F32))
        root, t = sb("root"), sb("root_t")
        prepared, rooted, stepped = (ctx.semaphore(n) for n in ("deg_prepared", "deg_rooted", "deg_step"))
        block = ctx.enter_context(nc.Block())

        @block.scalar
        def _(act):
            act.wait_ge(prepared, 3)
            nc.scalar.activation(root[:, :, :], m.deg[:, :, :], ACT.Sqrt).then_inc(rooted, 1)

        @block.vector
        def _(v):
            step = Chain(v, stepped, 0)
            nc.vector.tensor_scalar(m.deg[:, 0, :], m.deg[:, 0, :], 1.0, None, ALU.max).then_inc(prepared, 1)
            nc.vector.tensor_scalar(m.deg[:, 1, :], m.deg[:, 1, :], 1.0, None, ALU.add).then_inc(prepared, 1)
            nc.vector.tensor_scalar(m.deg[:, 2, :], m.deg[:, 2, :], 1.0, None, ALU.max).then_inc(prepared, 1)
            v.wait_ge(prepared, 3)
            v.wait_ge(rooted, 1)
            newton(nc, step, m.scale[:, :, :], m.deg[:, :, :], root[:, :, :], t[:, :, :])


def newton(nc, step, out, x, root, t):
    step(nc.vector.reciprocal(out, root))
    step(nc.vector.tensor_tensor(t, out, out, ALU.mult))
    step(nc.vector.tensor_tensor(t, t, x, ALU.mult))
    step(nc.vector.tensor_scalar(t, t, -0.5, 1.5, ALU.mult, ALU.add))
    step(nc.vector.tensor_tensor(out, out, t, ALU.mult))


NEWTON_STEPS = 5


def rows(table, c, width=D):
    return table[bass.ds(c * CH, CH), 0:width].rearrange("(k p) f -> p k f", p=P)


def scale_rows(nc, z, m):
    with Phase(nc) as ctx:
        xin = ctx.enter_context(nc.sbuf_tensor("sr_x", [P, 2, CT, D], F32))
        out = ctx.enter_context(nc.sbuf_tensor("sr_y", [P, 2, CT, D], F32))
        x_in = [ctx.semaphore(f"sr_x_in{i}") for i in range(2)]
        stored = [ctx.semaphore(f"sr_stored{i}") for i in range(2)]
        scaled = [ctx.semaphore(f"sr_scaled{i}") for i in range(2)]
        block = ctx.enter_context(nc.Block())

        @block.sync
        def _(sp):
            for c in range(z.chunks):
                if c >= 2:
                    sp.wait_ge(scaled[c % 2], c // 2)
                sp.dma_start(xin[:, c % 2, :, :], rows(m.x0, c)).then_inc(x_in[c % 2], 16)

        @block.vector
        def _(v):
            for c in range(z.chunks):
                v.wait_ge(x_in[c % 2], 16 * (c // 2 + 1))
                if c >= 2:
                    v.wait_ge(stored[c % 2], 16 * (c // 2))
                last = nc.vector.tensor_tensor(out[:, c % 2, :, :], xin[:, c % 2, :, :], bc(m.scale[:, 0, c * CT:(c + 1) * CT], D), ALU.mult)
                last.then_inc(scaled[c % 2], 1)

        @block.scalar
        def _(act):
            for c in range(z.chunks):
                act.wait_ge(scaled[c % 2], c // 2 + 1)
                act.dma_start(rows(m.table0, c), out[:, c % 2, :, :]).then_inc(stored[c % 2], 16)
            for i in range(2):
                act.wait_ge(stored[i], 16 * ((z.chunks + 1 - i) // 2))



def add_windows(nc, v, m, z, g, regs, targets, carried):
    v.load(regs, m.base_row[0:1, bass.ds(g * G, G)])
    with v.If_lt(regs[0], 0):
        for *_, added in targets:
            v.wait_ge(added, g * G + 1)
        v.sem_inc(carried, 1)
        with v.Fori(0, GE) as e:
            v.load(m.dst_reg, m.dst_pad[bass.ds(g, 1), bass.ds(e, 1)])
            col = v.snap(m.dst_reg, min_val=0, max_val=z.cols - 1)
            for target, source, n, op, _ in targets:
                nc.vector.tensor_tensor(target[0:n, bass.ds(col, 1)], target[0:n, bass.ds(col, 1)],
                                        source[0:n, bass.ds(e, 1)], op)
            v.drain()
        for *_, added in targets:
            v.drain().then_inc(added, G)
    with v.Else():
        for k in range(G):
            base = v.snap(regs[k], min_val=0, max_val=z.cols - P)
            for target, source, n, op, added in targets:
                v.wait_ge(added, g * G + k + 1)
                nc.vector.tensor_tensor(target[0:n, bass.ds(base, P)], target[0:n, bass.ds(base, P)],
                                        source[0:n, k * P:(k + 1) * P], op).then_inc(added, 1)


def alloc_window_registers(v, m, name):
    m.dst_reg = v.alloc_register(f"{name}_dst")
    return [v.alloc_register(f"{name}_base{k}") for k in range(G)]


def sum_over_edges(nc, z, m, table, weights, name):
    B = z.groups // 2
    with Phase(nc) as ctx:
        rows_ = ctx.enter_context(nc.sbuf_tensor(f"{name}_rows", [P, 2, G, D], F32))
        hot = ctx.enter_context(nc.sbuf_tensor(f"{name}_hot", [P, 2, G, P], F32))
        idx = ctx.enter_context(nc.sbuf_tensor(f"{name}_idx", [P, 2, G], I32))
        ps = [ctx.enter_context(nc.psum_tensor(f"{name}_ps{i}", [P, GE], F32)) for i in range(2)]
        two = lambda n: [ctx.semaphore(f"{name}_{n}{i}") for i in range(2)]
        gather_begun = ctx.semaphore(f"{name}_begun")
        idx_staged, rows_in, hot_ready, summed = two("idx_staged"), two("rows_in"), two("hot_ready"), two("summed")
        added = ctx.semaphore(f"{name}_added")
        block = ctx.enter_context(nc.Block())

        @block.scalar
        def _(act):
            with act.Fori(0, B) as b:
                for par in range(2):
                    act.wait_ge(summed[par], b + 1)
                    nc.scalar.copy(idx[:, par, :], cols(m.src_idx, (b * 2 + par) * G, G)).then_inc(idx_staged[par], 1)

        @block.gpsimd
        def _(pool):
            with pool.Fori(0, B) as b:
                for par in range(2):
                    pool.wait_ge(idx_staged[par], b + 1)
                    pool.wait_ge(summed[par], b + 1)
                    pool.sem_inc(gather_begun, 1)
                    for k in range(G):
                        pool.indirect_dma_start(out=rows_[:, par, k, :], out_offset=None, in_=table[:, :],
                                                in_offset=bass.IndirectOffsetOnAxis(ap=idx[:, par, k:k + 1], axis=0)).then_inc(rows_in[par], 16)

        @block.tensor
        def _(pe):
            for par in range(2):
                pe.sem_inc(summed[par], 1)
            with pe.Fori(0, B) as b:
                for par in range(2):
                    pe.wait_ge(hot_ready[par], b + 1)
                    pe.wait_ge(rows_in[par], (b + 1) * (16 * G))
                    for k in range(G):
                        last = nc.tensor.matmul(ps[par][:, k * P:(k + 1) * P], rows_[:, par, k, :], hot[:, par, k, :], start=True, stop=True)
                    last.then_inc(summed[par], 1)

        @block.vector
        def _(v):
            regs = alloc_window_registers(v, m, name)

            def one_hot(b, par):
                v.wait_ge(summed[par], b + 1)
                for k in range(G):
                    t = (b * 2 + par) * G + k
                    if weights is None:
                        last = nc.vector.tensor_scalar(hot[:, par, k, :], m.lane[:, :], cols(m.loc, t, 1), None, ALU.is_equal)
                    else:
                        last = nc.vector.tensor_scalar(hot[:, par, k, :], m.lane[:, :], cols(m.loc, t, 1), cols(weights, t, 1), ALU.is_equal, ALU.mult)
                last.then_inc(hot_ready[par], 1)

            def windows(b, par):
                v.wait_ge(summed[par], b + 2)
                add_windows(nc, v, m, z, b * 2 + par, regs, [(m.acc, ps[par], P, ALU.add, added)], gather_begun)

            nc.vector.memset(m.acc[:, :], 0.0).then_inc(added, 1)
            one_hot(0, 0)
            if B > 1:
                with v.Fori(0, B - 1) as b:
                    one_hot(b, 1)
                    windows(b, 0)
                    one_hot(b + 1, 0)
                    windows(b, 1)
            one_hot(B - 1, 1)
            windows(B - 1, 0)
            windows(B - 1, 1)
            v.wait_ge(added, z.tiles + 1)



class NodePhase:

    def __init__(self, nc, ctx, name):
        self.nc, self.ctx, self.name = nc, ctx, name

    def sb(self, name, shape, dt=F32):
        return self.ctx.enter_context(self.nc.sbuf_tensor(f"{self.name}_{name}", shape, dt))

    def ps(self, name, shape):
        return self.ctx.enter_context(self.nc.psum_tensor(f"{self.name}_{name}", shape, F32))

    def sem(self, name):
        return self.ctx.semaphore(f"{self.name}_{name}")


LN_STEPS = 2 * CT + 1 + NEWTON_STEPS + CT


class Norm:

    def __init__(self, nc, ph):
        self.nc = nc
        self.stats = ph.sb("stats", [P, CT, 6])
        self.mv = ph.sb("meanvar", [P, CT, 2])
        self.var = ph.sb("var", [P, CT])
        self.root = ph.sb("rootv", [P, CT])
        self.rstd = ph.sb("rstd", [P, CT])
        self.t = ph.sb("rstd_t", [P, CT])
        self.var_ready = ph.sem("var_ready")
        self.root_ready = ph.sem("root_ready")
        self.stats_taken = ph.sem("stats_taken")

    def vector(self, v, step, c, y, out):
        nc = self.nc
        for k in range(CT):
            step.go(nc.vector.bn_stats(self.stats[:, k, :], y[:, k, :]))
        step.wait()
        v.sem_inc(self.stats_taken, 1)
        for k in range(CT):
            step.go(nc.vector.bn_aggr(self.mv[:, k, :], self.stats[:, k, :]))
        step.wait()
        step(nc.vector.tensor_scalar(self.var[:, :], self.mv[:, :, 1], EPS, None, ALU.add))
        v.sem_inc(self.var_ready, 1)
        v.wait_ge(self.root_ready, c + 1)
        newton(nc, step, self.rstd[:, :], self.var[:, :], self.root[:, :], self.t[:, :])
        for k in range(CT):
            step(nc.vector.tensor_scalar(out[:, k, :], y[:, k, :], self.mv[:, k, 0:1], self.rstd[:, k:k + 1], ALU.subtract, ALU.mult))

    def scalar(self, act, c):
        act.wait_ge(self.var_ready, c + 1)
        self.nc.scalar.activation(self.root[:, :], self.var[:, :], ACT.Sqrt).then_inc(self.root_ready, 1)


def layer0_nodes(nc, z, m, ins):
    NCH = z.chunks
    with Phase(nc) as ctx:
        ph = NodePhase(nc, ctx, "n0")
        w_self, w_inter = ph.sb("w_self", [D, D]), ph.sb("w_inter", [D, D])
        x = ph.sb("x", [P, CT, D])
        acc_c, xt, hx = ph.sb("acc_c", [D, CH]), ph.sb("xt", [D, CH]), ph.sb("hx", [D, CH])
        y, out, tab = ph.sb("y", [P, CT, D]), ph.sb("out", [P, CT, D]), ph.sb("tab", [P, CT, D])
        ps_t, ps_a, ps_b = ph.ps("ps_t", [D, CH]), ph.ps("ps_a", [P, CT, D]), ph.ps("ps_b", [P, CT, D])
        norm = Norm(nc, ph)
        w_in, x_in, stored, turned, acc_taken, ready, product, step_s, out_ready, x_read, root2 = (ph.sem(n) for n in (
            "w_in", "x_in", "stored", "turned", "acc_taken", "ready", "product", "step", "out_ready", "x_read", "root2"))
        block = ctx.enter_context(nc.Block())
        PER = 2 + CT + 1 + LN_STEPS + CT

        @block.sync
        def _(sp):
            sp.sem_inc(stored, 32)
            sp.dma_start(w_self[:, :], ins["L0_gnn_W_self"]).then_inc(w_in, 16)
            sp.dma_start(w_inter[:, :], ins["L0_gnn_W_inter"]).then_inc(w_in, 16)
            with sp.Fori(0, NCH) as c:
                sp.wait_ge(x_read, c + 1)
                sp.dma_start(x[:, :, :], rows(m.x0, c)).then_inc(x_in, 16)
                sp.wait_ge(out_ready, c + 1)
                sp.dma_start(rows(m.x1, c), out[:, :, :]).then_inc(stored, 16)
                sp.dma_start(rows(m.table1, c), tab[:, :, :]).then_inc(stored, 16)
            sp.wait_ge(stored, 32 * (NCH + 1))

        @block.tensor
        def _(pe):
            pe.sem_inc(product, 1)
            pe.wait_ge(w_in, 32)
            with pe.Fori(0, NCH) as c:
                pe.wait_ge(x_in, (c + 1) * 16)
                for k in range(CT):
                    last = nc.tensor.transpose(ps_t[:, k * P:(k + 1) * P], x[:, k, :], m.ident[:, :])
                last.then_inc(turned, 1)
                pe.wait_ge(ready, c + 1)
                for k in range(CT):
                    at = slice(k * P, (k + 1) * P)
                    nc.tensor.matmul(ps_a[:, k, :], acc_c[:, at], w_self[:, :], start=True, stop=False)
                    nc.tensor.matmul(ps_a[:, k, :], hx[:, at], w_inter[:, :], start=False, stop=True)
                    last = nc.tensor.matmul(ps_b[:, k, :], xt[:, at], w_self[:, :], start=True, stop=True)
                last.then_inc(product, 1)

        @block.scalar
        def _(act):
            with act.Fori(0, NCH) as c:
                act.wait_ge(product, c + 1)
                nc.scalar.copy(acc_c[:, :], cols(m.acc, c * CH, CH)).then_inc(acc_taken, 1)
                norm.scalar(act, c)

        @block.vector
        def _(v):
            v.sem_inc(x_read, 1)
            with v.Fori(0, NCH) as c:
                step = Chain(v, step_s, c * PER, PER)
                v.wait_ge(turned, c + 1)
                v.wait_ge(product, c + 1)
                step(nc.vector.tensor_copy(xt[:, :], ps_t[:, :]))
                v.wait_ge(acc_taken, c + 1)
                step(nc.vector.tensor_tensor(hx[:, :], acc_c[:, :], xt[:, :], ALU.mult))
                v.sem_inc(ready, 1)
                v.wait_ge(product, c + 2)
                for k in range(CT):
                    step(nc.vector.scalar_tensor_tensor(y[:, k, :], ps_a[:, k, :], cols(m.scale[:, 2, :], c * CT + k, 1), x[:, k, :], ALU.mult, ALU.add))
                v.sem_inc(x_read, 1)
                step(nc.vector.tensor_tensor(y[:, :, :], y[:, :, :], ps_b[:, :, :], ALU.add))
                v.wait_ge(stored, c * 32 + 32)
                norm.vector(v, step, c, y, out)
                for k in range(CT):
                    step(nc.vector.tensor_scalar(tab[:, k, :], out[:, k, :], cols(m.scale[:, 1, :], c * CT + k, 1), None, ALU.mult))
                v.sem_inc(out_ready, 1)
                step.done()



def layer1_nodes(nc, z, m, ins):
    NCH = z.chunks
    with Phase(nc) as ctx:
        ph = NodePhase(nc, ctx, "n1")
        w_raw, w_t, w2 = ph.sb("w_raw", [D, D]), ph.sb("w_t", [D, D]), ph.sb("w2", [D, D])
        att, bias = ph.sb("att", [D, 2 * HEADS]), ph.sb("bias", [P, D])
        x, tab_in = ph.sb("x", [P, CT, D]), ph.sb("tab_in", [P, CT, D])
        acc_s, xt, ht = ph.sb("acc_s", [D, CH]), ph.sb("xt", [D, CH]), ph.sb("ht", [D, CH])
        y, out, tab = ph.sb("y", [P, CT, D]), ph.sb("out", [P, CT, D]), ph.sb("tab", [P, CT, ROW2])
        ps_t, ps_a, ps_u = ph.ps("ps_t", [D, CH]), ph.ps("ps_a", [P, CT, D]), ph.ps("ps_u", [D, CH])
        ps_h, ps_ht, ps_att = ph.ps("ps_h", [P, CT, D]), ph.ps("ps_ht", [D, CH]), ph.ps("ps_att", [P, CT, 2 * HEADS])
        norm = Norm(nc, ph)
        names = ("w_in", "att_zero", "w_turned", "w_copied", "rows_in", "stored", "tab_turned", "acc_ready", "product",
                 "normed", "x2_turned", "x2_copied", "h_done", "ht_copied", "att_done", "table_ready", "step")
        q = {n: ph.sem(n) for n in names}
        block = ctx.enter_context(nc.Block())
        PER = 1 + CT + 1 + LN_STEPS + 1 + 3

        @block.sync
        def _(sp):
            sp.sem_inc(q["stored"], 32)
            sp.dma_start(w_raw[:, :], ins["L1_gnn_W"]).then_inc(q["w_in"], 16)
            sp.dma_start(w2[:, :], ins["L2_gnn_W"]).then_inc(q["w_in"], 16)
            sp.dma_start(bias[:, :], ins["L1_gnn_b"].partition_broadcast(P)).then_inc(q["w_in"], 16)
            sp.wait_ge(q["att_zero"], 1)
            for h in range(HEADS):
                for i, name in enumerate(("L2_gnn_att_src", "L2_gnn_att_dst")):
                    sp.dma_start(att[h * HD:(h + 1) * HD, i * HEADS + h:i * HEADS + h + 1],
                                 ins[name][h:h + 1, :].rearrange("o c -> c o"), allow_slow_non_contiguous=True).then_inc(q["w_in"], 16)
            with sp.Fori(0, NCH) as c:
                sp.wait_ge(q["normed"], c + 1)
                sp.dma_start(x[:, :, :], rows(m.x1, c)).then_inc(q["rows_in"], 16)
                sp.dma_start(tab_in[:, :, :], rows(m.table1, c)).then_inc(q["rows_in"], 16)
                sp.wait_ge(q["table_ready"], c + 1)
                sp.dma_start(rows(m.x2, c), out[:, :, :]).then_inc(q["stored"], 16)
                sp.dma_start(rows(m.table2, c, ROW2), tab[:, :, :]).then_inc(q["stored"], 16)
            sp.wait_ge(q["stored"], 32 * (NCH + 1))

        @block.tensor
        def _(pe):
            pe.wait_ge(q["w_in"], 16 * (3 + 2 * HEADS))
            nc.tensor.transpose(ps_t[:, 0:D], w_raw[:, :], m.ident[:, :]).then_inc(q["w_turned"], 1)
            pe.wait_ge(q["w_copied"], 1)
            with pe.Fori(0, NCH) as c:
                pe.wait_ge(q["rows_in"], (c + 1) * 32)
                for k in range(CT):
                    last = nc.tensor.transpose(ps_t[:, k * P:(k + 1) * P], tab_in[:, k, :], m.ident[:, :])
                last.then_inc(q["tab_turned"], 1)
                pe.wait_ge(q["acc_ready"], c + 1)
                for k in range(CT):
                    last = nc.tensor.matmul(ps_a[:, k, :], acc_s[:, k * P:(k + 1) * P], w_t[:, :], start=True, stop=True)
                last.then_inc(q["product"], 1)
                pe.wait_ge(q["normed"], c + 2)
                for k in range(CT):
                    last = nc.tensor.transpose(ps_u[:, k * P:(k + 1) * P], out[:, k, :], m.ident[:, :])
                last.then_inc(q["x2_turned"], 1)
                pe.wait_ge(q["x2_copied"], c + 1)
                nc.tensor.matmul(ps_ht[:, :], w2[:, :], xt[:, :], start=True, stop=True).then_inc(q["h_done"], 1)
                for k in range(CT):
                    nc.tensor.matmul(ps_h[:, k, :], xt[:, k * P:(k + 1) * P], w2[:, :], start=True, stop=True)
                pe.wait_ge(q["ht_copied"], c + 1)
                for k in range(CT):
                    last = nc.tensor.matmul(ps_att[:, k, :], ht[:, k * P:(k + 1) * P], att[:, :], start=True, stop=True)
                last.then_inc(q["att_done"], 1)

        @block.scalar
        def _(act):
            with act.Fori(0, NCH) as c:
                norm.scalar(act, c)
                act.wait_ge(q["h_done"], c + 1)
                nc.scalar.copy(ht[:, :], ps_ht[:, :]).then_inc(q["ht_copied"], 1)

        @block.vector
        def _(v):
            nc.vector.memset(att[:, :], 0.0).then_inc(q["att_zero"], 1)
            v.sem_inc(q["normed"], 1)
            v.wait_ge(q["w_turned"], 1)
            nc.vector.tensor_copy(w_t[:, :], ps_t[:, 0:D]).then_inc(q["w_copied"], 1)
            with v.Fori(0, NCH) as c:
                step = Chain(v, q["step"], c * PER, PER)
                v.wait_ge(q["tab_turned"], c + 1)
                step(nc.vector.tensor_tensor(acc_s[:, :], cols(m.acc, c * CH, CH), ps_t[:, :], ALU.add))
                v.sem_inc(q["acc_ready"], 1)
                v.wait_ge(q["product"], c + 1)
                for k in range(CT):
                    step(nc.vector.scalar_tensor_tensor(y[:, k, :], ps_a[:, k, :], cols(m.scale[:, 1, :], c * CT + k, 1), x[:, k, :], ALU.mult, ALU.add))
                step(nc.vector.tensor_tensor(y[:, :, :], y[:, :, :], bias[:, :].unsqueeze(1).to_broadcast([P, CT, D]), ALU.add))
                v.wait_ge(q["stored"], c * 32 + 32)
                norm.vector(v, step, c, y, out)
                v.sem_inc(q["normed"], 1)
                v.wait_ge(q["x2_turned"], c + 1)
                step(nc.vector.tensor_copy(xt[:, :], ps_u[:, :]))
                v.sem_inc(q["x2_copied"], 1)
                v.wait_ge(q["att_done"], c + 1)
                step(nc.vector.tensor_copy(tab[:, :, 0:D], ps_h[:, :, :]))
                step(nc.vector.tensor_copy(tab[:, :, D:ROW2], ps_att[:, :, 0:HEADS]))
                step(nc.vector.tensor_copy(m.att[:, bass.ds(c * CT, CT), :], ps_att[:, :, :]))
                v.sem_inc(q["table_ready"], 1)
                step.done()


def lowest_source(nc, z, m):
    with Phase(nc) as ctx:
        part = ctx.enter_context(nc.sbuf_tensor("low_part", [P, 1], F32))
        per_lane, over = ctx.semaphore("low_per_lane"), ctx.semaphore("low_over")
        block = ctx.enter_context(nc.Block())

        @block.vector
        def _(v):
            nc.vector.tensor_reduce(part[:, :], m.att[:, :, 0:HEADS], mybir.AxisListType.XY, ALU.min, negate=True).then_inc(per_lane, 1)
            v.wait_ge(over, 1)

        @block.gpsimd
        def _(pool):
            pool.wait_ge(per_lane, 1)
            nc.gpsimd.partition_all_reduce(m.low[:, :], part[:, :], P, bass.bass_isa.ReduceOp.max).then_inc(over, 1)


def highest_source(nc, z, m):
    B = z.groups // 2
    GH = G * HEADS
    with Phase(nc) as ctx:
        name = "e2"
        sb = lambda n, shape, dt=F32: ctx.enter_context(nc.sbuf_tensor(f"{name}_{n}", shape, dt))
        rows_, hot, idx = sb("rows", [P, 2, G, ROW2]), sb("hot", [P, 2, G, P]), sb("idx", [P, 2, G], I32)
        a_e, a_t, run_t, run_e = sb("a_e", [P, 2, GH]), sb("a_t", [GH, 2, P]), sb("run_t", [GH, 2, P]), sb("run_e", [P, 2, GH])
        resets = sb("resets", [GH, 2, P])
        ps = [ctx.enter_context(nc.psum_tensor(f"{name}_ps{i}", [HEADS, GE], F32)) for i in range(2)]
        ps_a = [ctx.enter_context(nc.psum_tensor(f"{name}_ps_a{i}", [GH, P], F32)) for i in range(2)]
        ps_r = [ctx.enter_context(nc.psum_tensor(f"{name}_ps_r{i}", [P, GH], F32)) for i in range(2)]
        names = ("idx_staged", "rows_in", "resets_in", "stashed", "a_ready", "a_turned", "a_copied", "run_ready",
                 "run_turned", "run_copied", "summed")
        q = {n: [ctx.semaphore(f"{name}_{n}{i}") for i in range(2)] for n in names}
        joined, begun, turning = (ctx.semaphore(f"{name}_{n}") for n in ("joined", "begun", "turning"))
        block = ctx.enter_context(nc.Block())

        @block.gpsimd
        def _(pool):
            with pool.Fori(0, B) as b:
                for par in range(2):
                    pool.wait_ge(q["idx_staged"][par], b + 1)
                    pool.wait_ge(q["a_ready"][par], b + 1)
                    pool.wait_ge(q["stashed"][par], b * 16 + 16)
                    pool.sem_inc(begun, 1)
                    for k in range(G):
                        pool.indirect_dma_start(out=rows_[:, par, k, :], out_offset=None, in_=m.table2[:, :],
                                                in_offset=bass.IndirectOffsetOnAxis(ap=idx[:, par, k:k + 1], axis=0)).then_inc(q["rows_in"][par], 16)

        @block.sync
        def _(sp):
            for par in range(2):
                sp.sem_inc(q["stashed"][par], 16)
            with sp.Fori(0, B) as b:
                for par in range(2):
                    g = b * 2 + par
                    sp.wait_ge(q["run_ready"][par], b + 1)
                    sp.dma_start(resets[:, par, :], m.resets4[bass.ds(g, 1), :].rearrange("o (r e) -> (o r) e", e=P)).then_inc(q["resets_in"][par], 16)
                    sp.wait_ge(q["rows_in"][par], (b + 1) * (16 * G))
                    sp.dma_start(m.stash[bass.ds(g * P, P), :], rows_[:, par, :, :].rearrange("p k f -> p (k f)")).then_inc(q["stashed"][par], 16)
            for par in range(2):
                sp.wait_ge(q["stashed"][par], 16 * (B + 1))

        @block.scalar
        def _(act):
            with act.Fori(0, B) as b:
                for par in range(2):
                    act.wait_ge(q["a_ready"][par], b + 1)
                    nc.scalar.copy(idx[:, par, :], cols(m.src_idx, (b * 2 + par) * G, G)).then_inc(q["idx_staged"][par], 1)
                for par in range(2):
                    act.wait_ge(q["a_turned"][par], b + 1)
                    nc.scalar.copy(a_t[:, par, :], ps_a[par][:, :]).then_inc(q["a_copied"][par], 1)
                    act.wait_ge(q["run_turned"][par], b + 1)
                    nc.scalar.copy(run_e[:, par, :], ps_r[par][:, :]).then_inc(q["run_copied"][par], 1)

        @block.tensor
        def _(pe):
            for par in range(2):
                pe.sem_inc(q["summed"][par], 1)
            with pe.Fori(0, B) as b:
                for par in range(2):
                    pe.wait_ge(q["a_ready"][par], b + 2)
                    nc.tensor.transpose(ps_a[par][:, :], a_e[:, par, :], m.ident[:, :]).then_inc(q["a_turned"][par], 1)
                    pe.wait_ge(q["run_ready"][par], b + 2)
                    pe.sem_inc(turning, 1)
                    nc.tensor.transpose(ps_r[par][:, :], run_t[:, par, :], m.ident[0:GH, 0:GH]).then_inc(q["run_turned"][par], 1)
                    pe.wait_ge(q["run_copied"][par], b + 1)
                    for k in range(G):
                        last = nc.tensor.matmul(ps[par][:, k * P:(k + 1) * P], run_e[:, par, k * HEADS:(k + 1) * HEADS],
                                                hot[:, par, k, :], start=True, stop=True)
                    last.then_inc(q["summed"][par], 1)

        @block.vector
        def _(v):
            regs = alloc_window_registers(v, m, name)
            nc.vector.memset(m.acc[0:HEADS, :], 0.0).then_inc(joined, 1)
            for par in range(2):
                v.sem_inc(q["a_ready"][par], 1)
                v.sem_inc(q["run_ready"][par], 1)
            with v.Fori(0, B) as b:
                for par in range(2):
                    v.wait_ge(q["summed"][par], b + 1)
                    for k in range(G):
                        t = (b * 2 + par) * G + k
                        nc.vector.tensor_scalar(hot[:, par, k, :], m.lane[:, :], cols(m.last, t, 1), None, ALU.is_equal)
                    v.wait_ge(q["rows_in"][par], (b + 1) * (16 * G))
                    nc.vector.tensor_scalar(a_e[:, par, :].rearrange("p (k h) -> p k h", h=HEADS), rows_[:, par, :, D:ROW2],
                                            m.low[:, 0:1], None, ALU.add).then_inc(q["a_ready"][par], 1)
                    v.wait_ge(q["a_copied"][par], b + 1)
                    v.wait_ge(q["resets_in"][par], b * 16 + 16)
                    nc.vector.tensor_tensor_scan(run_t[:, par, :], resets[:, par, :], a_t[:, par, :], 0.0, ALU.add, ALU.max).then_inc(q["run_ready"][par], 1)
                    v.wait_ge(q["summed"][par], b + 2)
                    add_windows(nc, v, m, z, b * 2 + par, regs, [(m.acc, ps[par], HEADS, ALU.max, joined)], begun)
            v.wait_ge(joined, z.tiles + 1)


def attention_nodes(nc, z, m):
    NCH, NPT = z.chunks, z.node_tiles
    with Phase(nc) as ctx:
        ph = NodePhase(nc, ctx, "na")
        top_c, top = ph.sb("top_c", [HEADS, CH]), ph.sb("top", [P, NPT, HEADS])
        e_self, t, dn = ph.sb("e_self", [P, NPT, HEADS]), ph.sb("t", [P, NPT, HEADS]), ph.sb("dn", [P, NPT, 2 * HEADS])
        ps = ph.ps("ps", [P, CT, HEADS])
        q = {n: ph.sem(n) for n in ("taken", "turned", "copied", "begun", "step", "e_ready", "exped", "dn_ready", "stored")}
        block = ctx.enter_context(nc.Block())

        @block.scalar
        def _(act):
            with act.Fori(0, NCH) as c:
                act.wait_ge(q["turned"], c + 1)
                nc.scalar.copy(top_c[:, :], m.acc[0:HEADS, bass.ds(c * CH, CH)]).then_inc(q["taken"], 1)
            act.wait_ge(q["e_ready"], 1)
            nc.scalar.activation(m.p_self[:, :, :], e_self[:, :, :], ACT.Exp).then_inc(q["exped"], 1)

        @block.tensor
        def _(pe):
            pe.sem_inc(q["turned"], 1)
            with pe.Fori(0, NCH) as c:
                pe.wait_ge(q["taken"], c + 1)
                pe.wait_ge(q["copied"], c + 1)
                pe.sem_inc(q["begun"], 1)
                for k in range(CT):
                    last = nc.tensor.transpose(ps[:, k, :], top_c[:, k * P:(k + 1) * P], m.ident[0:HEADS, 0:HEADS])
                last.then_inc(q["turned"], 1)

        @block.vector
        def _(v):
            step = Chain(v, q["step"], 0)
            v.sem_inc(q["copied"], 1)
            with v.Fori(0, NCH) as c:
                v.wait_ge(q["turned"], c + 2)
                nc.vector.tensor_copy(top[:, bass.ds(c * CT, CT), :], ps[:, :, :]).then_inc(q["copied"], 1)
            v.wait_ge(q["copied"], NCH + 1)
            a_src, a_dst = m.att[:, :, 0:HEADS], m.att[:, :, HEADS:]
            step(nc.vector.tensor_scalar(top[:, :, :], top[:, :, :], m.low[:, 0:1], None, ALU.subtract))
            step(nc.vector.tensor_tensor(top[:, :, :], top[:, :, :], a_src, ALU.max))
            step(nc.vector.tensor_tensor(top[:, :, :], top[:, :, :], a_dst, ALU.add))
            step(nc.vector.tensor_scalar(t[:, :, :], top[:, :, :], 0.2, None, ALU.mult))
            step(nc.vector.tensor_tensor(dn[:, :, HEADS:], top[:, :, :], t[:, :, :], ALU.max))
            step(nc.vector.tensor_copy(dn[:, :, 0:HEADS], a_dst))
            v.sem_inc(q["dn_ready"], 1)
            step(nc.vector.tensor_tensor(e_self[:, :, :], a_src, a_dst, ALU.add))
            step(nc.vector.tensor_scalar(t[:, :, :], e_self[:, :, :], 0.2, None, ALU.mult))
            step(nc.vector.tensor_tensor(e_self[:, :, :], e_self[:, :, :], t[:, :, :], ALU.max))
            step(nc.vector.tensor_tensor(e_self[:, :, :], e_self[:, :, :], dn[:, :, HEADS:], ALU.subtract))
            v.sem_inc(q["e_ready"], 1)
            v.wait_ge(q["exped"], 1)

        @block.sync
        def _(sp):
            sp.wait_ge(q["dn_ready"], 1)
            sp.dma_start(m.dst_terms[:, :].rearrange("(k p) f -> p k f", p=P), dn[:, :, :], allow_slow_non_contiguous=True).then_inc(q["stored"], 16)
            sp.wait_ge(q["stored"], 16)


def weighted_sum(nc, z, m):
    B = z.groups // 2
    with Phase(nc) as ctx:
        name = "e3"
        sb = lambda n, shape, dt=F32: ctx.enter_context(nc.sbuf_tensor(f"{name}_{n}", shape, dt))
        rows_, hot, idx = sb("rows", [P, 2, G, ROW2]), sb("hot", [P, 2, G, P]), sb("idx", [P, 2, G], I32)
        terms, e, e2, prob, msg = (sb("terms", [P, 2, G, 2 * HEADS]), sb("e", [P, 2, G, HEADS]), sb("e2", [P, 2, G, HEADS]),
                                   sb("prob", [P, 2, G, HEADS]), sb("msg", [P, 2, G, D]))
        ps = [ctx.enter_context(nc.psum_tensor(f"{name}_ps{i}", [P, GE], F32)) for i in range(2)]
        ps_p = [ctx.enter_context(nc.psum_tensor(f"{name}_ps_p{i}", [HEADS, GE], F32)) for i in range(2)]
        names = ("idx_staged", "rows_in", "terms_in", "e_ready", "prob_ready", "msg_ready", "summed")
        q = {n: [ctx.semaphore(f"{name}_{n}{i}") for i in range(2)] for n in names}
        added, added_p, begun, small = (ctx.semaphore(f"{name}_{n}") for n in ("added", "added_p", "begun", "small"))
        block = ctx.enter_context(nc.Block())

        @block.gpsimd
        def _(pool):
            with pool.Fori(0, B) as b:
                for par in range(2):
                    pool.wait_ge(q["idx_staged"][par], b + 1)
                    pool.wait_ge(q["e_ready"][par], b + 1)
                    pool.sem_inc(begun, 1)
                    for k in range(G):
                        pool.indirect_dma_start(out=terms[:, par, k, :], out_offset=None, in_=m.dst_terms[:, :],
                                                in_offset=bass.IndirectOffsetOnAxis(ap=idx[:, par, k:k + 1], axis=0)).then_inc(q["terms_in"][par], 16)

        @block.sync
        def _(sp):
            with sp.Fori(0, B) as b:
                for par in range(2):
                    sp.wait_ge(q["msg_ready"][par], b + 1)
                    sp.dma_start(rows_[:, par, :, :].rearrange("p k f -> p (k f)"), m.stash[bass.ds((b * 2 + par) * P, P), :]).then_inc(q["rows_in"][par], 16)

        @block.scalar
        def _(act):
            with act.Fori(0, B) as b:
                for par in range(2):
                    act.wait_ge(q["e_ready"][par], b + 1)
                    nc.scalar.copy(idx[:, par, :], cols(m.dst_idx, (b * 2 + par) * G, G)).then_inc(q["idx_staged"][par], 1)
                for par in range(2):
                    act.wait_ge(q["e_ready"][par], b + 2)
                    nc.scalar.activation(prob[:, par, :, :], e[:, par, :, :], ACT.Exp).then_inc(q["prob_ready"][par], 1)

        @block.tensor
        def _(pe):
            for par in range(2):
                pe.sem_inc(q["summed"][par], 1)
            with pe.Fori(0, B) as b:
                for par in range(2):
                    pe.wait_ge(q["msg_ready"][par], b + 2)
                    for k in range(G):
                        at = slice(k * P, (k + 1) * P)
                        nc.tensor.matmul(ps[par][:, at], msg[:, par, k, :], hot[:, par, k, :], start=True, stop=True)
                        last = nc.tensor.matmul(ps_p[par][:, at], prob[:, par, k, :], hot[:, par, k, :], start=True, stop=True)
                    last.then_inc(q["summed"][par], 1)

        @block.vector
        def _(v):
            regs = alloc_window_registers(v, m, name)
            for par in range(2):
                v.sem_inc(q["e_ready"][par], 1)
                v.sem_inc(q["msg_ready"][par], 1)
            nc.vector.memset(m.acc[:, :], 0.0).then_inc(added, 1)
            nc.vector.memset(m.side[0:HEADS, :], 0.0).then_inc(added_p, 1)

            def messages(b, par):
                step = Chain(v, small, (b * 2 + par) * 3, 3)
                v.wait_ge(q["summed"][par], b + 1)
                for k in range(G):
                    t = (b * 2 + par) * G + k
                    nc.vector.tensor_scalar(hot[:, par, k, :], m.lane[:, :], cols(m.loc, t, 1), None, ALU.is_equal)
                v.wait_ge(q["rows_in"][par], b * 16 + 16)
                v.wait_ge(q["terms_in"][par], (b + 1) * (16 * G))
                step(nc.vector.tensor_tensor(e2[:, par, :, :], rows_[:, par, :, D:ROW2], terms[:, par, :, 0:HEADS], ALU.add))
                step(nc.vector.tensor_scalar(e[:, par, :, :], e2[:, par, :, :], 0.2, None, ALU.mult))
                step(nc.vector.tensor_tensor(e2[:, par, :, :], e[:, par, :, :], e2[:, par, :, :], ALU.max))
                nc.vector.tensor_tensor(e[:, par, :, :], e2[:, par, :, :], terms[:, par, :, HEADS:], ALU.subtract).then_inc(q["e_ready"][par], 1)
                v.wait_ge(q["prob_ready"][par], b + 1)
                nc.vector.tensor_tensor(msg[:, par, :, :].rearrange("p k (h c) -> p k h c", h=HEADS), rows_[:, par, :, 0:D].rearrange("p k (h c) -> p k h c", h=HEADS),
                                        prob[:, par, :, :].unsqueeze(3).to_broadcast([P, G, HEADS, HD]), ALU.mult).then_inc(q["msg_ready"][par], 1)
                step.done()

            def windows(b, par):
                v.wait_ge(q["summed"][par], b + 2)
                add_windows(nc, v, m, z, b * 2 + par, regs, [(m.acc, ps[par], P, ALU.add, added), (m.side, ps_p[par], HEADS, ALU.add, added_p)], begun)

            messages(0, 0)
            if B > 1:
                with v.Fori(0, B - 1) as b:
                    messages(b, 1)
                    windows(b, 0)
                    messages(b + 1, 0)
                    windows(b, 1)
            messages(B - 1, 1)
            windows(B - 1, 0)
            windows(B - 1, 1)
            v.wait_ge(added, z.tiles + 1)
            v.wait_ge(added_p, z.tiles + 1)


def layer2_nodes(nc, z, m, ins):
    NCH = z.chunks
    with Phase(nc) as ctx:
        ph = NodePhase(nc, ctx, "n2")
        bias, lin1, conv1, sa, w_sa, b0 = (ph.sb("bias", [P, D]), ph.sb("lin1", [D, D]), ph.sb("conv1", [D, D]),
                                           ph.sb("sa", [2, 1]), ph.sb("w_sa", [2, D]), ph.sb("b0", [D, 1]))
        b_lin = ph.sb("b_lin", [D, 1])
        x, tab_in, acc_c, s_c = ph.sb("x", [P, CT, D]), ph.sb("tab_in", [P, CT, ROW2]), ph.sb("acc_c", [D, CH]), ph.sb("s_c", [HEADS, CH])
        den, y, out, xt, ht, tab = (ph.sb("den", [P, CT, HEADS]), ph.sb("y", [P, CT, D]), ph.sb("out", [P, CT, D]),
                                    ph.sb("xt", [D, CH]), ph.sb("ht", [D, CH]), ph.sb("tab", [P, CT, D]))
        ps_n, ps_s, ps_t, ps_h, ps_x, ps_b = (ph.ps("ps_n", [P, CT, D]), ph.ps("ps_s", [P, CT, HEADS]), ph.ps("ps_t", [D, CH]),
                                              ph.ps("ps_h", [D, CH]), ph.ps("ps_x", [P, CT, D]), ph.ps("ps_b", [D, 1]))
        norm = Norm(nc, ph)
        names = ("w_in", "b_done", "b_ready", "rows_in", "stored", "taken", "turned", "normed", "x3_turned", "x3_copied",
                 "h_done", "h_copied", "xm_done", "table_ready", "step")
        q = {n: ph.sem(n) for n in names}
        block = ctx.enter_context(nc.Block())
        PER = 8 + LN_STEPS + 2
        heads = lambda a: a.rearrange("p k (h c) -> p k h c", h=HEADS)

        @block.sync
        def _(sp):
            sp.sem_inc(q["stored"], 32)
            for dst, src in ((bias[:, :], ins["L2_gnn_bias"].partition_broadcast(P)), (lin1[:, :], ins["L3_gnn_lin1_w"][0, 2:2 + D, :]),
                             (w_sa[:, :], ins["L3_gnn_lin1_w"][0, 0:2, :]), (conv1[:, :], ins["L3_gnn_conv1_w"][0]),
                             (sa[:, :], ins["L3_gnn_state_attr"][0:1, :].rearrange("o s -> s o")),
                             (b_lin[:, :], ins["L3_gnn_lin1_b"][0:1, :].rearrange("o d -> d o"))):
                sp.dma_start(dst, src, allow_slow_non_contiguous=True).then_inc(q["w_in"], 16)
            with sp.Fori(0, NCH) as c:
                sp.wait_ge(q["normed"], c + 1)
                sp.dma_start(x[:, :, :], rows(m.x2, c)).then_inc(q["rows_in"], 16)
                sp.dma_start(tab_in[:, :, :], rows(m.table2, c, ROW2)).then_inc(q["rows_in"], 16)
                sp.wait_ge(q["table_ready"], c + 1)
                sp.dma_start(rows(m.x3, c), out[:, :, :]).then_inc(q["stored"], 16)
                sp.dma_start(rows(m.table3, c), tab[:, :, :]).then_inc(q["stored"], 16)
            sp.wait_ge(q["stored"], 32 * (NCH + 1))

        @block.tensor
        def _(pe):
            pe.sem_inc(q["turned"], 1)
            pe.wait_ge(q["w_in"], 16 * 6)
            nc.tensor.matmul(ps_b[:, :], w_sa[:, :], sa[:, :], start=True, stop=True).then_inc(q["b_done"], 1)
            with pe.Fori(0, NCH) as c:
                pe.wait_ge(q["taken"], c + 1)
                for k in range(CT):
                    at = slice(k * P, (k + 1) * P)
                    nc.tensor.transpose(ps_n[:, k, :], acc_c[:, at], m.ident[:, :])
                    last = nc.tensor.transpose(ps_s[:, k, :], s_c[:, at], m.ident[0:HEADS, 0:HEADS])
                last.then_inc(q["turned"], 1)
                pe.wait_ge(q["normed"], c + 2)
                for k in range(CT):
                    last = nc.tensor.transpose(ps_t[:, k * P:(k + 1) * P], out[:, k, :], m.ident[:, :])
                last.then_inc(q["x3_turned"], 1)
                pe.wait_ge(q["x3_copied"], c + 1)
                nc.tensor.matmul(ps_h[:, :], lin1[:, :], xt[:, :], start=True, stop=True).then_inc(q["h_done"], 1)
                pe.wait_ge(q["h_copied"], c + 1)
                for k in range(CT):
                    last = nc.tensor.matmul(ps_x[:, k, :], ht[:, k * P:(k + 1) * P], conv1[:, :], start=True, stop=True)
                last.then_inc(q["xm_done"], 1)

        @block.scalar
        def _(act):
            act.wait_ge(q["b_ready"], 1)
            with act.Fori(0, NCH) as c:
                act.wait_ge(q["turned"], c + 1)
                nc.scalar.copy(acc_c[:, :], cols(m.acc, c * CH, CH))
                nc.scalar.copy(s_c[:, :], m.side[0:HEADS, bass.ds(c * CH, CH)]).then_inc(q["taken"], 1)
                norm.scalar(act, c)
                act.wait_ge(q["h_done"], c + 1)
                nc.scalar.activation(ht[:, :], ps_h[:, :], ACT.Identity, bias=b0[:, 0:1]).then_inc(q["h_copied"], 1)
                nc.scalar.activation(cols(m.hidden, c * CH, CH), ps_h[:, :], ACT.Identity, bias=b0[:, 0:1])

        @block.vector
        def _(v):
            v.sem_inc(q["normed"], 1)
            v.wait_ge(q["b_done"], 1)
            nc.vector.tensor_tensor(b0[:, :], ps_b[:, :], b_lin[:, :], ALU.add).then_inc(q["b_ready"], 1)
            with v.Fori(0, NCH) as c:
                step = Chain(v, q["step"], c * PER, PER)
                p_self = m.p_self[:, bass.ds(c * CT, CT), :]
                v.wait_ge(q["rows_in"], c * 32 + 32)
                v.wait_ge(q["turned"], c + 2)
                step(nc.vector.tensor_tensor(den[:, :, :], ps_s[:, :, :], p_self, ALU.add))
                step(nc.vector.tensor_scalar(den[:, :, :], den[:, :, :], 1e-16, None, ALU.add))
                step(nc.vector.reciprocal(den[:, :, :], den[:, :, :]))
                step(nc.vector.tensor_tensor(heads(y[:, :, :]), heads(tab_in[:, :, 0:D]), p_self.unsqueeze(3).to_broadcast([P, CT, HEADS, HD]), ALU.mult))
                step(nc.vector.tensor_tensor(y[:, :, :], y[:, :, :], ps_n[:, :, :], ALU.add))
                step(nc.vector.tensor_tensor(heads(y[:, :, :]), heads(y[:, :, :]), den[:, :, :].unsqueeze(3).to_broadcast([P, CT, HEADS, HD]), ALU.mult))
                step(nc.vector.tensor_tensor(y[:, :, :], y[:, :, :], bias[:, :].unsqueeze(1).to_broadcast([P, CT, D]), ALU.add))
                step(nc.vector.tensor_tensor(y[:, :, :], y[:, :, :], x[:, :, :], ALU.add))
                v.wait_ge(q["stored"], c * 32 + 32)
                norm.vector(v, step, c, y, out)
                v.sem_inc(q["normed"], 1)
                v.wait_ge(q["x3_turned"], c + 1)
                step(nc.vector.tensor_copy(xt[:, :], ps_t[:, :]))
                v.sem_inc(q["x3_copied"], 1)
                v.wait_ge(q["xm_done"], c + 1)
                step(nc.vector.tensor_copy(tab[:, :, :], ps_x[:, :, :]))
                v.sem_inc(q["table_ready"], 1)
                step.done()


def cutoffs(nc, z, m):
    NT = z.tiles
    with Phase(nc) as ctx:
        u, k = (ctx.enter_context(nc.sbuf_tensor(n, [P, NT], F32)) for n in ("cut_u", "cut_k"))
        half_pi = ctx.enter_context(nc.sbuf_tensor("half_pi", [P, 1], F32))
        step_s, r_ready, absed, sined = (ctx.semaphore(n) for n in ("cut_step", "cut_r", "cut_abs", "cut_sin"))
        block = ctx.enter_context(nc.Block())
        ROUND = 12582912.0
        two_pi_hi = float(np.float32(6.28125))
        two_pi_lo = float(2 * np.pi - 6.28125)

        @block.vector
        def _(v):
            step = Chain(v, step_s, 0)
            step(nc.vector.memset(half_pi[:, :], PI / 2))
            step(nc.vector.tensor_scalar(u[:, :], m.w[:, :], float(np.float32(PI / 10.0)), None, ALU.mult))
            step(nc.vector.tensor_scalar(k[:, :], u[:, :], 1.0 / (2 * PI), ROUND, ALU.mult, ALU.add))
            step(nc.vector.tensor_scalar(k[:, :], k[:, :], -ROUND, None, ALU.add))
            step(nc.vector.scalar_tensor_tensor(u[:, :], k[:, :], -two_pi_hi, u[:, :], ALU.mult, ALU.add))
            step(nc.vector.scalar_tensor_tensor(u[:, :], k[:, :], -two_pi_lo, u[:, :], ALU.mult, ALU.add))
            v.sem_inc(r_ready, 1)
            v.wait_ge(absed, 1)
            step(nc.vector.tensor_scalar(k[:, :], k[:, :], PI, None, ALU.min))
            v.sem_inc(r_ready, 1)
            v.wait_ge(sined, 1)
            step(nc.vector.tensor_scalar(m.w[:, :], u[:, :], 1.0, 0.5, ALU.add, ALU.mult))

        @block.scalar
        def _(act):
            act.wait_ge(r_ready, 1)
            nc.scalar.activation(k[:, :], u[:, :], ACT.Abs).then_inc(absed, 1)
            act.wait_ge(r_ready, 2)
            nc.scalar.activation(u[:, :], k[:, :], ACT.Sin, bias=half_pi[:, 0:1], scale=-1.0).then_inc(sined, 1)


LOG_SET = "natural_log_exp_and_others"


class Ssp:

    def __init__(self, nc, ph):
        self.nc = nc
        self.pos, self.neg, self.log = ph.sb("ssp_pos", [P, 2, CH]), ph.sb("ssp_neg", [P, 2, CH]), ph.sb("ssp_log", [P, 2, CH])
        self.chain = ph.sem("ssp_chain")

    def vector(self, out, par):
        return self.nc.vector.scalar_tensor_tensor(out, self.pos[:, par, :], -LN2, self.log[:, par, :], ALU.add, ALU.add)


def continuous_conv(nc, z, m, ins, layer):
    NG, K = z.groups, z.gauss
    name = f"c{layer}"
    with Phase(nc) as ctx:
        ph = NodePhase(nc, ctx, name)
        w1, w2, b1, b2 = ph.sb("w1", [K, D]), ph.sb("w2", [D, D]), ph.sb("b1", [D, 1]), ph.sb("b2", [P, D])
        rows_, hot, idx = ph.sb("rows", [P, 2, G, D]), ph.sb("hot", [P, 2, G, P]), ph.sb("idx", [P, 2, G], I32)
        attr, attr_t = ph.sb("attr", [P, 2, G, K]), ph.sb("attr_t", [K, GE])
        act_t, filt, msg = ph.sb("act_t", [D, 2, GE]), ph.sb("filt", [P, CT, D]), ph.sb("msg", [P, 2, G, D])
        ssp = Ssp(nc, ph)
        ps_t, ps_1 = ph.ps("ps_t", [K, CH]), ph.ps("ps_1", [D, CH])
        ps_2 = [ph.ps(f"ps_2{i}", [P, CT, D]) for i in range(2)]
        ps = [ph.ps(f"ps{i}", [P, GE]) for i in range(2)]
        pairs = {n: [ph.sem(f"{n}{i}") for i in range(2)] for n in (
            "idx_staged", "rows_in", "attr_in", "attr_read", "act_ready", "hot_ready", "filter_done", "msg_ready", "summed")}
        one = {n: ph.sem(n) for n in ("w_in", "turned", "turned_copied", "first_done", "first_read", "ssp_ready", "filter_read",
                                      "added", "begun", "filt_ready", "msg_half", "ssp_used", "turning", "attr_part")}
        block = ctx.enter_context(nc.Block())

        def pipeline(run, eng):
            run(-2, True, False, False, 0, 0)
            run(-1, True, True, False, 1, 0)
            if NG > 2:
                with eng.Fori(0, NG // 2 - 1) as b:
                    for par in range(2):
                        run(b * 2 + par, True, True, True, par, b)
            run(NG - 2, False, True, True, 0, NG // 2 - 1)
            run(NG - 1, False, False, True, 1, NG // 2 - 1)

        def last_attr_dmas(g):
            left = max(0, min(GE, z.edges - g * GE))
            full, rest = left // G, left % G
            return ([(0, full, G)] if full else []) + ([(full, 1, rest)] if rest else [])

        @block.sync
        def _(sp):
            for dst, src in ((w1[:, :], ins["L3_gnn_mlp1_w"][layer]), (w2[:, :], ins["L3_gnn_mlp2_w"][layer]),
                             (b1[:, :], ins["L3_gnn_mlp1_b"][layer:layer + 1, :].rearrange("o d -> d o")),
                             (b2[:, :], ins["L3_gnn_mlp2_b"][layer].partition_broadcast(P))):
                sp.dma_start(dst, src, allow_slow_non_contiguous=True).then_inc(one["w_in"], 16)

            def load(g, b, par):
                sp.wait_ge(pairs["attr_read"][par], b + 1)
                sp.dma_start(attr[:, par, :, :].rearrange("p j f -> p (j f)"),
                             ins["edge_attr_50"][bass.ds(g * GE, GE), :].rearrange("(p j) f -> p (j f)", j=G)).then_inc(pairs["attr_in"][par], 16)

            if NG > 2:
                with sp.Fori(0, NG // 2 - 1) as b:
                    for par in range(2):
                        load(b * 2 + par, b, par)
            attr_parts = 0
            for par in range(2):
                g = NG - 2 + par
                sp.wait_ge(pairs["attr_read"][par], NG // 2)
                parts = last_attr_dmas(g)
                for i, (p0, n, j) in enumerate(parts):
                    at = g * GE + p0 * G
                    load_part = sp.dma_start(attr[p0:p0 + n, par, 0:j, :].rearrange("p j f -> p (j f)"),
                                             ins["edge_attr_50"][at:at + n * j, :].rearrange("(p j) f -> p (j f)", j=j))
                    if i < len(parts) - 1:
                        load_part.then_inc(one["attr_part"], 16)
                        attr_parts += 1
                        sp.wait_ge(one["attr_part"], 16 * attr_parts)
                    else:
                        load_part.then_inc(pairs["attr_in"][par], 16)
                if not parts:
                    sp.sem_inc(pairs["attr_in"][par], 16)

        @block.gpsimd
        def _(pool):
            with pool.Fori(0, NG // 2) as b:
                for par in range(2):
                    pool.wait_ge(pairs["idx_staged"][par], b + 1)
                    pool.wait_ge(pairs["msg_ready"][par], b + 1)
                    pool.sem_inc(one["begun"], 1)
                    for k in range(G):
                        pool.indirect_dma_start(out=rows_[:, par, k, :], out_offset=None, in_=m.table3[:, :],
                                                in_offset=bass.IndirectOffsetOnAxis(ap=idx[:, par, k:k + 1], axis=0)).then_inc(pairs["rows_in"][par], 16)

        @block.tensor
        def _(pe):
            for par in range(2):
                pe.sem_inc(pairs["attr_read"][par], 1)
            pe.sem_inc(pairs["summed"][0], 1)
            pe.sem_inc(pairs["summed"][1], 1)
            pe.wait_ge(one["w_in"], 64)

            def run(g, filters, messages, sums, par, b):
                if messages:
                    o, bo = 1 - par, (b if par == 0 else b + 1)
                    if isinstance(g, int) and g < 0:
                        o, bo = 0, 0
                    pe.wait_ge(pairs["act_ready"][o], bo + 1)
                    for h in range(2):
                        pe.wait_ge(one["filter_read"], (g + 1) * 2 + h + 1)
                        for k in range(CT):
                            at = h * CH + k * P
                            last = nc.tensor.matmul(ps_2[h][:, k, :], act_t[:, o, at:at + P], w2[:, :], start=True, stop=True)
                        last.then_inc(pairs["filter_done"][h], 1)
                if filters:
                    p2, b2_ = par, b + 1
                    if isinstance(g, int) and g < 0:
                        p2, b2_ = g + 2, 0
                    pe.wait_ge(pairs["attr_in"][p2], b2_ * 16 + 16)
                    for h in range(2):
                        pe.wait_ge(one["turned_copied"], (g + 2) * 2 + h + 1)
                        pe.sem_inc(one["turning"], 1)
                        for j in range(CT):
                            last = nc.tensor.transpose(ps_t[:, j * P:(j + 1) * P], attr[:, p2, h * CT + j, :], m.ident[:, :])
                        last.then_inc(one["turned"], 1)
                    pe.wait_ge(one["turned_copied"], (g + 2) * 2 + 3)
                    for h in range(2):
                        pe.wait_ge(one["first_read"], (g + 2) * 2 + h + 1)
                        last = nc.tensor.matmul(ps_1[:, :], w1[:, :], attr_t[:, h * CH:(h + 1) * CH], start=True, stop=True)
                        last.then_inc(one["first_done"], 1)
                    pe.wait_ge(one["first_done"], (g + 2) * 2 + 2)
                    pe.sem_inc(pairs["attr_read"][p2], 1)
                if sums:
                    pe.wait_ge(pairs["msg_ready"][par], b + 2)
                    for k in range(G):
                        last = nc.tensor.matmul(ps[par][:, k * P:(k + 1) * P], msg[:, par, k, :], hot[:, par, k, :], start=True, stop=True)
                    last.then_inc(pairs["summed"][par], 1)

            pipeline(run, pe)

        @block.scalar
        def _(act):
            act.preload_act_table_set(LOG_SET)
            act.sem_inc(one["turned_copied"], 1)
            act.sem_inc(one["first_read"], 1)
            act.wait_ge(one["w_in"], 64)

            def stage(b, par):
                act.wait_ge(pairs["msg_ready"][par], b + 1)
                nc.scalar.copy(idx[:, par, :], cols(m.src_idx, (b * 2 + par) * G, G)).then_inc(pairs["idx_staged"][par], 1)

            def run(g, filters, messages, sums, par, b):
                if isinstance(g, int) and g < 0:
                    stage(0, g + 2)
                elif filters:
                    stage(b + 1, par)
                if not filters:
                    return
                for h in range(2):
                    act.wait_ge(one["turned"], (g + 2) * 2 + h + 1)
                    out = attr_t[:, :].rearrange("f (p j) -> f j p", j=G)[:, h * CT:(h + 1) * CT, :]
                    nc.scalar.copy(out, ps_t[:, :].rearrange("f (j p) -> f j p", j=CT)).then_inc(one["turned_copied"], 1)
                for h in range(2):
                    act.wait_ge(one["first_done"], (g + 2) * 2 + h + 1)
                    act.wait_ge(one["ssp_used"], (g + 2) * 2 + h + 1)
                    x = ps_1[:, :]
                    nc.scalar.activation(ssp.pos[:, h, :], x, ACT.Relu, bias=b1[:, 0:1])
                    nc.scalar.activation(ssp.neg[:, h, :], x, ACT.Abs, bias=b1[:, 0:1]).then_inc(one["first_read"], 1)
                    act.wait_ge(one["first_read"], (g + 2) * 2 + h + 2)
                    nc.scalar.activation(ssp.log[:, h, :], ssp.neg[:, h, :], ACT.Exp, scale=-1.0).then_inc(ssp.chain, 1)
                    act.wait_ge(ssp.chain, (g + 2) * 2 + h + 1)
                    nc.scalar.activation(ssp.log[:, h, :], ssp.log[:, h, :], ACT.Ln, bias=1.0).then_inc(one["ssp_ready"], 1)

            pipeline(run, act)

        @block.vector
        def _(v):
            regs = alloc_window_registers(v, m, name)
            nc.vector.memset(m.acc[:, :], 0.0).then_inc(one["added"], 1)
            v.sem_inc(one["filter_read"], 2)
            v.sem_inc(one["ssp_used"], 2)
            v.sem_inc(one["msg_half"], 1)
            for par in range(2):
                v.sem_inc(pairs["msg_ready"][par], 1)
            v.wait_ge(one["w_in"], 64)

            def run(g, filters, messages, sums, par, b):
                if messages:
                    o, bo = 1 - par, (b if par == 0 else b + 1)
                    if isinstance(g, int) and g < 0:
                        o, bo = 0, 0
                    v.wait_ge(pairs["summed"][o], bo + 1)
                    for k in range(G):
                        t = (g + 1) * G + k
                        nc.vector.tensor_scalar(hot[:, o, k, :], m.lane[:, :], cols(m.loc, t, 1), cols(m.w, t, 1), ALU.is_equal, ALU.mult)
                    v.wait_ge(pairs["rows_in"][o], (bo + 1) * (16 * G))
                    for h in range(2):
                        v.wait_ge(pairs["filter_done"][h], g + 2)
                        v.wait_ge(one["msg_half"], (g + 1) * 2 + h + 1)
                        nc.vector.tensor_tensor(filt[:, :, :], ps_2[h][:, :, :], b2[:, :].unsqueeze(1).to_broadcast([P, CT, D]), ALU.add).then_inc(one["filter_read"], 1)
                        v.wait_ge(one["filter_read"], (g + 1) * 2 + h + 3)
                        nc.vector.tensor_tensor(msg[:, o, h * CT:(h + 1) * CT, :], filt[:, :, :], rows_[:, o, h * CT:(h + 1) * CT, :], ALU.mult).then_inc(one["msg_half"], 1)
                    v.wait_ge(one["msg_half"], (g + 1) * 2 + 3)
                    v.sem_inc(pairs["msg_ready"][o], 1)
                if sums:
                    v.wait_ge(pairs["summed"][par], b + 2)
                    add_windows(nc, v, m, z, g, regs, [(m.acc, ps[par], P, ALU.add, one["added"])], one["begun"])
                if filters:
                    p2 = g + 2 if isinstance(g, int) and g < 0 else par
                    b2_ = 0 if isinstance(g, int) and g < 0 else b + 1
                    for h in range(2):
                        v.wait_ge(one["ssp_ready"], (g + 2) * 2 + h + 1)
                        last = ssp.vector(act_t[:, p2, h * CH:(h + 1) * CH], h)
                        last.then_inc(one["ssp_used"], 1)
                    v.wait_ge(one["ssp_used"], (g + 2) * 2 + 4)
                    v.sem_inc(pairs["act_ready"][p2], 1)

            pipeline(run, v)
            v.wait_ge(one["added"], z.tiles + 1)


def conv_nodes(nc, z, m, ins, layer):
    NCH = z.chunks
    real = z.nodes - (NCH - 1) * CH
    with Phase(nc) as ctx:
        ph = NodePhase(nc, ctx, f"u{layer}")
        conv2, blin, b2, bb = ph.sb("conv2", [D, D]), ph.sb("blin", [D, D]), ph.sb("b2", [D, 1]), ph.sb("bb", [D, 1])
        act_c = ph.sb("act_c", [D, CH])
        ssp = Ssp(nc, ph)
        ps_1, ps_2 = ph.ps("ps_1", [D, CH]), ph.ps("ps_2", [D, CH])
        q = {n: ph.sem(n) for n in ("w_in", "first_done", "first_read", "ssp_ready", "act_ready", "second_done", "updated", "summed")}
        block = ctx.enter_context(nc.Block())

        @block.sync
        def _(sp):
            for dst, src in ((conv2[:, :], ins["L3_gnn_conv2_w"][layer]), (blin[:, :], ins["L3_gnn_blin_w"][layer]),
                             (b2[:, :], ins["L3_gnn_conv2_b"][layer:layer + 1, :].rearrange("o d -> d o")),
                             (bb[:, :], ins["L3_gnn_blin_b"][layer:layer + 1, :].rearrange("o d -> d o"))):
                sp.dma_start(dst, src, allow_slow_non_contiguous=True).then_inc(q["w_in"], 16)

        @block.tensor
        def _(pe):
            pe.wait_ge(q["w_in"], 64)
            with pe.Fori(0, NCH) as c:
                pe.wait_ge(q["first_read"], c + 1)
                nc.tensor.matmul(ps_1[:, :], conv2[:, :], cols(m.acc, c * CH, CH), start=True, stop=True).then_inc(q["first_done"], 1)
                pe.wait_ge(q["act_ready"], c + 1)
                pe.wait_ge(q["updated"], c + 1)
                nc.tensor.matmul(ps_2[:, :], blin[:, :], act_c[:, :], start=True, stop=True).then_inc(q["second_done"], 1)

        @block.scalar
        def _(act):
            act.preload_act_table_set(LOG_SET)
            act.wait_ge(q["w_in"], 64)
            act.sem_inc(q["first_read"], 1)
            with act.Fori(0, NCH) as c:
                act.wait_ge(q["first_done"], c + 1)
                act.wait_ge(q["updated"], c + 1)
                nc.scalar.activation(ssp.pos[:, 0, :], ps_1[:, :], ACT.Relu, bias=b2[:, 0:1])
                nc.scalar.activation(ssp.neg[:, 0, :], ps_1[:, :], ACT.Abs, bias=b2[:, 0:1]).then_inc(q["first_read"], 1)
                act.wait_ge(q["first_read"], c + 2)
                nc.scalar.activation(ssp.log[:, 0, :], ssp.neg[:, 0, :], ACT.Exp, scale=-1.0).then_inc(ssp.chain, 1)
                act.wait_ge(ssp.chain, c + 1)
                nc.scalar.activation(ssp.log[:, 0, :], ssp.log[:, 0, :], ACT.Ln, bias=1.0).then_inc(q["ssp_ready"], 1)

        @block.vector
        def _(v):
            v.sem_inc(q["updated"], 1)
            v.wait_ge(q["w_in"], 64)

            def update(c, n):
                v.wait_ge(q["ssp_ready"], c + 1)
                ssp.vector(act_c[:, :], 0).then_inc(q["act_ready"], 1)
                v.wait_ge(q["second_done"], c + 1)
                h = cols(m.hidden, c * CH, CH)
                nc.vector.scalar_tensor_tensor(h, ps_2[:, :], bb[:, 0:1], h, ALU.add, ALU.add).then_inc(q["updated"], 1)
                v.wait_ge(q["updated"], c + 2)
                nc.vector.tensor_reduce(cols(m.sums, c, 1), m.hidden[:, bass.ds(c * CH, n)], AX, ALU.add).then_inc(q["summed"], 1)

            if NCH > 1:
                with v.Fori(0, NCH - 1) as c:
                    update(c, CH)
            update(NCH - 1, real)
            v.wait_ge(q["summed"], NCH)


def next_messages(nc, z, m, ins):
    NCH = z.chunks
    with Phase(nc) as ctx:
        ph = NodePhase(nc, ctx, "nm")
        lin1, conv1, w_a, w_b, b_lin, b1 = (ph.sb("lin1", [D, D]), ph.sb("conv1", [D, D]), ph.sb("w_a", [D, 1]),
                                            ph.sb("w_b", [D, 1]), ph.sb("b_lin", [D, 1]), ph.sb("b1", [D, 1]))
        part, total, ht, tab = ph.sb("part", [P, 1]), ph.sb("total", [P, 1]), ph.sb("ht", [D, CH]), ph.sb("tab", [P, CT, D])
        ps_h, ps_x = ph.ps("ps_h", [D, CH]), ph.ps("ps_x", [P, CT, D])
        q = {n: ph.sem(n) for n in ("w_in", "part_ready", "totalled", "step", "b_ready", "h_done", "h_copied", "h_kept", "xm_done", "table_ready", "stored")}
        block = ctx.enter_context(nc.Block())

        @block.sync
        def _(sp):
            sp.sem_inc(q["stored"], 16)
            w = ins["L3_gnn_lin1_w"]
            for dst, src in ((lin1[:, :], w[1, 2:2 + D, :]), (conv1[:, :], ins["L3_gnn_conv1_w"][1]),
                             (w_a[:, :], w[1, 0:1, :].rearrange("o d -> d o")), (w_b[:, :], w[1, 1:2, :].rearrange("o d -> d o")),
                             (b_lin[:, :], ins["L3_gnn_lin1_b"][1:2, :].rearrange("o d -> d o"))):
                sp.dma_start(dst, src, allow_slow_non_contiguous=True).then_inc(q["w_in"], 16)
            with sp.Fori(0, NCH) as c:
                sp.wait_ge(q["table_ready"], c + 2)
                sp.dma_start(rows(m.table3, c), tab[:, :, :]).then_inc(q["stored"], 16)
            sp.wait_ge(q["stored"], 16 * (NCH + 1))

        @block.gpsimd
        def _(pool):
            pool.wait_ge(q["part_ready"], 1)
            nc.gpsimd.partition_all_reduce(total[:, :], part[:, :], P, bass.bass_isa.ReduceOp.add).then_inc(q["totalled"], 1)

        @block.tensor
        def _(pe):
            pe.wait_ge(q["w_in"], 80)
            with pe.Fori(0, NCH) as c:
                pe.wait_ge(q["h_kept"], c + 1)
                nc.tensor.matmul(ps_h[:, :], lin1[:, :], cols(m.hidden, c * CH, CH), start=True, stop=True).then_inc(q["h_done"], 1)
                pe.wait_ge(q["h_copied"], c + 1)
                pe.wait_ge(q["table_ready"], c + 1)
                for k in range(CT):
                    last = nc.tensor.matmul(ps_x[:, k, :], ht[:, k * P:(k + 1) * P], conv1[:, :], start=True, stop=True)
                last.then_inc(q["xm_done"], 1)

        @block.scalar
        def _(act):
            act.sem_inc(q["h_kept"], 1)
            act.wait_ge(q["b_ready"], 1)
            with act.Fori(0, NCH) as c:
                act.wait_ge(q["h_done"], c + 1)
                act.wait_ge(q["xm_done"], c + 1)
                nc.scalar.activation(ht[:, :], ps_h[:, :], ACT.Identity, bias=b1[:, 0:1]).then_inc(q["h_copied"], 1)
                nc.scalar.activation(cols(m.hidden, c * CH, CH), ps_h[:, :], ACT.Identity, bias=b1[:, 0:1]).then_inc(q["h_kept"], 1)

        @block.vector
        def _(v):
            step = Chain(v, q["step"], 0)
            v.sem_inc(q["xm_done"], 1)
            v.sem_inc(q["table_ready"], 1)
            nc.vector.tensor_reduce(part[:, :], m.sums[:, 0:NCH], AX, ALU.add).then_inc(q["part_ready"], 1)
            v.wait_ge(q["w_in"], 80)
            v.wait_ge(q["totalled"], 1)
            step(nc.vector.tensor_scalar(total[:, :], total[:, :], 1.0 / z.nodes, None, ALU.mult))
            step(nc.vector.tensor_tensor(w_a[:, :], w_a[:, :], w_b[:, :], ALU.add))
            step(nc.vector.tensor_tensor(w_a[:, :], w_a[:, :], total[:, :], ALU.mult))
            step(nc.vector.tensor_tensor(b1[:, :], w_a[:, :], b_lin[:, :], ALU.add))
            v.sem_inc(q["b_ready"], 1)
            with v.Fori(0, NCH) as c:
                v.wait_ge(q["xm_done"], c + 2)
                v.wait_ge(q["stored"], c * 16 + 16)
                nc.vector.tensor_copy(tab[:, :, :], ps_x[:, :, :]).then_inc(q["table_ready"], 1)


def last_nodes(nc, z, m, ins, out_dram):
    NCH = z.chunks
    with Phase(nc) as ctx:
        ph = NodePhase(nc, ctx, "nl")
        w, bias = ph.sb("w", [D, D]), ph.sb("bias", [P, D])
        x, ht, y, out = ph.sb("x", [P, CT, D]), ph.sb("ht", [D, CH]), ph.sb("y", [P, CT, D]), ph.sb("out", [P, CT, D])
        ps = ph.ps("ps", [P, CT, D])
        norm = Norm(nc, ph)
        q = {n: ph.sem(n) for n in ("w_in", "x_in", "x_read", "taken", "product", "normed", "stored", "step")}
        block = ctx.enter_context(nc.Block())
        PER = 3 + LN_STEPS

        @block.sync
        def _(sp):
            sp.sem_inc(q["stored"], 16)
            sp.dma_start(w[:, :], ins["L3_gnn_out_w"]).then_inc(q["w_in"], 16)
            sp.dma_start(bias[:, :], ins["L3_gnn_out_b"].partition_broadcast(P)).then_inc(q["w_in"], 16)

            def load(c):
                sp.wait_ge(q["x_read"], c + 1)
                sp.dma_start(x[:, :, :], rows(m.x3, c)).then_inc(q["x_in"], 16)
                sp.wait_ge(q["normed"], c + 1)

            if NCH > 1:
                with sp.Fori(0, NCH - 1) as c:
                    load(c)
                    sp.dma_start(rows(out_dram, c), out[:, :, :]).then_inc(q["stored"], 16)
            load(NCH - 1)
            n = 0
            for k in range(CT):
                at = (NCH - 1) * CH + k * P
                real = min(P, z.nodes - at)
                if real > 0:
                    sp.dma_start(out_dram[at:at + real, :], out[0:real, k, :]).then_inc(q["stored"], 16)
                    n += 1
            sp.wait_ge(q["stored"], 16 * (NCH + n))

        @block.tensor
        def _(pe):
            pe.sem_inc(q["product"], 1)
            pe.wait_ge(q["w_in"], 32)
            with pe.Fori(0, NCH) as c:
                pe.wait_ge(q["taken"], c + 1)
                pe.wait_ge(q["x_read"], c + 1)
                for k in range(CT):
                    last = nc.tensor.matmul(ps[:, k, :], ht[:, k * P:(k + 1) * P], w[:, :], start=True, stop=True)
                last.then_inc(q["product"], 1)

        @block.scalar
        def _(act):
            with act.Fori(0, NCH) as c:
                act.wait_ge(q["product"], c + 1)
                nc.scalar.copy(ht[:, :], cols(m.hidden, c * CH, CH)).then_inc(q["taken"], 1)
                norm.scalar(act, c)

        @block.vector
        def _(v):
            v.sem_inc(q["x_read"], 1)
            v.wait_ge(q["w_in"], 32)
            with v.Fori(0, NCH) as c:
                step = Chain(v, q["step"], c * PER, PER)
                v.wait_ge(q["product"], c + 2)
                step(nc.vector.tensor_tensor(y[:, :, :], ps[:, :, :], bias[:, :].unsqueeze(1).to_broadcast([P, CT, D]), ALU.add))
                step(nc.vector.tensor_scalar(y[:, :, :], y[:, :, :], 0.0, None, ALU.max))
                v.wait_ge(q["x_in"], c * 16 + 16)
                step(nc.vector.tensor_tensor(y[:, :, :], y[:, :, :], x[:, :, :], ALU.add))
                v.sem_inc(q["x_read"], 1)
                v.wait_ge(q["stored"], c * 16 + 16)
                norm.vector(v, step, c, y, out)
                v.sem_inc(q["normed"], 1)
                step.done()


def build(nc, z, ins, out, layers):
    class M:
        pass

    m = M()
    with ExitStack() as ctx:
        def sb(name, shape, dt=F32):
            return ctx.enter_context(nc.sbuf_tensor(name, shape, dt))

        NT, NP = z.tiles, z.padded
        m.ident, m.lane = sb("ident", [P, P]), sb("lane", [P, P])
        m.lane_bf, m.ones = sb("lane_bf", [P, P], BF16), sb("ones", [P, P])
        m.edge_zero = sb("edge_zero", [P, 1])
        m.src_idx, m.dst_idx = sb("src_idx", [P, NT], I32), sb("dst_idx", [P, NT], I32)
        m.loc, m.last, m.w = sb("loc", [P, NT]), sb("last", [P, NT]), sb("w", [P, NT])
        m.base_row = sb("base_row", [1, NT], I32)
        m.acc = sb("acc", [P, z.cols])
        m.deg, m.scale = sb("deg", [P, 3, z.node_tiles]), sb("scale", [P, 3, z.node_tiles])

        m.x0, m.x1, m.x2, m.x3 = (nc.dram_tensor(f"x{i}", [NP, D], F32) for i in range(4))
        m.table0, m.table1, m.table3 = (nc.dram_tensor(f"table{i}", [NP, D], F32) for i in (0, 1, 3))
        m.dst_pad = nc.dram_tensor("dst_pad", [z.groups, GE], I32)
        m.bases = nc.dram_tensor("bases", [z.groups, G], I32)

        m.resets4 = nc.dram_tensor("resets4", [z.groups, HEADS * GE], F32)
        m.table2 = nc.dram_tensor("table2", [NP, ROW2], F32)
        m.dst_terms = nc.dram_tensor("dst_terms", [NP, 2 * HEADS], F32)
        m.stash = nc.dram_tensor("stash", [z.groups * P, G * ROW2], F32)
        m.att, m.p_self = sb("att", [P, z.node_tiles, 2 * HEADS]), sb("p_self", [P, z.node_tiles, HEADS])
        m.low, m.sums = sb("low", [P, 1]), sb("sums", [P, z.chunks])

        with ExitStack() as early:
            m.src_lo, m.src_hi, m.dst_lo, m.dst_hi = (early.enter_context(nc.sbuf_tensor(n, [P, NT], F32))
                                                      for n in ("src_lo", "src_hi", "dst_lo", "dst_hi"))
            prepare(nc, z, m, ins)
            degrees(nc, z, m)
        inverse_roots(nc, z, m)
        scale_rows(nc, z, m)
        sum_over_edges(nc, z, m, m.table0, None, "e0")
        layer0_nodes(nc, z, m, ins)
        if layers == 1:
            return dump(nc, z, m.x1, out)
        sum_over_edges(nc, z, m, m.table1, m.w, "e1")
        layer1_nodes(nc, z, m, ins)
        if layers == 2:
            return dump(nc, z, m.x2, out)
        lowest_source(nc, z, m)
        highest_source(nc, z, m)
        attention_nodes(nc, z, m)
        m.side = m.hidden = sb("side", [P, z.cols])
        weighted_sum(nc, z, m)
        layer2_nodes(nc, z, m, ins)
        if layers == 3:
            return dump(nc, z, m.x3, out)
        cutoffs(nc, z, m)
        continuous_conv(nc, z, m, ins, 0)
        conv_nodes(nc, z, m, ins, 0)
        next_messages(nc, z, m, ins)
        continuous_conv(nc, z, m, ins, 1)
        conv_nodes(nc, z, m, ins, 1)
        last_nodes(nc, z, m, ins, out)


def dump(nc, z, x, out):
    with nc.semaphore("dumped") as s, nc.Block() as block:
        @block.sync
        def _(sp):
            sp.dma_start(out, x[0:z.nodes, :]).then_inc(s, 16)
            sp.wait_ge(s, 16)


LAYERS = 4


def kernel(**inputs):
    import concourse.bacc as bacc
    from concourse.bass_utils import run_bass_kernel_spmd as run

    z = Sizes(inputs["x"].shape[0], inputs["src"].shape[0], inputs["edge_attr_50"].shape[1])
    nc = bacc.Bacc("TRN2", target_bir_lowering=False, num_devices=1)
    arrays, ins = {}, {}
    for name, a in inputs.items():
        a = np.ascontiguousarray(a)
        arrays[f"in_{name}"] = a
        ins[name] = nc.dram_tensor(f"in_{name}", a.shape, mybir.dt.from_np(a.dtype), kind="ExternalInput").ap()
    out = nc.dram_tensor("out", [z.nodes, D], F32, kind="ExternalOutput").ap()
    build(nc, z, ins, out, LAYERS)
    return run(nc, [arrays], core_ids=[0]).results[0]["out"]
```

```python
from contextlib import ExitStack

import numpy as np
import concourse.bass as bass
from concourse import mybir

F32 = mybir.dt.float32
BF16 = mybir.dt.bfloat16
I32 = mybir.dt.int32
ALU = mybir.AluOpType
ACT = mybir.ActivationFunctionType
AX = mybir.AxisListType.X

P = 128
D = 128
G = 8
GE = G * P
QUAD = 4
QPG = G // QUAD
QE = QUAD * P
SLOTS = 64
CT = 4
CH = CT * P
HEADS = 4
HD = D // HEADS
EPS = 1e-5
ROW2 = D + HEADS
RESET = -1.0e30
PI = float(np.pi)
LN2 = float(np.log(2.0))


def ceil_to(n, k):
    return -(-n // k) * k


class Sizes:

    def __init__(self, nodes, edges, gauss):
        self.nodes, self.edges, self.gauss = nodes, edges, gauss
        self.groups = ceil_to(-(-edges // GE), 2)
        self.half = self.groups // 2
        self.tiles = self.groups * G
        self.padded = ceil_to(nodes + 1, CH)
        self.chunks = self.padded // CH
        self.node_tiles = self.padded // P
        self.cols = self.padded + P


class Chain:

    def __init__(self, eng, sem, base, per=None):
        self.eng, self.sem, self.base, self.per, self.n = eng, sem, base, per, 0

    def go(self, ins):
        self.n += 1
        ins.then_inc(self.sem, 1)

    def wait(self):
        self.eng.wait_ge(self.sem, self.base + self.n)

    def __call__(self, ins):
        self.go(ins)
        self.wait()

    def done(self):
        assert self.per is None or self.n == self.per, self.n


class Phase(ExitStack):

    def __init__(self, nc):
        super().__init__()
        self.nc, self.sems = nc, []

    def semaphore(self, name):
        self.sems.append(self.nc.alloc_semaphore(name))
        return self.sems[-1]

    def __exit__(self, *what):
        super().__exit__(*what)
        if what[0] is None:
            self.nc.clear_and_free_semaphores(self.sems)
            self.nc.all_engine_barrier()


class Group:

    def __init__(self, no, par, rnd):
        self.no, self.par, self.rnd = no, par, rnd


def pipeline(eng, groups, depth, run):
    def static(g):
        return lambda i: Group(g + i, (g + i) % 2, (g + i) // 2) if 0 <= g + i < groups else None

    def looped(b, p):
        return lambda i: Group(b * 2 + (p + i), (p + i) % 2, b + (p + i) // 2)

    loops = max(0, (groups - depth) // 2)
    for g in range(-depth, 0):
        run(static(g))
    if loops:
        with eng.Fori(0, loops) as b:
            for p in range(2):
                run(looped(b, p))
    for g in range(2 * loops, groups):
        run(static(g))


def bc(ap, n):
    return ap.unsqueeze(2).to_broadcast([ap.shape[0], ap.shape[1], n])


def cols(t, start, size):
    return t[:, bass.ds(start, size)]



def prepare(nc, z, m, ins):
    E, HG, NT = z.edges, z.half, z.tiles
    full = E // GE - HG
    rest = E % GE
    with Phase(nc) as ctx:
        def sb(name, shape, dt=F32):
            return ctx.enter_context(nc.sbuf_tensor(name, shape, dt))

        src_i = sb("src_i", [HG, 2 * GE], I32)
        dst_i = sb("dst_i", [HG, 2 * GE], I32)
        src_f, dst_f, loc, last, change = (m.side[0:HG, i * 2 * GE:(i + 1) * 2 * GE] for i in range(5))
        w_e = sb("w_e", [HG, 2 * GE])
        lane_i = sb("lane_i", [P, P], I32)
        NQ = 2 * QPG
        lo, hi, bad, tmp = (sb(n, [HG, NQ]) for n in ("lo_q", "hi_q", "bad_q", "tmp_q"))
        badg = sb("bad_g", [HG, 2])
        base_i = sb("base_i", [HG, NQ], I32)
        lohi_i = sb("lohi_i", [P, NT], I32)
        zeros = sb("zeros", [P, D])
        ps = [ctx.enter_context(nc.psum_tensor(f"prep_ps{i}", [P, 4, P], F32)) for i in range(4)]

        sem = {n: ctx.semaphore(n) for n in (
            "edges_in", "padded", "consts", "ident_zero", "prep_step", "moved", "copied", "spilled",
            "rows_padded", "tables", "weights_in", "lanes")}

        def whole(t):
            return t[:, :].rearrange("p (h n) -> p h n", h=2)

        tile3 = lambda t: t[:, :].rearrange("p (t e) -> p t e", e=P)
        quad3 = lambda t: t[:, :].rearrange("p (q e) -> p q e", e=QE)
        block = ctx.enter_context(nc.Block())
        moves = [(src_f, m.src_idx), (dst_f, m.dst_idx), (loc, m.loc), (last, m.last), (w_e, m.w)]
        n_edge_dmas = 3 * (1 + (full > 0) + (rest > 0))

        @block.sync
        def _(sp):
            sp.wait_ge(sem["padded"], 4)
            for name, t in (("src", src_i), ("dst", dst_i), ("edge_weight", w_e)):
                a = ins[name]
                sp.dma_start(t[:, 0:GE], a[0:HG * GE].rearrange("(p n) -> p n", n=GE)).then_inc(sem["edges_in"], 16)
                if full:
                    sp.dma_start(t[0:full, GE:2 * GE], a[HG * GE:(HG + full) * GE].rearrange("(p n) -> p n", n=GE)).then_inc(sem["edges_in"], 16)
                if rest:
                    at = (HG + full) * GE
                    sp.dma_start(t[full:full + 1, GE:GE + rest], a[at:E].rearrange("(p n) -> p n", p=1)).then_inc(sem["edges_in"], 16)
            n = 0
            sp.dma_start(m.x0[0:z.nodes, :], ins["x"]).then_inc(sem["rows_padded"], 16)
            n += 1
            for at in range(z.nodes, z.padded, P):
                k = min(P, z.padded - at)
                sp.dma_start(m.x0[at:at + k, :], zeros[0:k, :]).then_inc(sem["rows_padded"], 16)
                n += 1
            sp.wait_ge(sem["edges_in"], 16 * n_edge_dmas)
            for h in range(2):
                sp.dma_start(m.dst_pad[h * HG:(h + 1) * HG, :], dst_i[:, h * GE:(h + 1) * GE]).then_inc(sem["spilled"], 16)
            sp.wait_ge(sem["tables"], 2)
            for h in range(2):
                for r_ in range(HEADS):
                    sp.dma_start(m.resets4[h * HG:(h + 1) * HG, :].rearrange("g (k r e) -> g k r e", r=HEADS, e=P)[:, :, r_, :],
                                 change[:, h * GE:(h + 1) * GE].rearrange("g (k e) -> g k e", e=P)).then_inc(sem["spilled"], 16)
                sp.dma_start(m.bases[h * HG:(h + 1) * HG, :], base_i[:, h * QPG:(h + 1) * QPG]).then_inc(sem["spilled"], 16)
            n_spilled = 2 * (1 + HEADS + 1)
            sp.wait_ge(sem["spilled"], 16 * n_spilled)
            sp.dma_start(m.base_row[:, :], m.bases[:, :].rearrange("g k -> (g k)").rearrange("(o n) -> o n", o=1)).then_inc(sem["spilled"], 16)
            sp.wait_ge(sem["spilled"], 16 * (n_spilled + 1))
            sp.wait_ge(sem["rows_padded"], 16 * n)

        @block.gpsimd
        def _(pool):
            nc.gpsimd.memset(m.ident[:, :], 0.0).then_inc(sem["ident_zero"], 1)
            pool.wait_ge(sem["ident_zero"], 1)
            nc.gpsimd.affine_select(out=m.ident[:, :], in_=m.ident[:, :], compare_op=ALU.not_equal, fill=1.0,
                                    base=0, pattern=[[-1, P]], channel_multiplier=1).then_inc(sem["consts"], 1)
            nc.gpsimd.iota(lane_i[:, :], pattern=[[1, P]], base=0, channel_multiplier=0).then_inc(sem["consts"], 1)

        @block.tensor
        def _(pe):
            pe.wait_ge(sem["consts"], 1)
            pe.wait_ge(sem["tables"], 2)
            i = 0
            for src, _ in moves:
                for h in range(2):
                    for q in range(2):
                        if i >= 4:
                            pe.wait_ge(sem["copied"], i - 3)
                        for k in range(4):
                            at = h * GE + (q * 4 + k) * P
                            last_one = nc.tensor.transpose(ps[i % 4][:, k, 0:HG], src[:, at:at + P], m.ident[0:HG, 0:HG])
                        last_one.then_inc(sem["moved"], 1)
                        i += 1

        @block.vector
        def _(v):
            step = Chain(v, sem["prep_step"], 0)
            nc.vector.memset(src_i[:, :], z.nodes).then_inc(sem["padded"], 1)
            nc.vector.memset(dst_i[:, :], z.nodes).then_inc(sem["padded"], 1)
            nc.vector.memset(w_e[:, :], 0.0).then_inc(sem["padded"], 1)
            nc.vector.memset(zeros[:, :], 0.0).then_inc(sem["padded"], 1)
            step(nc.vector.memset(m.ones[:, :], 1.0))
            v.wait_ge(sem["consts"], 2)
            step(nc.vector.tensor_copy(m.lane[:, :], lane_i[:, :]))
            step(nc.vector.tensor_copy(m.lane_bf[:, :], lane_i[:, :]))
            v.wait_ge(sem["edges_in"], 16 * n_edge_dmas)
            step(nc.vector.tensor_copy(src_f[:, :], src_i[:, :]))
            step(nc.vector.tensor_copy(dst_f[:, :], dst_i[:, :]))
            l3, c3, e3 = tile3(loc), tile3(change), tile3(last)
            dq, lq, cq = quad3(dst_f), quad3(loc), quad3(change)
            step(nc.vector.tensor_reduce(lo[:, :], dq, AX, ALU.min))
            step(nc.vector.tensor_reduce(hi[:, :], dq, AX, ALU.max))
            step(nc.vector.tensor_tensor(cq[:, :, 1:QE], dq[:, :, 1:QE], dq[:, :, 0:QE - 1], ALU.subtract))
            step(nc.vector.tensor_reduce(tmp[:, :], cq[:, :, 1:QE], AX, ALU.min))
            step(nc.vector.tensor_scalar(tmp[:, :], tmp[:, :], 0.0, None, ALU.is_lt))
            step(nc.vector.tensor_tensor(hi[:, :], hi[:, :], lo[:, :], ALU.subtract))
            step(nc.vector.tensor_scalar(hi[:, :], hi[:, :], float(SLOTS), None, ALU.is_ge))
            step(nc.vector.tensor_tensor(hi[:, :], hi[:, :], tmp[:, :], ALU.max))
            step(nc.vector.tensor_reduce(badg[:, :], hi[:, :].rearrange("p (h k) -> p h k", h=2), AX, ALU.max))
            step(nc.vector.tensor_copy(bad[:, :].rearrange("p (h k) -> p h k", h=2), bc(badg[:, :], QPG)))
            step(nc.vector.tensor_tensor(lq, dq, bc(lo[:, :], QE), ALU.subtract))
            step(nc.vector.tensor_tensor(c3, m.lane[0:HG, :].unsqueeze(1).to_broadcast([HG, 2 * G, P]), l3, ALU.subtract))
            step(nc.vector.tensor_tensor(cq, cq, bc(bad[:, :], QE), ALU.mult))
            step(nc.vector.tensor_tensor(l3, l3, c3, ALU.add))
            step(nc.vector.tensor_scalar(tmp[:, :], lo[:, :], 1.0, None, ALU.add))
            step(nc.vector.tensor_tensor(tmp[:, :], tmp[:, :], bad[:, :], ALU.mult))
            step(nc.vector.tensor_tensor(tmp[:, :], lo[:, :], tmp[:, :], ALU.subtract))
            step(nc.vector.tensor_copy(base_i[:, :], tmp[:, :]))
            step(nc.vector.tensor_tensor(c3[:, :, 1:P], l3[:, :, 1:P], l3[:, :, 0:P - 1], ALU.not_equal))
            step(nc.vector.memset(c3[:, :, 0:1], 1.0))
            step(nc.vector.tensor_scalar(e3[:, :, 0:P - 1], l3[:, :, 0:P - 1], 1.0, None, ALU.add))
            step(nc.vector.tensor_tensor(e3[:, :, 0:P - 1], e3[:, :, 0:P - 1], c3[:, :, 1:P], ALU.mult))
            step(nc.vector.tensor_scalar(e3[:, :, 0:P - 1], e3[:, :, 0:P - 1], -1.0, None, ALU.add))
            step(nc.vector.tensor_copy(e3[:, :, P - 1:P], l3[:, :, P - 1:P]))
            nc.vector.tensor_scalar(change[:, :], change[:, :], RESET, None, ALU.mult).then_inc(sem["tables"], 1)
            v.wait_ge(sem["tables"], 1)
            v.sem_inc(sem["tables"], 1)
            i = 0
            for _, table in moves:
                for h in range(2):
                    for q in range(2):
                        v.wait_ge(sem["moved"], i + 1)
                        out = table[:, 0:NT].rearrange("p (h g k) -> p h k g", h=2, k=G)[:, h, q * 4:q * 4 + 4, :]
                        nc.vector.tensor_copy(out, ps[i % 4][:, :, 0:HG]).then_inc(sem["copied"], 1)
                        i += 1
            v.wait_ge(sem["copied"], i)
            step(nc.vector.tensor_scalar(lohi_i[:, :], m.src_idx[:, 0:NT], P - 1, None, ALU.bitwise_and))
            step(nc.vector.tensor_copy(m.src_lo[:, :], lohi_i[:, :]))
            step(nc.vector.tensor_scalar(lohi_i[:, :], m.src_idx[:, 0:NT], 7, None, ALU.logical_shift_right))
            step(nc.vector.tensor_copy(m.src_hi[:, :], lohi_i[:, :]))



def out_degrees(nc, z, m):
    NPT = z.node_tiles
    with Phase(nc) as ctx:
        def sb(name, shape, dt=F32):
            return ctx.enter_context(nc.sbuf_tensor(name, shape, dt))

        low, high = sb("low1", [P, 2, G, P], BF16), sb("high1", [P, 2, G, NPT], BF16)
        low_t, high_t = sb("low_t", [P, z.tiles], BF16), sb("high_t", [P, z.tiles], BF16)
        ps = [ctx.enter_context(nc.psum_tensor(f"ps_deg{i}", [P, NPT], F32)) for i in range(2)]
        hot_ready = [ctx.semaphore(f"hot_ready{i}") for i in range(2)]
        summed = [ctx.semaphore(f"summed{i}") for i in range(2)]
        added, cast = ctx.semaphore("hist_added"), ctx.semaphore("hist_cast")
        block = ctx.enter_context(nc.Block())

        @block.vector
        def _(v):
            nc.vector.tensor_copy(low_t[:, :], m.src_lo[:, :]).then_inc(cast, 1)
            nc.vector.tensor_copy(high_t[:, :], m.src_hi[:, :]).then_inc(cast, 1)
            nc.vector.memset(m.deg[:, :, :], 0.0).then_inc(added, 1)
            v.wait_ge(cast, 2)

            def run(f):
                if a := f(1):
                    v.wait_ge(summed[a.par], a.rnd + 1)
                    lanes = lambda n: m.lane_bf[:, 0:n].unsqueeze(1).to_broadcast([P, G, n])
                    nc.vector.tensor_tensor(low[:, a.par, :, :], lanes(P), bc(cols(low_t, a.no * G, G), P), ALU.is_equal)
                    nc.vector.tensor_tensor(high[:, a.par, :, :], lanes(NPT), bc(cols(high_t, a.no * G, G), NPT), ALU.is_equal).then_inc(hot_ready[a.par], 1)
                if g := f(0):
                    v.wait_ge(summed[g.par], g.rnd + 2)
                    v.wait_ge(added, g.no + 1)
                    nc.vector.tensor_tensor(m.deg[:, 0, :], m.deg[:, 0, :], ps[g.par][:, :], ALU.add).then_inc(added, 1)

            pipeline(v, z.groups, 1, run)
            v.wait_ge(added, z.groups + 1)

        @block.tensor
        def _(pe):
            for par in range(2):
                pe.sem_inc(summed[par], 1)

            def run(f):
                g = f(0)
                pe.wait_ge(hot_ready[g.par], g.rnd + 1)
                for k in range(G):
                    last = nc.tensor.matmul(ps[g.par][:, :], low[:, g.par, k, :], high[:, g.par, k, :], start=(k == 0), stop=(k == G - 1))
                last.then_inc(summed[g.par], 1)

            pipeline(pe, z.groups, 0, run)


def inverse_roots(nc, z, m, which):
    NPT = z.node_tiles
    a, b = which.start, which.stop
    with Phase(nc) as ctx:
        root, t = (ctx.enter_context(nc.sbuf_tensor(f"{n}{a}", [P, b - a, NPT], F32)) for n in ("root", "root_t"))
        count_t = ctx.enter_context(nc.sbuf_tensor(f"count_t{a}", [NPT, P], F32))
        ps = ctx.enter_context(nc.psum_tensor(f"count_ps{a}", [P, NPT], F32))
        counts, prepared, rooted, stepped, turned = (ctx.semaphore(f"{n}{a}") for n in ("counts_in", "deg_prepared", "deg_rooted", "deg_step", "deg_turned"))
        block = ctx.enter_context(nc.Block())
        in_degree = b > 2

        if in_degree:
            @block.sync
            def _(sp):
                sp.dma_start(m.counts[:, :], m.side[0:1, 0:z.padded]).then_inc(counts, 16)
                sp.wait_ge(counts, 16)
                sp.dma_start(count_t[:, :], m.counts[:, :].rearrange("o (t p) -> (o t) p", p=P)).then_inc(counts, 16)

            @block.tensor
            def _(pe):
                pe.wait_ge(counts, 32)
                nc.tensor.transpose(ps[:, :], count_t[:, :], m.ident[0:NPT, 0:NPT]).then_inc(turned, 1)

        @block.scalar
        def _(act):
            act.wait_ge(prepared, 1)
            nc.scalar.activation(root[:, :, :], m.deg[:, a:b, :], ACT.Sqrt).then_inc(rooted, 1)

        @block.vector
        def _(v):
            step = Chain(v, stepped, 0)
            for i in which:
                if i == 2:
                    v.wait_ge(turned, 1)
                    step(nc.vector.tensor_copy(m.deg[:, 2, :], ps[:, :]))
                step(nc.vector.tensor_scalar(m.deg[:, i, :], m.deg[:, i, :], 1.0, None, ALU.add if i == 1 else ALU.max))
            v.sem_inc(prepared, 1)
            v.wait_ge(rooted, 1)
            newton(nc, step, m.scale[:, a:b, :], m.deg[:, a:b, :], root[:, :, :], t[:, :, :])


def newton(nc, step, out, x, root, t):
    step(nc.vector.reciprocal(out, root))
    step(nc.vector.tensor_tensor(t, out, out, ALU.mult))
    step(nc.vector.tensor_tensor(t, t, x, ALU.mult))
    step(nc.vector.tensor_scalar(t, t, -0.5, 1.5, ALU.mult, ALU.add))
    step(nc.vector.tensor_tensor(out, out, t, ALU.mult))


NEWTON_STEPS = 5


def rows(table, c, width=D):
    return table[bass.ds(c * CH, CH), 0:width].rearrange("(k p) f -> p k f", p=P)


def scale_rows(nc, z, m):
    with Phase(nc) as ctx:
        xin = ctx.enter_context(nc.sbuf_tensor("sr_x", [P, 2, CT, D], F32))
        out = ctx.enter_context(nc.sbuf_tensor("sr_y", [P, 2, CT, D], F32))
        x_in = [ctx.semaphore(f"sr_x_in{i}") for i in range(2)]
        stored = [ctx.semaphore(f"sr_stored{i}") for i in range(2)]
        scaled = [ctx.semaphore(f"sr_scaled{i}") for i in range(2)]
        block = ctx.enter_context(nc.Block())

        @block.sync
        def _(sp):
            for c in range(z.chunks):
                if c >= 2:
                    sp.wait_ge(scaled[c % 2], c // 2)
                sp.dma_start(xin[:, c % 2, :, :], rows(m.x0, c)).then_inc(x_in[c % 2], 16)

        @block.vector
        def _(v):
            for c in range(z.chunks):
                v.wait_ge(x_in[c % 2], 16 * (c // 2 + 1))
                if c >= 2:
                    v.wait_ge(stored[c % 2], 16 * (c // 2))
                last = nc.vector.tensor_tensor(out[:, c % 2, :, :], xin[:, c % 2, :, :], bc(m.scale[:, 0, c * CT:(c + 1) * CT], D), ALU.mult)
                last.then_inc(scaled[c % 2], 1)

        @block.scalar
        def _(act):
            for c in range(z.chunks):
                act.wait_ge(scaled[c % 2], c // 2 + 1)
                act.dma_start(rows(m.table0, c), out[:, c % 2, :, :]).then_inc(stored[c % 2], 16)
            for i in range(2):
                act.wait_ge(stored[i], 16 * ((z.chunks + 1 - i) // 2))



class Windows:

    def __init__(self, nc, ctx, m, z, name, targets, apart=False):
        self.nc, self.m, self.z, self.name, self.targets, self.apart = nc, m, z, name, targets, apart
        self.n = G if apart else QPG
        self.added = [ctx.semaphore(f"{name}_added{i}") for i in range(len(targets))]
        self.hot_written = ctx.semaphore(f"{name}_hot_written")
        self.begun = ctx.semaphore(f"{name}_begun")

    def registers(self, v):
        self.bases = [[v.alloc_register(f"{self.name}_base{p}{k}") for k in range(QPG)] for p in range(2)]
        self.dst = v.alloc_register(f"{self.name}_dst")

    def clear(self):
        for (target, _, n, _), added in zip(self.targets, self.added):
            self.nc.vector.memset(target[0:n, :], 0.0).then_inc(added, 1)

    def free(self, eng, g):
        for added in self.added:
            eng.wait_ge(added, g.no * self.n + 1)

    def finish(self, v):
        for added in self.added:
            v.wait_ge(added, self.z.groups * self.n + 1)

    def one_hot(self, v, g, hot, slot, weights=None):
        nc, m = self.nc, self.m
        v.load(self.bases[g.par], m.base_row[0:1, bass.ds(g.no * QPG, QPG)])

        def write(width):
            if weights is None:
                last = nc.vector.tensor_tensor(hot[:, g.par, :, 0:width], m.lane[:, 0:width].unsqueeze(1).to_broadcast([P, G, width]),
                                               bc(cols(slot, g.no * G, G), width), ALU.is_equal)
            else:
                for k in range(G):
                    t = g.no * G + k
                    last = nc.vector.tensor_scalar(hot[:, g.par, k, 0:width], m.lane[:, 0:width], cols(slot, t, 1), cols(weights, t, 1),
                                                   ALU.is_equal, ALU.mult)
            return last

        with v.If_lt(self.bases[g.par][0], 0):
            write(P).then_inc(self.hot_written, 1)
        with v.Else():
            write(SLOTS).then_inc(self.hot_written, 1)

    def hot_ready(self, eng, g):
        eng.wait_ge(self.hot_written, g.no + 1)

    def product(self, pe, g, reg, pairs, hot):
        nc = self.nc
        pe.load(reg, self.m.base_row[0:1, bass.ds(g.no * QPG, 1)])
        with pe.If_lt(reg, 0):
            for k in range(G):
                for out, left in pairs:
                    nc.tensor.matmul(out[:, k * P:(k + 1) * P], left(k), hot[:, g.par, k, :], start=True, stop=True)
        with pe.Else():
            for k in range(G):
                for out, left in pairs:
                    at = k * P if self.apart else k // QUAD * SLOTS
                    nc.tensor.matmul(out[:, at:at + SLOTS], left(k), hot[:, g.par, k, 0:SLOTS],
                                     start=self.apart or k % QUAD == 0, stop=self.apart or k % QUAD == QUAD - 1)

    def add(self, v, g):
        nc, z, m = self.nc, self.z, self.m
        v.sem_inc(self.begun, 1)
        with v.If_lt(self.bases[g.par][0], 0):
            self.free(v, g)
            v.sem_inc(self.begun, 1)
            with v.Fori(0, GE) as e:
                v.load(self.dst, m.dst_pad[bass.ds(g.no, 1), bass.ds(e, 1)])
                col = v.snap(self.dst, min_val=0, max_val=z.cols - 1)
                for target, source, n, op in self.targets:
                    nc.vector.tensor_tensor(target[0:n, bass.ds(col, 1)], target[0:n, bass.ds(col, 1)],
                                            source[0:n, bass.ds(e, 1)], op)
                v.drain()
            for added in self.added:
                v.drain().then_inc(added, self.n)
        with v.Else():
            for i in range(self.n):
                at, quad = (i * P, i // QUAD) if self.apart else (i * SLOTS, i)
                base = v.snap(self.bases[g.par][quad], min_val=0, max_val=z.cols - P)
                for (target, source, n, op), added in zip(self.targets, self.added):
                    v.wait_ge(added, g.no * self.n + i + 1)
                    nc.vector.tensor_tensor(target[0:n, bass.ds(base, SLOTS)], target[0:n, bass.ds(base, SLOTS)],
                                            source[0:n, at:at + SLOTS], op).then_inc(added, 1)


def gather(nc, pool, table, idx, out, g, landed):
    for k in range(G):
        pool.indirect_dma_start(out=out[:, g.par, k, :], out_offset=None, in_=table[:, :],
                                in_offset=bass.IndirectOffsetOnAxis(ap=idx[:, g.par, k:k + 1], axis=0)).then_inc(landed[g.par], 16)


def sum_over_edges(nc, z, m, table, weights, name, degrees=False):
    NPT = z.node_tiles
    with Phase(nc) as ctx:
        sb = lambda n, shape, dt=F32: ctx.enter_context(nc.sbuf_tensor(f"{name}_{n}", shape, dt))
        psum = lambda n, shape: ctx.enter_context(nc.psum_tensor(f"{name}_{n}", shape, F32))
        rows_, hot, idx = sb("rows", [P, 2, G, D]), sb("hot", [P, 2, G, P]), sb("idx", [P, 2, G], I32)
        ps = psum("ps", [P, GE])
        targets = [(m.acc, ps, P, ALU.add)]
        if degrees:
            low, high = sb("low", [P, 2, G, P]), sb("high", [P, 2, G, NPT])
            ps_count = psum("ps_count", [1, GE])
            ps_w = [psum(f"ps_w{i}", [P, NPT]) for i in range(2)]
            targets.append((m.side, ps_count, 1, ALU.add))
        two = lambda n: [ctx.semaphore(f"{name}_{n}{i}") for i in range(2)]
        idx_staged, rows_in, summed, hist_ready = two("idx_staged"), two("rows_in"), two("summed"), two("hist_ready")
        gather_begun, hist_added = ctx.semaphore(f"{name}_gather_begun"), ctx.semaphore(f"{name}_hist_added")
        windows = Windows(nc, ctx, m, z, name, targets)
        block = ctx.enter_context(nc.Block())

        @block.scalar
        def _(act):
            def run(f):
                g = f(0)
                act.wait_ge(summed[g.par], g.rnd + 1)
                nc.scalar.copy(idx[:, g.par, :], cols(m.src_idx, g.no * G, G)).then_inc(idx_staged[g.par], 1)

            pipeline(act, z.groups, 0, run)

        @block.gpsimd
        def _(pool):
            def run(f):
                g = f(0)
                pool.wait_ge(idx_staged[g.par], g.rnd + 1)
                pool.wait_ge(summed[g.par], g.rnd + 1)
                pool.sem_inc(gather_begun, 1)
                gather(nc, pool, table, idx, rows_, g, rows_in)

            pipeline(pool, z.groups, 0, run)

        @block.tensor
        def _(pe):
            reg = pe.alloc_register(f"{name}_pe_base")
            for par in range(2):
                pe.sem_inc(summed[par], 1)

            def run(f):
                g = f(0)
                pairs = [(ps, lambda k: rows_[:, g.par, k, :])]
                if degrees:
                    pairs.append((ps_count, lambda k: m.ones[:, 0:1]))
                    pe.wait_ge(hist_ready[g.par], g.rnd + 1)
                    for k in range(G):
                        nc.tensor.matmul(ps_w[g.par][:, :], low[:, g.par, k, :], high[:, g.par, k, :], start=(k == 0), stop=(k == G - 1))
                windows.hot_ready(pe, g)
                pe.wait_ge(rows_in[g.par], (g.rnd + 1) * (16 * G))
                windows.free(pe, g)
                windows.product(pe, g, reg, pairs, hot)
                pe.drain().then_inc(summed[g.par], 1)

            pipeline(pe, z.groups, 0, run)

        @block.vector
        def _(v):
            windows.registers(v)
            windows.clear()
            v.sem_inc(hist_added, 1)

            def run(f):
                if a := f(1):
                    v.wait_ge(summed[a.par], a.rnd + 1)
                    windows.one_hot(v, a, hot, m.loc, weights)
                    if degrees:
                        for k in range(G):
                            t = a.no * G + k
                            nc.vector.tensor_scalar(low[:, a.par, k, :], m.lane[:, :], cols(m.src_lo, t, 1), None, ALU.is_equal)
                            last = nc.vector.tensor_scalar(high[:, a.par, k, :], m.lane[:, 0:NPT], cols(m.src_hi, t, 1), cols(m.w, t, 1),
                                                           ALU.is_equal, ALU.mult)
                        last.then_inc(hist_ready[a.par], 1)
                if g := f(0):
                    v.wait_ge(summed[g.par], g.rnd + 2)
                    windows.add(v, g)
                    if degrees:
                        v.wait_ge(hist_added, g.no + 1)
                        nc.vector.tensor_tensor(m.deg[:, 1, :], m.deg[:, 1, :], ps_w[g.par][:, :], ALU.add).then_inc(hist_added, 1)

            pipeline(v, z.groups, 1, run)
            windows.finish(v)
            if degrees:
                v.wait_ge(hist_added, z.groups + 1)



class NodePhase:

    def __init__(self, nc, ctx, name):
        self.nc, self.ctx, self.name = nc, ctx, name

    def sb(self, name, shape, dt=F32):
        return self.ctx.enter_context(self.nc.sbuf_tensor(f"{self.name}_{name}", shape, dt))

    def ps(self, name, shape):
        return self.ctx.enter_context(self.nc.psum_tensor(f"{self.name}_{name}", shape, F32))

    def sem(self, name):
        return self.ctx.semaphore(f"{self.name}_{name}")


LN_STEPS = 2 * CT + 1 + NEWTON_STEPS + CT


class Norm:

    def __init__(self, nc, ph):
        self.nc = nc
        self.stats = ph.sb("stats", [P, CT, 6])
        self.mv = ph.sb("meanvar", [P, CT, 2])
        self.var = ph.sb("var", [P, CT])
        self.root = ph.sb("rootv", [P, CT])
        self.rstd = ph.sb("rstd", [P, CT])
        self.t = ph.sb("rstd_t", [P, CT])
        self.var_ready = ph.sem("var_ready")
        self.root_ready = ph.sem("root_ready")
        self.stats_taken = ph.sem("stats_taken")

    def vector(self, v, step, c, y, out):
        nc = self.nc
        for k in range(CT):
            step.go(nc.vector.bn_stats(self.stats[:, k, :], y[:, k, :]))
        step.wait()
        v.sem_inc(self.stats_taken, 1)
        for k in range(CT):
            step.go(nc.vector.bn_aggr(self.mv[:, k, :], self.stats[:, k, :]))
        step.wait()
        step(nc.vector.tensor_scalar(self.var[:, :], self.mv[:, :, 1], EPS, None, ALU.add))
        v.sem_inc(self.var_ready, 1)
        v.wait_ge(self.root_ready, c + 1)
        newton(nc, step, self.rstd[:, :], self.var[:, :], self.root[:, :], self.t[:, :])
        for k in range(CT):
            step(nc.vector.tensor_scalar(out[:, k, :], y[:, k, :], self.mv[:, k, 0:1], self.rstd[:, k:k + 1], ALU.subtract, ALU.mult))

    def scalar(self, act, c):
        act.wait_ge(self.var_ready, c + 1)
        self.nc.scalar.activation(self.root[:, :], self.var[:, :], ACT.Sqrt).then_inc(self.root_ready, 1)


def layer0_nodes(nc, z, m, ins):
    NCH = z.chunks
    with Phase(nc) as ctx:
        ph = NodePhase(nc, ctx, "n0")
        w_self, w_inter = ph.sb("w_self", [D, D]), ph.sb("w_inter", [D, D])
        x = ph.sb("x", [P, CT, D])
        acc_c, xt, hx = ph.sb("acc_c", [D, CH]), ph.sb("xt", [D, CH]), ph.sb("hx", [D, CH])
        y, out, tab = ph.sb("y", [P, CT, D]), ph.sb("out", [P, CT, D]), ph.sb("tab", [P, CT, D])
        ps_t, ps_a, ps_b = ph.ps("ps_t", [D, CH]), ph.ps("ps_a", [P, CT, D]), ph.ps("ps_b", [P, CT, D])
        norm = Norm(nc, ph)
        w_in, x_in, stored, turned, acc_taken, ready, product, step_s, out_ready, x_read, root2 = (ph.sem(n) for n in (
            "w_in", "x_in", "stored", "turned", "acc_taken", "ready", "product", "step", "out_ready", "x_read", "root2"))
        block = ctx.enter_context(nc.Block())
        PER = 2 + CT + 1 + LN_STEPS + CT

        @block.sync
        def _(sp):
            sp.sem_inc(stored, 32)
            sp.dma_start(w_self[:, :], ins["L0_gnn_W_self"]).then_inc(w_in, 16)
            sp.dma_start(w_inter[:, :], ins["L0_gnn_W_inter"]).then_inc(w_in, 16)
            with sp.Fori(0, NCH) as c:
                sp.wait_ge(x_read, c + 1)
                sp.dma_start(x[:, :, :], rows(m.x0, c)).then_inc(x_in, 16)
                sp.wait_ge(out_ready, c + 1)
                sp.dma_start(rows(m.x1, c), out[:, :, :]).then_inc(stored, 16)
                sp.dma_start(rows(m.table1, c), tab[:, :, :]).then_inc(stored, 16)
            sp.wait_ge(stored, 32 * (NCH + 1))

        @block.tensor
        def _(pe):
            pe.sem_inc(product, 1)
            pe.wait_ge(w_in, 32)
            with pe.Fori(0, NCH) as c:
                pe.wait_ge(x_in, (c + 1) * 16)
                for k in range(CT):
                    last = nc.tensor.transpose(ps_t[:, k * P:(k + 1) * P], x[:, k, :], m.ident[:, :])
                last.then_inc(turned, 1)
                pe.wait_ge(ready, c + 1)
                for k in range(CT):
                    at = slice(k * P, (k + 1) * P)
                    nc.tensor.matmul(ps_a[:, k, :], acc_c[:, at], w_self[:, :], start=True, stop=False)
                    nc.tensor.matmul(ps_a[:, k, :], hx[:, at], w_inter[:, :], start=False, stop=True)
                    last = nc.tensor.matmul(ps_b[:, k, :], xt[:, at], w_self[:, :], start=True, stop=True)
                last.then_inc(product, 1)

        @block.scalar
        def _(act):
            with act.Fori(0, NCH) as c:
                act.wait_ge(product, c + 1)
                nc.scalar.copy(acc_c[:, :], cols(m.acc, c * CH, CH)).then_inc(acc_taken, 1)
                norm.scalar(act, c)

        @block.vector
        def _(v):
            v.sem_inc(x_read, 1)
            with v.Fori(0, NCH) as c:
                step = Chain(v, step_s, c * PER, PER)
                v.wait_ge(turned, c + 1)
                v.wait_ge(product, c + 1)
                step(nc.vector.tensor_copy(xt[:, :], ps_t[:, :]))
                v.wait_ge(acc_taken, c + 1)
                step(nc.vector.tensor_tensor(hx[:, :], acc_c[:, :], xt[:, :], ALU.mult))
                v.sem_inc(ready, 1)
                v.wait_ge(product, c + 2)
                for k in range(CT):
                    step(nc.vector.scalar_tensor_tensor(y[:, k, :], ps_a[:, k, :], cols(m.scale[:, 2, :], c * CT + k, 1), x[:, k, :], ALU.mult, ALU.add))
                v.sem_inc(x_read, 1)
                step(nc.vector.tensor_tensor(y[:, :, :], y[:, :, :], ps_b[:, :, :], ALU.add))
                v.wait_ge(stored, c * 32 + 32)
                norm.vector(v, step, c, y, out)
                for k in range(CT):
                    step(nc.vector.tensor_scalar(tab[:, k, :], out[:, k, :], cols(m.scale[:, 1, :], c * CT + k, 1), None, ALU.mult))
                v.sem_inc(out_ready, 1)
                step.done()



def layer1_nodes(nc, z, m, ins):
    NCH = z.chunks
    with Phase(nc) as ctx:
        ph = NodePhase(nc, ctx, "n1")
        w_raw, w_t, w2 = ph.sb("w_raw", [D, D]), ph.sb("w_t", [D, D]), ph.sb("w2", [D, D])
        att, bias = ph.sb("att", [D, 2 * HEADS]), ph.sb("bias", [P, D])
        x, tab_in = ph.sb("x", [P, CT, D]), ph.sb("tab_in", [P, CT, D])
        acc_s, xt, ht = ph.sb("acc_s", [D, CH]), ph.sb("xt", [D, CH]), ph.sb("ht", [D, CH])
        y, out, tab = ph.sb("y", [P, CT, D]), ph.sb("out", [P, CT, D]), ph.sb("tab", [P, CT, ROW2])
        ps_t, ps_a, ps_u = ph.ps("ps_t", [D, CH]), ph.ps("ps_a", [P, CT, D]), ph.ps("ps_u", [D, CH])
        ps_h, ps_ht, ps_att = ph.ps("ps_h", [P, CT, D]), ph.ps("ps_ht", [D, CH]), ph.ps("ps_att", [P, CT, 2 * HEADS])
        norm = Norm(nc, ph)
        names = ("w_in", "att_zero", "w_turned", "w_copied", "rows_in", "stored", "tab_turned", "acc_ready", "product",
                 "normed", "x2_turned", "x2_copied", "h_done", "ht_copied", "att_done", "table_ready", "step")
        q = {n: ph.sem(n) for n in names}
        block = ctx.enter_context(nc.Block())
        PER = 1 + CT + 1 + LN_STEPS + 1 + 3

        @block.sync
        def _(sp):
            sp.sem_inc(q["stored"], 32)
            sp.dma_start(w_raw[:, :], ins["L1_gnn_W"]).then_inc(q["w_in"], 16)
            sp.dma_start(w2[:, :], ins["L2_gnn_W"]).then_inc(q["w_in"], 16)
            sp.dma_start(bias[:, :], ins["L1_gnn_b"].partition_broadcast(P)).then_inc(q["w_in"], 16)
            sp.wait_ge(q["att_zero"], 1)
            for h in range(HEADS):
                for i, name in enumerate(("L2_gnn_att_src", "L2_gnn_att_dst")):
                    sp.dma_start(att[h * HD:(h + 1) * HD, i * HEADS + h:i * HEADS + h + 1],
                                 ins[name][h:h + 1, :].rearrange("o c -> c o"), allow_slow_non_contiguous=True).then_inc(q["w_in"], 16)
            with sp.Fori(0, NCH) as c:
                sp.wait_ge(q["normed"], c + 1)
                sp.dma_start(x[:, :, :], rows(m.x1, c)).then_inc(q["rows_in"], 16)
                sp.dma_start(tab_in[:, :, :], rows(m.table1, c)).then_inc(q["rows_in"], 16)
                sp.wait_ge(q["table_ready"], c + 1)
                sp.dma_start(rows(m.x2, c), out[:, :, :]).then_inc(q["stored"], 16)
                sp.dma_start(rows(m.table2, c, ROW2), tab[:, :, :]).then_inc(q["stored"], 16)
            sp.wait_ge(q["stored"], 32 * (NCH + 1))

        @block.tensor
        def _(pe):
            pe.wait_ge(q["w_in"], 16 * (3 + 2 * HEADS))
            nc.tensor.transpose(ps_t[:, 0:D], w_raw[:, :], m.ident[:, :]).then_inc(q["w_turned"], 1)
            pe.wait_ge(q["w_copied"], 1)
            with pe.Fori(0, NCH) as c:
                pe.wait_ge(q["rows_in"], (c + 1) * 32)
                for k in range(CT):
                    last = nc.tensor.transpose(ps_t[:, k * P:(k + 1) * P], tab_in[:, k, :], m.ident[:, :])
                last.then_inc(q["tab_turned"], 1)
                pe.wait_ge(q["acc_ready"], c + 1)
                for k in range(CT):
                    last = nc.tensor.matmul(ps_a[:, k, :], acc_s[:, k * P:(k + 1) * P], w_t[:, :], start=True, stop=True)
                last.then_inc(q["product"], 1)
                pe.wait_ge(q["normed"], c + 2)
                for k in range(CT):
                    last = nc.tensor.transpose(ps_u[:, k * P:(k + 1) * P], out[:, k, :], m.ident[:, :])
                last.then_inc(q["x2_turned"], 1)
                pe.wait_ge(q["x2_copied"], c + 1)
                nc.tensor.matmul(ps_ht[:, :], w2[:, :], xt[:, :], start=True, stop=True).then_inc(q["h_done"], 1)
                for k in range(CT):
                    nc.tensor.matmul(ps_h[:, k, :], xt[:, k * P:(k + 1) * P], w2[:, :], start=True, stop=True)
                pe.wait_ge(q["ht_copied"], c + 1)
                for k in range(CT):
                    last = nc.tensor.matmul(ps_att[:, k, :], ht[:, k * P:(k + 1) * P], att[:, :], start=True, stop=True)
                last.then_inc(q["att_done"], 1)

        @block.scalar
        def _(act):
            with act.Fori(0, NCH) as c:
                norm.scalar(act, c)
                act.wait_ge(q["h_done"], c + 1)
                nc.scalar.copy(ht[:, :], ps_ht[:, :]).then_inc(q["ht_copied"], 1)

        @block.vector
        def _(v):
            nc.vector.memset(att[:, :], 0.0).then_inc(q["att_zero"], 1)
            v.sem_inc(q["normed"], 1)
            v.wait_ge(q["w_turned"], 1)
            nc.vector.tensor_copy(w_t[:, :], ps_t[:, 0:D]).then_inc(q["w_copied"], 1)
            with v.Fori(0, NCH) as c:
                step = Chain(v, q["step"], c * PER, PER)
                v.wait_ge(q["tab_turned"], c + 1)
                step(nc.vector.tensor_tensor(acc_s[:, :], cols(m.acc, c * CH, CH), ps_t[:, :], ALU.add))
                v.sem_inc(q["acc_ready"], 1)
                v.wait_ge(q["product"], c + 1)
                for k in range(CT):
                    step(nc.vector.scalar_tensor_tensor(y[:, k, :], ps_a[:, k, :], cols(m.scale[:, 1, :], c * CT + k, 1), x[:, k, :], ALU.mult, ALU.add))
                step(nc.vector.tensor_tensor(y[:, :, :], y[:, :, :], bias[:, :].unsqueeze(1).to_broadcast([P, CT, D]), ALU.add))
                v.wait_ge(q["stored"], c * 32 + 32)
                norm.vector(v, step, c, y, out)
                v.sem_inc(q["normed"], 1)
                v.wait_ge(q["x2_turned"], c + 1)
                step(nc.vector.tensor_copy(xt[:, :], ps_u[:, :]))
                v.sem_inc(q["x2_copied"], 1)
                v.wait_ge(q["att_done"], c + 1)
                step(nc.vector.tensor_copy(tab[:, :, 0:D], ps_h[:, :, :]))
                step(nc.vector.tensor_copy(tab[:, :, D:ROW2], ps_att[:, :, 0:HEADS]))
                step(nc.vector.tensor_copy(m.att[:, bass.ds(c * CT, CT), :], ps_att[:, :, :]))
                v.sem_inc(q["table_ready"], 1)
                step.done()


def lowest_source(nc, z, m):
    with Phase(nc) as ctx:
        part = ctx.enter_context(nc.sbuf_tensor("low_part", [P, 1], F32))
        per_lane, over = ctx.semaphore("low_per_lane"), ctx.semaphore("low_over")
        block = ctx.enter_context(nc.Block())

        @block.vector
        def _(v):
            nc.vector.tensor_reduce(part[:, :], m.att[:, :, 0:HEADS], mybir.AxisListType.XY, ALU.min, negate=True).then_inc(per_lane, 1)
            v.wait_ge(over, 1)

        @block.gpsimd
        def _(pool):
            pool.wait_ge(per_lane, 1)
            nc.gpsimd.partition_all_reduce(m.low[:, :], part[:, :], P, bass.bass_isa.ReduceOp.max).then_inc(over, 1)


def highest_source(nc, z, m):
    GH = G * HEADS
    with Phase(nc) as ctx:
        name = "e2"
        sb = lambda n, shape, dt=F32: ctx.enter_context(nc.sbuf_tensor(f"{name}_{n}", shape, dt))
        rows_, hot, idx = sb("rows", [P, 2, G, ROW2]), sb("hot", [P, 2, G, P]), sb("idx", [P, 2, G], I32)
        a_e, a_t, run_t, run_e = sb("a_e", [P, 2, GH]), sb("a_t", [GH, 2, P]), sb("run_t", [GH, 2, P]), sb("run_e", [P, 2, GH])
        resets = sb("resets", [GH, 2, P])
        ps = ctx.enter_context(nc.psum_tensor(f"{name}_ps", [HEADS, GE], F32))
        ps_a = [ctx.enter_context(nc.psum_tensor(f"{name}_ps_a{i}", [GH, P], F32)) for i in range(2)]
        ps_r = [ctx.enter_context(nc.psum_tensor(f"{name}_ps_r{i}", [P, GH], F32)) for i in range(2)]
        names = ("idx_staged", "rows_in", "resets_in", "stashed", "a_ready", "a_turned", "a_copied", "run_ready",
                 "run_turned", "run_copied", "summed")
        q = {n: [ctx.semaphore(f"{name}_{n}{i}") for i in range(2)] for n in names}
        gather_begun, turning = (ctx.semaphore(f"{name}_{n}") for n in ("gather_begun", "turning"))
        windows = Windows(nc, ctx, m, z, name, [(m.acc, ps, HEADS, ALU.max)], apart=True)
        block = ctx.enter_context(nc.Block())

        @block.gpsimd
        def _(pool):
            def run(f):
                g = f(0)
                pool.wait_ge(q["idx_staged"][g.par], g.rnd + 1)
                pool.wait_ge(q["a_ready"][g.par], g.rnd + 1)
                pool.wait_ge(q["stashed"][g.par], g.rnd * 16 + 16)
                pool.sem_inc(gather_begun, 1)
                gather(nc, pool, m.table2, idx, rows_, g, q["rows_in"])

            pipeline(pool, z.groups, 0, run)

        @block.sync
        def _(sp):
            for par in range(2):
                sp.sem_inc(q["stashed"][par], 16)

            def run(f):
                if a := f(1):
                    sp.wait_ge(q["run_ready"][a.par], a.rnd + 1)
                    sp.dma_start(resets[:, a.par, :], m.resets4[bass.ds(a.no, 1), :].rearrange("o (r e) -> (o r) e", e=P)).then_inc(q["resets_in"][a.par], 16)
                if g := f(0):
                    sp.wait_ge(q["rows_in"][g.par], (g.rnd + 1) * (16 * G))
                    sp.dma_start(m.stash[bass.ds(g.no * P, P), :], rows_[:, g.par, :, :].rearrange("p k f -> p (k f)")).then_inc(q["stashed"][g.par], 16)

            pipeline(sp, z.groups, 1, run)
            for par in range(2):
                sp.wait_ge(q["stashed"][par], 16 * (z.groups // 2 + 1))

        @block.scalar
        def _(act):
            def run(f):
                if a := f(1):
                    act.wait_ge(q["a_ready"][a.par], a.rnd + 1)
                    nc.scalar.copy(idx[:, a.par, :], cols(m.src_idx, a.no * G, G)).then_inc(q["idx_staged"][a.par], 1)
                if g := f(0):
                    act.wait_ge(q["a_turned"][g.par], g.rnd + 1)
                    nc.scalar.copy(a_t[:, g.par, :], ps_a[g.par][:, :]).then_inc(q["a_copied"][g.par], 1)
                    act.wait_ge(q["run_turned"][g.par], g.rnd + 1)
                    nc.scalar.copy(run_e[:, g.par, :], ps_r[g.par][:, :]).then_inc(q["run_copied"][g.par], 1)

            pipeline(act, z.groups, 1, run)

        @block.tensor
        def _(pe):
            reg = pe.alloc_register(f"{name}_pe_base")
            for par in range(2):
                pe.sem_inc(q["summed"][par], 1)

            def run(f):
                a, g = f(1), f(0)
                if a:
                    pe.wait_ge(q["a_ready"][a.par], a.rnd + 2)
                    nc.tensor.transpose(ps_a[a.par][:, :], a_e[:, a.par, :], m.ident[:, :]).then_inc(q["a_turned"][a.par], 1)
                if g:
                    pe.wait_ge(q["run_copied"][g.par], g.rnd + 1)
                    windows.hot_ready(pe, g)
                    windows.free(pe, g)
                    windows.product(pe, g, reg, [(ps, lambda k: run_e[:, g.par, k * HEADS:(k + 1) * HEADS])], hot)
                    pe.drain().then_inc(q["summed"][g.par], 1)
                if a:
                    pe.wait_ge(q["run_ready"][a.par], a.rnd + 2)
                    pe.sem_inc(turning, 1)
                    nc.tensor.transpose(ps_r[a.par][:, :], run_t[:, a.par, :], m.ident[0:GH, 0:GH]).then_inc(q["run_turned"][a.par], 1)

            pipeline(pe, z.groups, 1, run)

        @block.vector
        def _(v):
            windows.registers(v)
            windows.clear()
            for par in range(2):
                v.sem_inc(q["a_ready"][par], 1)
                v.sem_inc(q["run_ready"][par], 1)

            def run(f):
                if a := f(1):
                    v.wait_ge(q["rows_in"][a.par], (a.rnd + 1) * (16 * G))
                    nc.vector.tensor_scalar(a_e[:, a.par, :].rearrange("p (k h) -> p k h", h=HEADS), rows_[:, a.par, :, D:ROW2],
                                            m.low[:, 0:1], None, ALU.add).then_inc(q["a_ready"][a.par], 1)
                    v.wait_ge(q["summed"][a.par], a.rnd + 1)
                    windows.one_hot(v, a, hot, m.last)
                    v.wait_ge(q["a_copied"][a.par], a.rnd + 1)
                    v.wait_ge(q["resets_in"][a.par], a.rnd * 16 + 16)
                    nc.vector.tensor_tensor_scan(run_t[:, a.par, :], resets[:, a.par, :], a_t[:, a.par, :], 0.0, ALU.add, ALU.max).then_inc(q["run_ready"][a.par], 1)
                if g := f(0):
                    v.wait_ge(q["summed"][g.par], g.rnd + 2)
                    windows.add(v, g)

            pipeline(v, z.groups, 1, run)
            windows.finish(v)


def attention_nodes(nc, z, m):
    NCH, NPT = z.chunks, z.node_tiles
    with Phase(nc) as ctx:
        ph = NodePhase(nc, ctx, "na")
        top_c, top = ph.sb("top_c", [HEADS, CH]), ph.sb("top", [P, NPT, HEADS])
        e_self, t, dn = ph.sb("e_self", [P, NPT, HEADS]), ph.sb("t", [P, NPT, HEADS]), ph.sb("dn", [P, NPT, 2 * HEADS])
        ps = ph.ps("ps", [P, CT, HEADS])
        q = {n: ph.sem(n) for n in ("taken", "turned", "copied", "begun", "step", "e_ready", "exped", "dn_ready", "stored")}
        block = ctx.enter_context(nc.Block())

        @block.scalar
        def _(act):
            with act.Fori(0, NCH) as c:
                act.wait_ge(q["turned"], c + 1)
                nc.scalar.copy(top_c[:, :], m.acc[0:HEADS, bass.ds(c * CH, CH)]).then_inc(q["taken"], 1)
            act.wait_ge(q["e_ready"], 1)
            nc.scalar.activation(m.p_self[:, :, :], e_self[:, :, :], ACT.Exp).then_inc(q["exped"], 1)

        @block.tensor
        def _(pe):
            pe.sem_inc(q["turned"], 1)
            with pe.Fori(0, NCH) as c:
                pe.wait_ge(q["taken"], c + 1)
                pe.wait_ge(q["copied"], c + 1)
                pe.sem_inc(q["begun"], 1)
                for k in range(CT):
                    last = nc.tensor.transpose(ps[:, k, :], top_c[:, k * P:(k + 1) * P], m.ident[0:HEADS, 0:HEADS])
                last.then_inc(q["turned"], 1)

        @block.vector
        def _(v):
            step = Chain(v, q["step"], 0)
            v.sem_inc(q["copied"], 1)
            with v.Fori(0, NCH) as c:
                v.wait_ge(q["turned"], c + 2)
                nc.vector.tensor_copy(top[:, bass.ds(c * CT, CT), :], ps[:, :, :]).then_inc(q["copied"], 1)
            v.wait_ge(q["copied"], NCH + 1)
            a_src, a_dst = m.att[:, :, 0:HEADS], m.att[:, :, HEADS:]
            step(nc.vector.tensor_scalar(top[:, :, :], top[:, :, :], m.low[:, 0:1], None, ALU.subtract))
            step(nc.vector.tensor_tensor(top[:, :, :], top[:, :, :], a_src, ALU.max))
            step(nc.vector.tensor_tensor(top[:, :, :], top[:, :, :], a_dst, ALU.add))
            step(nc.vector.tensor_scalar(t[:, :, :], top[:, :, :], 0.2, None, ALU.mult))
            step(nc.vector.tensor_tensor(dn[:, :, HEADS:], top[:, :, :], t[:, :, :], ALU.max))
            step(nc.vector.tensor_copy(dn[:, :, 0:HEADS], a_dst))
            v.sem_inc(q["dn_ready"], 1)
            step(nc.vector.tensor_tensor(e_self[:, :, :], a_src, a_dst, ALU.add))
            step(nc.vector.tensor_scalar(t[:, :, :], e_self[:, :, :], 0.2, None, ALU.mult))
            step(nc.vector.tensor_tensor(e_self[:, :, :], e_self[:, :, :], t[:, :, :], ALU.max))
            step(nc.vector.tensor_tensor(e_self[:, :, :], e_self[:, :, :], dn[:, :, HEADS:], ALU.subtract))
            v.sem_inc(q["e_ready"], 1)
            v.wait_ge(q["exped"], 1)

        @block.sync
        def _(sp):
            sp.wait_ge(q["dn_ready"], 1)
            sp.dma_start(m.dst_terms[:, :].rearrange("(k p) f -> p k f", p=P), dn[:, :, :], allow_slow_non_contiguous=True).then_inc(q["stored"], 16)
            sp.wait_ge(q["stored"], 16)


def weighted_sum(nc, z, m):
    with Phase(nc) as ctx:
        name = "e3"
        sb = lambda n, shape, dt=F32: ctx.enter_context(nc.sbuf_tensor(f"{name}_{n}", shape, dt))
        rows_, hot, idx = sb("rows", [P, 2, G, ROW2]), sb("hot", [P, 2, G, P]), sb("idx", [P, 2, G], I32)
        terms, e, e2, prob, msg = (sb("terms", [P, 2, G, 2 * HEADS]), sb("e", [P, 2, G, HEADS]), sb("e2", [P, 2, G, HEADS]),
                                   sb("prob", [P, 2, G, HEADS]), sb("msg", [P, 2, G, D]))
        ps = ctx.enter_context(nc.psum_tensor(f"{name}_ps", [P, GE], F32))
        ps_p = ctx.enter_context(nc.psum_tensor(f"{name}_ps_p", [HEADS, GE], F32))
        names = ("idx_staged", "rows_in", "terms_in", "e_ready", "prob_ready", "msg_ready", "summed")
        q = {n: [ctx.semaphore(f"{name}_{n}{i}") for i in range(2)] for n in names}
        gather_begun, small = (ctx.semaphore(f"{name}_{n}") for n in ("gather_begun", "small"))
        windows = Windows(nc, ctx, m, z, name, [(m.acc, ps, P, ALU.add), (m.side, ps_p, HEADS, ALU.add)])
        block = ctx.enter_context(nc.Block())

        @block.gpsimd
        def _(pool):
            def run(f):
                g = f(0)
                pool.wait_ge(q["idx_staged"][g.par], g.rnd + 1)
                pool.wait_ge(q["e_ready"][g.par], g.rnd + 1)
                pool.sem_inc(gather_begun, 1)
                gather(nc, pool, m.dst_terms, idx, terms, g, q["terms_in"])

            pipeline(pool, z.groups, 0, run)

        @block.sync
        def _(sp):
            def run(f):
                g = f(0)
                sp.wait_ge(q["msg_ready"][g.par], g.rnd + 1)
                sp.dma_start(rows_[:, g.par, :, :].rearrange("p k f -> p (k f)"), m.stash[bass.ds(g.no * P, P), :]).then_inc(q["rows_in"][g.par], 16)

            pipeline(sp, z.groups, 0, run)

        @block.scalar
        def _(act):
            def run(f):
                if a := f(1):
                    act.wait_ge(q["e_ready"][a.par], a.rnd + 1)
                    nc.scalar.copy(idx[:, a.par, :], cols(m.dst_idx, a.no * G, G)).then_inc(q["idx_staged"][a.par], 1)
                if g := f(0):
                    act.wait_ge(q["e_ready"][g.par], g.rnd + 2)
                    nc.scalar.activation(prob[:, g.par, :, :], e[:, g.par, :, :], ACT.Exp).then_inc(q["prob_ready"][g.par], 1)

            pipeline(act, z.groups, 1, run)

        @block.tensor
        def _(pe):
            reg = pe.alloc_register(f"{name}_pe_base")
            for par in range(2):
                pe.sem_inc(q["summed"][par], 1)

            def run(f):
                g = f(0)
                pe.wait_ge(q["msg_ready"][g.par], g.rnd + 2)
                windows.free(pe, g)
                windows.product(pe, g, reg, [(ps, lambda k: msg[:, g.par, k, :]), (ps_p, lambda k: prob[:, g.par, k, :])], hot)
                pe.drain().then_inc(q["summed"][g.par], 1)

            pipeline(pe, z.groups, 0, run)

        @block.vector
        def _(v):
            windows.registers(v)
            windows.clear()
            for par in range(2):
                v.sem_inc(q["e_ready"][par], 1)
                v.sem_inc(q["msg_ready"][par], 1)

            def messages(a):
                par = a.par
                step = Chain(v, small, a.no * 3, 3)
                v.wait_ge(q["summed"][par], a.rnd + 1)
                windows.one_hot(v, a, hot, m.loc)
                v.wait_ge(q["rows_in"][par], a.rnd * 16 + 16)
                v.wait_ge(q["terms_in"][par], (a.rnd + 1) * (16 * G))
                step(nc.vector.tensor_tensor(e2[:, par, :, :], rows_[:, par, :, D:ROW2], terms[:, par, :, 0:HEADS], ALU.add))
                step(nc.vector.tensor_scalar(e[:, par, :, :], e2[:, par, :, :], 0.2, None, ALU.mult))
                step(nc.vector.tensor_tensor(e2[:, par, :, :], e[:, par, :, :], e2[:, par, :, :], ALU.max))
                nc.vector.tensor_tensor(e[:, par, :, :], e2[:, par, :, :], terms[:, par, :, HEADS:], ALU.subtract).then_inc(q["e_ready"][par], 1)
                step.done()

            def weigh(a):
                par = a.par
                v.wait_ge(q["prob_ready"][par], a.rnd + 1)
                nc.vector.tensor_tensor(msg[:, par, :, :].rearrange("p k (h c) -> p k h c", h=HEADS), rows_[:, par, :, 0:D].rearrange("p k (h c) -> p k h c", h=HEADS),
                                        prob[:, par, :, :].unsqueeze(3).to_broadcast([P, G, HEADS, HD]), ALU.mult).then_inc(q["msg_ready"][par], 1)

            def run(f):
                a, g = f(1), f(0)
                if a:
                    messages(a)
                if g:
                    v.wait_ge(q["summed"][g.par], g.rnd + 2)
                    windows.add(v, g)
                if a:
                    weigh(a)

            pipeline(v, z.groups, 1, run)
            windows.finish(v)


def layer2_nodes(nc, z, m, ins):
    NCH = z.chunks
    with Phase(nc) as ctx:
        ph = NodePhase(nc, ctx, "n2")
        bias, lin1, conv1, sa, w_sa, b0 = (ph.sb("bias", [P, D]), ph.sb("lin1", [D, D]), ph.sb("conv1", [D, D]),
                                           ph.sb("sa", [2, 1]), ph.sb("w_sa", [2, D]), ph.sb("b0", [D, 1]))
        b_lin = ph.sb("b_lin", [D, 1])
        x, tab_in, acc_c, s_c = ph.sb("x", [P, CT, D]), ph.sb("tab_in", [P, CT, ROW2]), ph.sb("acc_c", [D, CH]), ph.sb("s_c", [HEADS, CH])
        den, y, out, xt, ht, tab = (ph.sb("den", [P, CT, HEADS]), ph.sb("y", [P, CT, D]), ph.sb("out", [P, CT, D]),
                                    ph.sb("xt", [D, CH]), ph.sb("ht", [D, CH]), ph.sb("tab", [P, CT, D]))
        ps_n, ps_s, ps_t, ps_h, ps_x, ps_b = (ph.ps("ps_n", [P, CT, D]), ph.ps("ps_s", [P, CT, HEADS]), ph.ps("ps_t", [D, CH]),
                                              ph.ps("ps_h", [D, CH]), ph.ps("ps_x", [P, CT, D]), ph.ps("ps_b", [D, 1]))
        norm = Norm(nc, ph)
        names = ("w_in", "b_done", "b_ready", "rows_in", "stored", "taken", "turned", "normed", "x3_turned", "x3_copied",
                 "h_done", "h_copied", "xm_done", "table_ready", "step")
        q = {n: ph.sem(n) for n in names}
        block = ctx.enter_context(nc.Block())
        PER = 8 + LN_STEPS + 2
        heads = lambda a: a.rearrange("p k (h c) -> p k h c", h=HEADS)

        @block.sync
        def _(sp):
            sp.sem_inc(q["stored"], 32)
            for dst, src in ((bias[:, :], ins["L2_gnn_bias"].partition_broadcast(P)), (lin1[:, :], ins["L3_gnn_lin1_w"][0, 2:2 + D, :]),
                             (w_sa[:, :], ins["L3_gnn_lin1_w"][0, 0:2, :]), (conv1[:, :], ins["L3_gnn_conv1_w"][0]),
                             (sa[:, :], ins["L3_gnn_state_attr"][0:1, :].rearrange("o s -> s o")),
                             (b_lin[:, :], ins["L3_gnn_lin1_b"][0:1, :].rearrange("o d -> d o"))):
                sp.dma_start(dst, src, allow_slow_non_contiguous=True).then_inc(q["w_in"], 16)
            with sp.Fori(0, NCH) as c:
                sp.wait_ge(q["normed"], c + 1)
                sp.dma_start(x[:, :, :], rows(m.x2, c)).then_inc(q["rows_in"], 16)
                sp.dma_start(tab_in[:, :, :], rows(m.table2, c, ROW2)).then_inc(q["rows_in"], 16)
                sp.wait_ge(q["table_ready"], c + 1)
                sp.dma_start(rows(m.x3, c), out[:, :, :]).then_inc(q["stored"], 16)
                sp.dma_start(rows(m.table3, c), tab[:, :, :]).then_inc(q["stored"], 16)
            sp.wait_ge(q["stored"], 32 * (NCH + 1))

        @block.tensor
        def _(pe):
            pe.sem_inc(q["turned"], 1)
            pe.wait_ge(q["w_in"], 16 * 6)
            nc.tensor.matmul(ps_b[:, :], w_sa[:, :], sa[:, :], start=True, stop=True).then_inc(q["b_done"], 1)
            with pe.Fori(0, NCH) as c:
                pe.wait_ge(q["taken"], c + 1)
                for k in range(CT):
                    at = slice(k * P, (k + 1) * P)
                    nc.tensor.transpose(ps_n[:, k, :], acc_c[:, at], m.ident[:, :])
                    last = nc.tensor.transpose(ps_s[:, k, :], s_c[:, at], m.ident[0:HEADS, 0:HEADS])
                last.then_inc(q["turned"], 1)
                pe.wait_ge(q["normed"], c + 2)
                for k in range(CT):
                    last = nc.tensor.transpose(ps_t[:, k * P:(k + 1) * P], out[:, k, :], m.ident[:, :])
                last.then_inc(q["x3_turned"], 1)
                pe.wait_ge(q["x3_copied"], c + 1)
                nc.tensor.matmul(ps_h[:, :], lin1[:, :], xt[:, :], start=True, stop=True).then_inc(q["h_done"], 1)
                pe.wait_ge(q["h_copied"], c + 1)
                for k in range(CT):
                    last = nc.tensor.matmul(ps_x[:, k, :], ht[:, k * P:(k + 1) * P], conv1[:, :], start=True, stop=True)
                last.then_inc(q["xm_done"], 1)

        @block.scalar
        def _(act):
            act.wait_ge(q["b_ready"], 1)
            with act.Fori(0, NCH) as c:
                act.wait_ge(q["turned"], c + 1)
                nc.scalar.copy(acc_c[:, :], cols(m.acc, c * CH, CH))
                nc.scalar.copy(s_c[:, :], m.side[0:HEADS, bass.ds(c * CH, CH)]).then_inc(q["taken"], 1)
                norm.scalar(act, c)
                act.wait_ge(q["h_done"], c + 1)
                nc.scalar.activation(ht[:, :], ps_h[:, :], ACT.Identity, bias=b0[:, 0:1]).then_inc(q["h_copied"], 1)
                nc.scalar.activation(cols(m.hidden, c * CH, CH), ps_h[:, :], ACT.Identity, bias=b0[:, 0:1])

        @block.vector
        def _(v):
            v.sem_inc(q["normed"], 1)
            v.wait_ge(q["b_done"], 1)
            nc.vector.tensor_tensor(b0[:, :], ps_b[:, :], b_lin[:, :], ALU.add).then_inc(q["b_ready"], 1)
            with v.Fori(0, NCH) as c:
                step = Chain(v, q["step"], c * PER, PER)
                p_self = m.p_self[:, bass.ds(c * CT, CT), :]
                v.wait_ge(q["rows_in"], c * 32 + 32)
                v.wait_ge(q["turned"], c + 2)
                step(nc.vector.tensor_tensor(den[:, :, :], ps_s[:, :, :], p_self, ALU.add))
                step(nc.vector.tensor_scalar(den[:, :, :], den[:, :, :], 1e-16, None, ALU.add))
                step(nc.vector.reciprocal(den[:, :, :], den[:, :, :]))
                step(nc.vector.tensor_tensor(heads(y[:, :, :]), heads(tab_in[:, :, 0:D]), p_self.unsqueeze(3).to_broadcast([P, CT, HEADS, HD]), ALU.mult))
                step(nc.vector.tensor_tensor(y[:, :, :], y[:, :, :], ps_n[:, :, :], ALU.add))
                step(nc.vector.tensor_tensor(heads(y[:, :, :]), heads(y[:, :, :]), den[:, :, :].unsqueeze(3).to_broadcast([P, CT, HEADS, HD]), ALU.mult))
                step(nc.vector.tensor_tensor(y[:, :, :], y[:, :, :], bias[:, :].unsqueeze(1).to_broadcast([P, CT, D]), ALU.add))
                step(nc.vector.tensor_tensor(y[:, :, :], y[:, :, :], x[:, :, :], ALU.add))
                v.wait_ge(q["stored"], c * 32 + 32)
                norm.vector(v, step, c, y, out)
                v.sem_inc(q["normed"], 1)
                v.wait_ge(q["x3_turned"], c + 1)
                step(nc.vector.tensor_copy(xt[:, :], ps_t[:, :]))
                v.sem_inc(q["x3_copied"], 1)
                v.wait_ge(q["xm_done"], c + 1)
                step(nc.vector.tensor_copy(tab[:, :, :], ps_x[:, :, :]))
                v.sem_inc(q["table_ready"], 1)
                step.done()


def cutoffs(nc, z, m):
    NT = z.tiles
    with Phase(nc) as ctx:
        u, k = (ctx.enter_context(nc.sbuf_tensor(n, [P, NT], F32)) for n in ("cut_u", "cut_k"))
        half_pi = ctx.enter_context(nc.sbuf_tensor("half_pi", [P, 1], F32))
        step_s, r_ready, absed, sined = (ctx.semaphore(n) for n in ("cut_step", "cut_r", "cut_abs", "cut_sin"))
        block = ctx.enter_context(nc.Block())
        ROUND = 12582912.0
        two_pi_hi = float(np.float32(6.28125))
        two_pi_lo = float(2 * np.pi - 6.28125)

        @block.vector
        def _(v):
            step = Chain(v, step_s, 0)
            step(nc.vector.memset(half_pi[:, :], PI / 2))
            step(nc.vector.tensor_scalar(u[:, :], m.w[:, :], float(np.float32(PI / 10.0)), None, ALU.mult))
            step(nc.vector.tensor_scalar(k[:, :], u[:, :], 1.0 / (2 * PI), ROUND, ALU.mult, ALU.add))
            step(nc.vector.tensor_scalar(k[:, :], k[:, :], -ROUND, None, ALU.add))
            step(nc.vector.scalar_tensor_tensor(u[:, :], k[:, :], -two_pi_hi, u[:, :], ALU.mult, ALU.add))
            step(nc.vector.scalar_tensor_tensor(u[:, :], k[:, :], -two_pi_lo, u[:, :], ALU.mult, ALU.add))
            v.sem_inc(r_ready, 1)
            v.wait_ge(absed, 1)
            step(nc.vector.tensor_scalar(k[:, :], k[:, :], PI, None, ALU.min))
            v.sem_inc(r_ready, 1)
            v.wait_ge(sined, 1)
            step(nc.vector.tensor_scalar(m.w[:, :], u[:, :], 1.0, 0.5, ALU.add, ALU.mult))

        @block.scalar
        def _(act):
            act.wait_ge(r_ready, 1)
            nc.scalar.activation(k[:, :], u[:, :], ACT.Abs).then_inc(absed, 1)
            act.wait_ge(r_ready, 2)
            nc.scalar.activation(u[:, :], k[:, :], ACT.Sin, bias=half_pi[:, 0:1], scale=-1.0).then_inc(sined, 1)


LOG_SET = "natural_log_exp_and_others"


class Ssp:

    def __init__(self, nc, ph):
        self.nc = nc
        self.pos, self.neg, self.log = ph.sb("ssp_pos", [P, 2, CH]), ph.sb("ssp_neg", [P, 2, CH]), ph.sb("ssp_log", [P, 2, CH])
        self.chain = ph.sem("ssp_chain")

    def vector(self, out, par):
        return self.nc.vector.scalar_tensor_tensor(out, self.pos[:, par, :], -LN2, self.log[:, par, :], ALU.add, ALU.add)


def continuous_conv(nc, z, m, ins, layer):
    NG, K = z.groups, z.gauss
    name = f"c{layer}"
    with Phase(nc) as ctx:
        ph = NodePhase(nc, ctx, name)
        w1, w2, b1, b2 = ph.sb("w1", [K, D]), ph.sb("w2", [D, D]), ph.sb("b1", [D, 1]), ph.sb("b2", [P, D])
        rows_, hot, idx = ph.sb("rows", [P, 2, G, D]), ph.sb("hot", [P, 2, G, P]), ph.sb("idx", [P, 2, G], I32)
        attr, attr_t = ph.sb("attr", [P, 2, G, K]), ph.sb("attr_t", [K, GE])
        act_t, filt, msg = ph.sb("act_t", [D, 2, GE]), ph.sb("filt", [P, 2, CT, D]), ph.sb("msg", [P, 2, G, D])
        ssp = Ssp(nc, ph)
        ps_t = [ph.ps(f"ps_t{i}", [K, CH]) for i in range(2)]
        ps_1 = [ph.ps(f"ps_1{i}", [D, CH]) for i in range(2)]
        ps_2 = [ph.ps(f"ps_2{i}", [P, CT, D]) for i in range(2)]
        ps = ph.ps("ps", [P, GE])
        pair = {n: [ph.sem(f"{n}{i}") for i in range(2)] for n in (
            "idx_staged", "rows_in", "attr_in", "attr_read", "msg_ready", "summed")}
        half = {n: [ph.sem(f"{n}{i}") for i in range(2)] for n in (
            "turned", "turned_copied", "first_done", "first_read", "exp_done", "ssp_ready", "ssp_used", "filter_done", "filter_read", "msg_half")}
        one = {n: ph.sem(n) for n in ("w_in", "gather_begun", "turning", "attr_part")}
        windows = Windows(nc, ctx, m, z, name, [(m.acc, ps, P, ALU.add)])
        block = ctx.enter_context(nc.Block())

        def last_attr_dmas(g):
            left = max(0, min(GE, z.edges - g * GE))
            full, rest = left // G, left % G
            return ([(0, full, G)] if full else []) + ([(full, 1, rest)] if rest else [])

        @block.sync
        def _(sp):
            for dst, src in ((w1[:, :], ins["L3_gnn_mlp1_w"][layer]), (w2[:, :], ins["L3_gnn_mlp2_w"][layer]),
                             (b1[:, :], ins["L3_gnn_mlp1_b"][layer:layer + 1, :].rearrange("o d -> d o")),
                             (b2[:, :], ins["L3_gnn_mlp2_b"][layer].partition_broadcast(P))):
                sp.dma_start(dst, src, allow_slow_non_contiguous=True).then_inc(one["w_in"], 16)
            flat = lambda a: a.rearrange("p j f -> p (j f)")

            def load(f):
                g = f(0)
                sp.wait_ge(pair["attr_read"][g.par], g.rnd + 1)
                sp.dma_start(flat(attr[:, g.par, :, :]),
                             ins["edge_attr_50"][bass.ds(g.no * GE, GE), :].rearrange("(p j) f -> p (j f)", j=G)).then_inc(pair["attr_in"][g.par], 16)

            whole = (NG - 2) // 2 * 2
            pipeline(sp, whole, 0, load)
            attr_parts = 0
            for g in range(whole, NG):
                par = g % 2
                sp.wait_ge(pair["attr_read"][par], g // 2 + 1)
                parts = last_attr_dmas(g)
                for i, (p0, n, j) in enumerate(parts):
                    at = g * GE + p0 * G
                    load_part = sp.dma_start(flat(attr[p0:p0 + n, par, 0:j, :]),
                                             ins["edge_attr_50"][at:at + n * j, :].rearrange("(p j) f -> p (j f)", j=j))
                    if i < len(parts) - 1:
                        load_part.then_inc(one["attr_part"], 16)
                        attr_parts += 1
                        sp.wait_ge(one["attr_part"], 16 * attr_parts)
                    else:
                        load_part.then_inc(pair["attr_in"][par], 16)
                if not parts:
                    sp.sem_inc(pair["attr_in"][par], 16)

        @block.gpsimd
        def _(pool):
            def run(f):
                g = f(0)
                pool.wait_ge(pair["idx_staged"][g.par], g.rnd + 1)
                pool.wait_ge(pair["msg_ready"][g.par], g.rnd + 1)
                pool.sem_inc(one["gather_begun"], 1)
                gather(nc, pool, m.table3, idx, rows_, g, pair["rows_in"])

            pipeline(pool, NG, 0, run)

        @block.tensor
        def _(pe):
            reg = pe.alloc_register(f"{name}_pe_base")
            for par in range(2):
                pe.sem_inc(pair["attr_read"][par], 1)
                pe.sem_inc(pair["summed"][par], 1)
            pe.wait_ge(one["w_in"], 64)

            def run(f):
                if u := f(2):
                    for h in range(2):
                        pe.wait_ge(half["turned_copied"][0], u.no + 2)
                        pe.wait_ge(half["turned_copied"][1], u.no + 2)
                        pe.wait_ge(half["first_read"][h], u.no + 1)
                        nc.tensor.matmul(ps_1[h][:, :], w1[:, :], attr_t[:, h * CH:(h + 1) * CH], start=True, stop=True).then_inc(half["first_done"][h], 1)
                if a := f(1):
                    for h in range(2):
                        pe.wait_ge(half["ssp_used"][h], a.no + 2)
                        pe.wait_ge(half["filter_read"][h], a.no + 1)
                        for k in range(CT):
                            at = h * CH + k * P
                            last = nc.tensor.matmul(ps_2[h][:, k, :], act_t[:, a.par, at:at + P], w2[:, :], start=True, stop=True)
                        last.then_inc(half["filter_done"][h], 1)
                if t := f(3):
                    pe.wait_ge(pair["attr_in"][t.par], t.rnd * 16 + 16)
                    for h in range(2):
                        pe.wait_ge(half["turned_copied"][h], t.no + 1)
                        pe.sem_inc(one["turning"], 1)
                        for j in range(CT):
                            last = nc.tensor.transpose(ps_t[h][:, j * P:(j + 1) * P], attr[:, t.par, h * CT + j, :], m.ident[:, :])
                        last.then_inc(half["turned"][h], 1)
                    pe.wait_ge(half["turned"][1], t.no + 1)
                    pe.sem_inc(pair["attr_read"][t.par], 1)
                if g := f(0):
                    pe.wait_ge(pair["msg_ready"][g.par], g.rnd + 2)
                    windows.free(pe, g)
                    windows.product(pe, g, reg, [(ps, lambda k: msg[:, g.par, k, :])], hot)
                    pe.drain().then_inc(pair["summed"][g.par], 1)

            pipeline(pe, NG, 3, run)

        @block.scalar
        def _(act):
            act.preload_act_table_set(LOG_SET)
            for h in range(2):
                act.sem_inc(half["turned_copied"][h], 1)
                act.sem_inc(half["first_read"][h], 1)
            act.wait_ge(one["w_in"], 64)

            def run(f):
                if u := f(2):
                    act.wait_ge(pair["msg_ready"][u.par], u.rnd + 1)
                    nc.scalar.copy(idx[:, u.par, :], cols(m.src_idx, u.no * G, G)).then_inc(pair["idx_staged"][u.par], 1)
                    for h in range(2):
                        act.wait_ge(half["first_done"][h], u.no + 1)
                        act.wait_ge(half["ssp_used"][h], u.no + 1)
                        nc.scalar.activation(ssp.pos[:, h, :], ps_1[h][:, :], ACT.Relu, bias=b1[:, 0:1])
                        nc.scalar.activation(ssp.neg[:, h, :], ps_1[h][:, :], ACT.Abs, bias=b1[:, 0:1]).then_inc(half["first_read"][h], 1)
                    for h in range(2):
                        act.wait_ge(half["first_read"][h], u.no + 2)
                        nc.scalar.activation(ssp.log[:, h, :], ssp.neg[:, h, :], ACT.Exp, scale=-1.0).then_inc(half["exp_done"][h], 1)
                    for h in range(2):
                        act.wait_ge(half["exp_done"][h], u.no + 1)
                        nc.scalar.activation(ssp.log[:, h, :], ssp.log[:, h, :], ACT.Ln, bias=1.0).then_inc(half["ssp_ready"][h], 1)
                if t := f(3):
                    for h in range(2):
                        act.wait_ge(half["turned"][h], t.no + 1)
                        out = attr_t[:, :].rearrange("f (p j) -> f j p", j=G)[:, h * CT:(h + 1) * CT, :]
                        nc.scalar.copy(out, ps_t[h][:, :].rearrange("f (j p) -> f j p", j=CT)).then_inc(half["turned_copied"][h], 1)

            pipeline(act, NG, 3, run)

        @block.vector
        def _(v):
            windows.registers(v)
            windows.clear()
            for h in range(2):
                v.sem_inc(half["filter_read"][h], 1)
                v.sem_inc(half["ssp_used"][h], 1)
                v.sem_inc(half["msg_half"][h], 1)
                v.sem_inc(pair["msg_ready"][h], 1)
            v.wait_ge(one["w_in"], 64)

            def run(f):
                if a := f(1):
                    v.wait_ge(pair["summed"][a.par], a.rnd + 1)
                    windows.one_hot(v, a, hot, m.loc, m.w)
                    v.wait_ge(pair["rows_in"][a.par], (a.rnd + 1) * (16 * G))
                    for h in range(2):
                        v.wait_ge(half["filter_done"][h], a.no + 1)
                        v.wait_ge(half["msg_half"][h], a.no + 1)
                        nc.vector.tensor_tensor(filt[:, h, :, :], ps_2[h][:, :, :], b2[:, :].unsqueeze(1).to_broadcast([P, CT, D]), ALU.add).then_inc(half["filter_read"][h], 1)
                    for h in range(2):
                        v.wait_ge(half["filter_read"][h], a.no + 2)
                        nc.vector.tensor_tensor(msg[:, a.par, h * CT:(h + 1) * CT, :], filt[:, h, :, :], rows_[:, a.par, h * CT:(h + 1) * CT, :], ALU.mult).then_inc(half["msg_half"][h], 1)
                    for h in range(2):
                        v.wait_ge(half["msg_half"][h], a.no + 2)
                    v.sem_inc(pair["msg_ready"][a.par], 1)
                if u := f(2):
                    for h in range(2):
                        v.wait_ge(half["ssp_ready"][h], u.no + 1)
                        ssp.vector(act_t[:, u.par, h * CH:(h + 1) * CH], h).then_inc(half["ssp_used"][h], 1)
                if g := f(0):
                    v.wait_ge(pair["summed"][g.par], g.rnd + 2)
                    windows.add(v, g)

            pipeline(v, NG, 3, run)
            windows.finish(v)


def conv_nodes(nc, z, m, ins, layer):
    NCH = z.chunks
    real = z.nodes - (NCH - 1) * CH
    with Phase(nc) as ctx:
        ph = NodePhase(nc, ctx, f"u{layer}")
        conv2, blin, b2, bb = ph.sb("conv2", [D, D]), ph.sb("blin", [D, D]), ph.sb("b2", [D, 1]), ph.sb("bb", [D, 1])
        act_c = ph.sb("act_c", [D, CH])
        ssp = Ssp(nc, ph)
        ps_1, ps_2 = ph.ps("ps_1", [D, CH]), ph.ps("ps_2", [D, CH])
        q = {n: ph.sem(n) for n in ("w_in", "first_done", "first_read", "ssp_ready", "act_ready", "second_done", "updated", "summed")}
        block = ctx.enter_context(nc.Block())

        @block.sync
        def _(sp):
            for dst, src in ((conv2[:, :], ins["L3_gnn_conv2_w"][layer]), (blin[:, :], ins["L3_gnn_blin_w"][layer]),
                             (b2[:, :], ins["L3_gnn_conv2_b"][layer:layer + 1, :].rearrange("o d -> d o")),
                             (bb[:, :], ins["L3_gnn_blin_b"][layer:layer + 1, :].rearrange("o d -> d o"))):
                sp.dma_start(dst, src, allow_slow_non_contiguous=True).then_inc(q["w_in"], 16)

        @block.tensor
        def _(pe):
            pe.wait_ge(q["w_in"], 64)
            with pe.Fori(0, NCH) as c:
                pe.wait_ge(q["first_read"], c + 1)
                nc.tensor.matmul(ps_1[:, :], conv2[:, :], cols(m.acc, c * CH, CH), start=True, stop=True).then_inc(q["first_done"], 1)
                pe.wait_ge(q["act_ready"], c + 1)
                pe.wait_ge(q["updated"], c + 1)
                nc.tensor.matmul(ps_2[:, :], blin[:, :], act_c[:, :], start=True, stop=True).then_inc(q["second_done"], 1)

        @block.scalar
        def _(act):
            act.preload_act_table_set(LOG_SET)
            act.wait_ge(q["w_in"], 64)
            act.sem_inc(q["first_read"], 1)
            with act.Fori(0, NCH) as c:
                act.wait_ge(q["first_done"], c + 1)
                act.wait_ge(q["updated"], c + 1)
                nc.scalar.activation(ssp.pos[:, 0, :], ps_1[:, :], ACT.Relu, bias=b2[:, 0:1])
                nc.scalar.activation(ssp.neg[:, 0, :], ps_1[:, :], ACT.Abs, bias=b2[:, 0:1]).then_inc(q["first_read"], 1)
                act.wait_ge(q["first_read"], c + 2)
                nc.scalar.activation(ssp.log[:, 0, :], ssp.neg[:, 0, :], ACT.Exp, scale=-1.0).then_inc(ssp.chain, 1)
                act.wait_ge(ssp.chain, c + 1)
                nc.scalar.activation(ssp.log[:, 0, :], ssp.log[:, 0, :], ACT.Ln, bias=1.0).then_inc(q["ssp_ready"], 1)

        @block.vector
        def _(v):
            v.sem_inc(q["updated"], 1)
            v.wait_ge(q["w_in"], 64)

            def update(c, n):
                v.wait_ge(q["ssp_ready"], c + 1)
                ssp.vector(act_c[:, :], 0).then_inc(q["act_ready"], 1)
                v.wait_ge(q["second_done"], c + 1)
                h = cols(m.hidden, c * CH, CH)
                nc.vector.scalar_tensor_tensor(h, ps_2[:, :], bb[:, 0:1], h, ALU.add, ALU.add).then_inc(q["updated"], 1)
                v.wait_ge(q["updated"], c + 2)
                nc.vector.tensor_reduce(cols(m.sums, c, 1), m.hidden[:, bass.ds(c * CH, n)], AX, ALU.add).then_inc(q["summed"], 1)

            if NCH > 1:
                with v.Fori(0, NCH - 1) as c:
                    update(c, CH)
            update(NCH - 1, real)
            v.wait_ge(q["summed"], NCH)


def next_messages(nc, z, m, ins):
    NCH = z.chunks
    with Phase(nc) as ctx:
        ph = NodePhase(nc, ctx, "nm")
        lin1, conv1, w_a, w_b, b_lin, b1 = (ph.sb("lin1", [D, D]), ph.sb("conv1", [D, D]), ph.sb("w_a", [D, 1]),
                                            ph.sb("w_b", [D, 1]), ph.sb("b_lin", [D, 1]), ph.sb("b1", [D, 1]))
        part, total, ht, tab = ph.sb("part", [P, 1]), ph.sb("total", [P, 1]), ph.sb("ht", [D, CH]), ph.sb("tab", [P, CT, D])
        ps_h, ps_x = ph.ps("ps_h", [D, CH]), ph.ps("ps_x", [P, CT, D])
        q = {n: ph.sem(n) for n in ("w_in", "part_ready", "totalled", "step", "b_ready", "h_done", "h_copied", "h_kept", "xm_done", "table_ready", "stored")}
        block = ctx.enter_context(nc.Block())

        @block.sync
        def _(sp):
            sp.sem_inc(q["stored"], 16)
            w = ins["L3_gnn_lin1_w"]
            for dst, src in ((lin1[:, :], w[1, 2:2 + D, :]), (conv1[:, :], ins["L3_gnn_conv1_w"][1]),
                             (w_a[:, :], w[1, 0:1, :].rearrange("o d -> d o")), (w_b[:, :], w[1, 1:2, :].rearrange("o d -> d o")),
                             (b_lin[:, :], ins["L3_gnn_lin1_b"][1:2, :].rearrange("o d -> d o"))):
                sp.dma_start(dst, src, allow_slow_non_contiguous=True).then_inc(q["w_in"], 16)
            with sp.Fori(0, NCH) as c:
                sp.wait_ge(q["table_ready"], c + 2)
                sp.dma_start(rows(m.table3, c), tab[:, :, :]).then_inc(q["stored"], 16)
            sp.wait_ge(q["stored"], 16 * (NCH + 1))

        @block.gpsimd
        def _(pool):
            pool.wait_ge(q["part_ready"], 1)
            nc.gpsimd.partition_all_reduce(total[:, :], part[:, :], P, bass.bass_isa.ReduceOp.add).then_inc(q["totalled"], 1)

        @block.tensor
        def _(pe):
            pe.wait_ge(q["w_in"], 80)
            with pe.Fori(0, NCH) as c:
                pe.wait_ge(q["h_kept"], c + 1)
                nc.tensor.matmul(ps_h[:, :], lin1[:, :], cols(m.hidden, c * CH, CH), start=True, stop=True).then_inc(q["h_done"], 1)
                pe.wait_ge(q["h_copied"], c + 1)
                pe.wait_ge(q["table_ready"], c + 1)
                for k in range(CT):
                    last = nc.tensor.matmul(ps_x[:, k, :], ht[:, k * P:(k + 1) * P], conv1[:, :], start=True, stop=True)
                last.then_inc(q["xm_done"], 1)

        @block.scalar
        def _(act):
            act.sem_inc(q["h_kept"], 1)
            act.wait_ge(q["b_ready"], 1)
            with act.Fori(0, NCH) as c:
                act.wait_ge(q["h_done"], c + 1)
                act.wait_ge(q["xm_done"], c + 1)
                nc.scalar.activation(ht[:, :], ps_h[:, :], ACT.Identity, bias=b1[:, 0:1]).then_inc(q["h_copied"], 1)
                nc.scalar.activation(cols(m.hidden, c * CH, CH), ps_h[:, :], ACT.Identity, bias=b1[:, 0:1]).then_inc(q["h_kept"], 1)

        @block.vector
        def _(v):
            step = Chain(v, q["step"], 0)
            v.sem_inc(q["xm_done"], 1)
            v.sem_inc(q["table_ready"], 1)
            nc.vector.tensor_reduce(part[:, :], m.sums[:, 0:NCH], AX, ALU.add).then_inc(q["part_ready"], 1)
            v.wait_ge(q["w_in"], 80)
            v.wait_ge(q["totalled"], 1)
            step(nc.vector.tensor_scalar(total[:, :], total[:, :], 1.0 / z.nodes, None, ALU.mult))
            step(nc.vector.tensor_tensor(w_a[:, :], w_a[:, :], w_b[:, :], ALU.add))
            step(nc.vector.tensor_tensor(w_a[:, :], w_a[:, :], total[:, :], ALU.mult))
            step(nc.vector.tensor_tensor(b1[:, :], w_a[:, :], b_lin[:, :], ALU.add))
            v.sem_inc(q["b_ready"], 1)
            with v.Fori(0, NCH) as c:
                v.wait_ge(q["xm_done"], c + 2)
                v.wait_ge(q["stored"], c * 16 + 16)
                nc.vector.tensor_copy(tab[:, :, :], ps_x[:, :, :]).then_inc(q["table_ready"], 1)


def last_nodes(nc, z, m, ins, out_dram):
    NCH = z.chunks
    with Phase(nc) as ctx:
        ph = NodePhase(nc, ctx, "nl")
        w, bias = ph.sb("w", [D, D]), ph.sb("bias", [P, D])
        x, ht, y, out = ph.sb("x", [P, CT, D]), ph.sb("ht", [D, CH]), ph.sb("y", [P, CT, D]), ph.sb("out", [P, CT, D])
        ps = ph.ps("ps", [P, CT, D])
        norm = Norm(nc, ph)
        q = {n: ph.sem(n) for n in ("w_in", "x_in", "x_read", "taken", "product", "normed", "stored", "step")}
        block = ctx.enter_context(nc.Block())
        PER = 3 + LN_STEPS

        @block.sync
        def _(sp):
            sp.sem_inc(q["stored"], 16)
            sp.dma_start(w[:, :], ins["L3_gnn_out_w"]).then_inc(q["w_in"], 16)
            sp.dma_start(bias[:, :], ins["L3_gnn_out_b"].partition_broadcast(P)).then_inc(q["w_in"], 16)

            def load(c):
                sp.wait_ge(q["x_read"], c + 1)
                sp.dma_start(x[:, :, :], rows(m.x3, c)).then_inc(q["x_in"], 16)
                sp.wait_ge(q["normed"], c + 1)

            if NCH > 1:
                with sp.Fori(0, NCH - 1) as c:
                    load(c)
                    sp.dma_start(rows(out_dram, c), out[:, :, :]).then_inc(q["stored"], 16)
            load(NCH - 1)
            n = 0
            for k in range(CT):
                at = (NCH - 1) * CH + k * P
                real = min(P, z.nodes - at)
                if real > 0:
                    sp.dma_start(out_dram[at:at + real, :], out[0:real, k, :]).then_inc(q["stored"], 16)
                    n += 1
            sp.wait_ge(q["stored"], 16 * (NCH + n))

        @block.tensor
        def _(pe):
            pe.sem_inc(q["product"], 1)
            pe.wait_ge(q["w_in"], 32)
            with pe.Fori(0, NCH) as c:
                pe.wait_ge(q["taken"], c + 1)
                pe.wait_ge(q["x_read"], c + 1)
                for k in range(CT):
                    last = nc.tensor.matmul(ps[:, k, :], ht[:, k * P:(k + 1) * P], w[:, :], start=True, stop=True)
                last.then_inc(q["product"], 1)

        @block.scalar
        def _(act):
            with act.Fori(0, NCH) as c:
                act.wait_ge(q["product"], c + 1)
                nc.scalar.copy(ht[:, :], cols(m.hidden, c * CH, CH)).then_inc(q["taken"], 1)
                norm.scalar(act, c)

        @block.vector
        def _(v):
            v.sem_inc(q["x_read"], 1)
            v.wait_ge(q["w_in"], 32)
            with v.Fori(0, NCH) as c:
                step = Chain(v, q["step"], c * PER, PER)
                v.wait_ge(q["product"], c + 2)
                step(nc.vector.tensor_tensor(y[:, :, :], ps[:, :, :], bias[:, :].unsqueeze(1).to_broadcast([P, CT, D]), ALU.add))
                step(nc.vector.tensor_scalar(y[:, :, :], y[:, :, :], 0.0, None, ALU.max))
                v.wait_ge(q["x_in"], c * 16 + 16)
                step(nc.vector.tensor_tensor(y[:, :, :], y[:, :, :], x[:, :, :], ALU.add))
                v.sem_inc(q["x_read"], 1)
                v.wait_ge(q["stored"], c * 16 + 16)
                norm.vector(v, step, c, y, out)
                v.sem_inc(q["normed"], 1)
                step.done()


def build(nc, z, ins, out, layers):
    class M:
        pass

    m = M()
    with ExitStack() as ctx:
        def sb(name, shape, dt=F32):
            return ctx.enter_context(nc.sbuf_tensor(name, shape, dt))

        NT, NP = z.tiles, z.padded
        m.ident, m.lane = sb("ident", [P, P]), sb("lane", [P, P])
        m.lane_bf, m.ones = sb("lane_bf", [P, P], BF16), sb("ones", [P, P])
        m.src_idx, m.dst_idx = sb("src_idx", [P, NT], I32), sb("dst_idx", [P, NT], I32)
        m.loc, m.last, m.w = sb("loc", [P, NT]), sb("last", [P, NT]), sb("w", [P, NT])
        m.base_row = sb("base_row", [1, z.groups * QPG], I32)
        m.acc = sb("acc", [P, z.cols])
        m.side = m.hidden = sb("side", [P, max(z.cols, 5 * 2 * GE)])
        m.deg, m.scale = sb("deg", [P, 3, z.node_tiles]), sb("scale", [P, 3, z.node_tiles])

        m.x0, m.x1, m.x2, m.x3 = (nc.dram_tensor(f"x{i}", [NP, D], F32) for i in range(4))
        m.table0, m.table1, m.table3 = (nc.dram_tensor(f"table{i}", [NP, D], F32) for i in (0, 1, 3))
        m.dst_pad = nc.dram_tensor("dst_pad", [z.groups, GE], I32)
        m.bases = nc.dram_tensor("bases", [z.groups, QPG], I32)
        m.counts = nc.dram_tensor("counts", [1, NP], F32)

        m.resets4 = nc.dram_tensor("resets4", [z.groups, HEADS * GE], F32)
        m.table2 = nc.dram_tensor("table2", [NP, ROW2], F32)
        m.dst_terms = nc.dram_tensor("dst_terms", [NP, 2 * HEADS], F32)
        m.stash = nc.dram_tensor("stash", [z.groups * P, G * ROW2], F32)
        m.att, m.p_self = sb("att", [P, z.node_tiles, 2 * HEADS]), sb("p_self", [P, z.node_tiles, HEADS])
        m.low, m.sums = sb("low", [P, 1]), sb("sums", [P, z.chunks])

        with ExitStack() as early:
            m.src_lo, m.src_hi = (early.enter_context(nc.sbuf_tensor(n, [P, NT], F32)) for n in ("src_lo", "src_hi"))
            prepare(nc, z, m, ins)
            out_degrees(nc, z, m)
            inverse_roots(nc, z, m, range(0, 1))
            scale_rows(nc, z, m)
            sum_over_edges(nc, z, m, m.table0, None, "e0", degrees=True)
        inverse_roots(nc, z, m, range(1, 3))
        layer0_nodes(nc, z, m, ins)
        if layers == 1:
            return dump(nc, z, m.x1, out)
        sum_over_edges(nc, z, m, m.table1, m.w, "e1")
        layer1_nodes(nc, z, m, ins)
        if layers == 2:
            return dump(nc, z, m.x2, out)
        lowest_source(nc, z, m)
        highest_source(nc, z, m)
        attention_nodes(nc, z, m)
        weighted_sum(nc, z, m)
        layer2_nodes(nc, z, m, ins)
        if layers == 3:
            return dump(nc, z, m.x3, out)
        cutoffs(nc, z, m)
        continuous_conv(nc, z, m, ins, 0)
        conv_nodes(nc, z, m, ins, 0)
        next_messages(nc, z, m, ins)
        continuous_conv(nc, z, m, ins, 1)
        conv_nodes(nc, z, m, ins, 1)
        last_nodes(nc, z, m, ins, out)


def dump(nc, z, x, out):
    with nc.semaphore("dumped") as s, nc.Block() as block:
        @block.sync
        def _(sp):
            sp.dma_start(out, x[0:z.nodes, :]).then_inc(s, 16)
            sp.wait_ge(s, 16)


LAYERS = 4


def kernel(**inputs):
    import concourse.bacc as bacc
    from concourse.bass_utils import run_bass_kernel_spmd as run

    z = Sizes(inputs["x"].shape[0], inputs["src"].shape[0], inputs["edge_attr_50"].shape[1])
    nc = bacc.Bacc("TRN2", target_bir_lowering=False, num_devices=1)
    arrays, ins = {}, {}
    for name, a in inputs.items():
        a = np.ascontiguousarray(a)
        arrays[f"in_{name}"] = a
        ins[name] = nc.dram_tensor(f"in_{name}", a.shape, mybir.dt.from_np(a.dtype), kind="ExternalInput").ap()
    out = nc.dram_tensor("out", [z.nodes, D], F32, kind="ExternalOutput").ap()
    build(nc, z, ins, out, LAYERS)
    return run(nc, [arrays], core_ids=[0]).results[0]["out"]
```

```python
from contextlib import ExitStack

import numpy as np
import concourse.bass as bass
from concourse import mybir

F32 = mybir.dt.float32
BF16 = mybir.dt.bfloat16
I32 = mybir.dt.int32
ALU = mybir.AluOpType
ACT = mybir.ActivationFunctionType
AX = mybir.AxisListType.X

P = 128
D = 128
G = 8
GE = G * P
QUAD = 4
QPG = G // QUAD
QE = QUAD * P
SLOTS = 64
CT = 4
CH = CT * P
HEADS = 4
HD = D // HEADS
EPS = 1e-5
ROW2 = D + HEADS
RESET = -1.0e30
PI = float(np.pi)
LN2 = float(np.log(2.0))


def ceil_to(n, k):
    return -(-n // k) * k


class Sizes:

    def __init__(self, nodes, edges, gauss):
        self.nodes, self.edges, self.gauss = nodes, edges, gauss
        self.groups = ceil_to(-(-edges // GE), 2)
        self.half = self.groups // 2
        self.tiles = self.groups * G
        self.padded = ceil_to(nodes + 1, CH)
        self.chunks = self.padded // CH
        self.node_tiles = self.padded // P
        self.cols = self.padded + P


class Chain:

    def __init__(self, eng, sem, base, per=None):
        self.eng, self.sem, self.base, self.per, self.n = eng, sem, base, per, 0

    def go(self, ins):
        self.n += 1
        ins.then_inc(self.sem, 1)

    def wait(self):
        self.eng.wait_ge(self.sem, self.base + self.n)

    def __call__(self, ins):
        self.go(ins)
        self.wait()

    def done(self):
        assert self.per is None or self.n == self.per, self.n


class Phase(ExitStack):

    def __init__(self, nc):
        super().__init__()
        self.nc, self.sems = nc, []

    def semaphore(self, name):
        self.sems.append(self.nc.alloc_semaphore(name))
        return self.sems[-1]

    def __exit__(self, *what):
        super().__exit__(*what)
        if what[0] is None:
            self.nc.clear_and_free_semaphores(self.sems)
            self.nc.all_engine_barrier()


class Group:

    def __init__(self, no, par, rnd):
        self.no, self.par, self.rnd = no, par, rnd


def pipeline(eng, groups, depth, run):
    def static(g):
        return lambda i: Group(g + i, (g + i) % 2, (g + i) // 2) if 0 <= g + i < groups else None

    def looped(b, p):
        return lambda i: Group(b * 2 + (p + i), (p + i) % 2, b + (p + i) // 2)

    loops = max(0, (groups - depth) // 2)
    for g in range(-depth, 0):
        run(static(g))
    if loops:
        with eng.Fori(0, loops) as b:
            for p in range(2):
                run(looped(b, p))
    for g in range(2 * loops, groups):
        run(static(g))


def bc(ap, n):
    return ap.unsqueeze(2).to_broadcast([ap.shape[0], ap.shape[1], n])


def cols(t, start, size):
    return t[:, bass.ds(start, size)]



def prepare(nc, z, m, ins):
    E, HG, NT = z.edges, z.half, z.tiles
    full = E // GE - HG
    rest = E % GE
    with Phase(nc) as ctx:
        def sb(name, shape, dt=F32):
            return ctx.enter_context(nc.sbuf_tensor(name, shape, dt))

        src_i = sb("src_i", [HG, 2 * GE], I32)
        dst_i = sb("dst_i", [HG, 2 * GE], I32)
        src_f, dst_f, loc, last, change = (m.side[0:HG, i * 2 * GE:(i + 1) * 2 * GE] for i in range(5))
        w_e = sb("w_e", [HG, 2 * GE])
        lane_i = sb("lane_i", [P, P], I32)
        NQ = 2 * QPG
        lo, hi, bad, tmp = (sb(n, [HG, NQ]) for n in ("lo_q", "hi_q", "bad_q", "tmp_q"))
        badg = sb("bad_g", [HG, 2])
        base_i = sb("base_i", [HG, NQ], I32)
        lohi_i = sb("lohi_i", [P, NT], I32)
        zeros = sb("zeros", [P, D])
        ps = [ctx.enter_context(nc.psum_tensor(f"prep_ps{i}", [P, 4, P], F32)) for i in range(4)]

        sem = {n: ctx.semaphore(n) for n in (
            "edges_in", "padded", "consts", "ident_zero", "prep_step", "moved", "copied", "spilled",
            "rows_padded", "tables", "weights_in", "lanes")}

        def whole(t):
            return t[:, :].rearrange("p (h n) -> p h n", h=2)

        tile3 = lambda t: t[:, :].rearrange("p (t e) -> p t e", e=P)
        quad3 = lambda t: t[:, :].rearrange("p (q e) -> p q e", e=QE)
        block = ctx.enter_context(nc.Block())
        moves = [(src_f, m.src_idx), (dst_f, m.dst_idx), (loc, m.loc), (last, m.last), (w_e, m.w)]
        n_edge_dmas = 3 * (1 + (full > 0) + (rest > 0))

        @block.sync
        def _(sp):
            sp.wait_ge(sem["padded"], 4)
            for name, t in (("src", src_i), ("dst", dst_i), ("edge_weight", w_e)):
                a = ins[name]
                sp.dma_start(t[:, 0:GE], a[0:HG * GE].rearrange("(p n) -> p n", n=GE)).then_inc(sem["edges_in"], 16)
                if full:
                    sp.dma_start(t[0:full, GE:2 * GE], a[HG * GE:(HG + full) * GE].rearrange("(p n) -> p n", n=GE)).then_inc(sem["edges_in"], 16)
                if rest:
                    at = (HG + full) * GE
                    sp.dma_start(t[full:full + 1, GE:GE + rest], a[at:E].rearrange("(p n) -> p n", p=1)).then_inc(sem["edges_in"], 16)
            n = 0
            sp.dma_start(m.x0[0:z.nodes, :], ins["x"]).then_inc(sem["rows_padded"], 16)
            n += 1
            for at in range(z.nodes, z.padded, P):
                k = min(P, z.padded - at)
                sp.dma_start(m.x0[at:at + k, :], zeros[0:k, :]).then_inc(sem["rows_padded"], 16)
                n += 1
            sp.wait_ge(sem["edges_in"], 16 * n_edge_dmas)
            for h in range(2):
                sp.dma_start(m.dst_pad[h * HG:(h + 1) * HG, :], dst_i[:, h * GE:(h + 1) * GE]).then_inc(sem["spilled"], 16)
            sp.wait_ge(sem["tables"], 2)
            for h in range(2):
                for r_ in range(HEADS):
                    sp.dma_start(m.resets4[h * HG:(h + 1) * HG, :].rearrange("g (k r e) -> g k r e", r=HEADS, e=P)[:, :, r_, :],
                                 change[:, h * GE:(h + 1) * GE].rearrange("g (k e) -> g k e", e=P)).then_inc(sem["spilled"], 16)
                sp.dma_start(m.bases[h * HG:(h + 1) * HG, :], base_i[:, h * QPG:(h + 1) * QPG]).then_inc(sem["spilled"], 16)
            n_spilled = 2 * (1 + HEADS + 1)
            sp.wait_ge(sem["spilled"], 16 * n_spilled)
            sp.dma_start(m.base_row[:, :], m.bases[:, :].rearrange("g k -> (g k)").rearrange("(o n) -> o n", o=1)).then_inc(sem["spilled"], 16)
            sp.wait_ge(sem["spilled"], 16 * (n_spilled + 1))
            sp.wait_ge(sem["rows_padded"], 16 * n)

        @block.gpsimd
        def _(pool):
            nc.gpsimd.memset(m.ident[:, :], 0.0).then_inc(sem["ident_zero"], 1)
            pool.wait_ge(sem["ident_zero"], 1)
            nc.gpsimd.affine_select(out=m.ident[:, :], in_=m.ident[:, :], compare_op=ALU.not_equal, fill=1.0,
                                    base=0, pattern=[[-1, P]], channel_multiplier=1).then_inc(sem["consts"], 1)
            nc.gpsimd.iota(lane_i[:, :], pattern=[[1, P]], base=0, channel_multiplier=0).then_inc(sem["consts"], 1)

        @block.tensor
        def _(pe):
            pe.wait_ge(sem["consts"], 1)
            pe.wait_ge(sem["tables"], 2)
            i = 0
            for src, _ in moves:
                for h in range(2):
                    for q in range(2):
                        if i >= 4:
                            pe.wait_ge(sem["copied"], i - 3)
                        for k in range(4):
                            at = h * GE + (q * 4 + k) * P
                            last_one = nc.tensor.transpose(ps[i % 4][:, k, 0:HG], src[:, at:at + P], m.ident[0:HG, 0:HG])
                        last_one.then_inc(sem["moved"], 1)
                        i += 1

        @block.vector
        def _(v):
            step = Chain(v, sem["prep_step"], 0)
            nc.vector.memset(src_i[:, :], z.nodes).then_inc(sem["padded"], 1)
            nc.vector.memset(dst_i[:, :], z.nodes).then_inc(sem["padded"], 1)
            nc.vector.memset(w_e[:, :], 0.0).then_inc(sem["padded"], 1)
            nc.vector.memset(zeros[:, :], 0.0).then_inc(sem["padded"], 1)
            step(nc.vector.memset(m.ones[:, :], 1.0))
            v.wait_ge(sem["consts"], 2)
            step(nc.vector.tensor_copy(m.lane[:, :], lane_i[:, :]))
            step(nc.vector.tensor_copy(m.lane_bf[:, :], lane_i[:, :]))
            v.wait_ge(sem["edges_in"], 16 * n_edge_dmas)
            step(nc.vector.tensor_copy(src_f[:, :], src_i[:, :]))
            step(nc.vector.tensor_copy(dst_f[:, :], dst_i[:, :]))
            l3, c3, e3 = tile3(loc), tile3(change), tile3(last)
            dq, lq, cq = quad3(dst_f), quad3(loc), quad3(change)
            step(nc.vector.tensor_reduce(lo[:, :], dq, AX, ALU.min))
            step(nc.vector.tensor_reduce(hi[:, :], dq, AX, ALU.max))
            step(nc.vector.tensor_tensor(cq[:, :, 1:QE], dq[:, :, 1:QE], dq[:, :, 0:QE - 1], ALU.subtract))
            step(nc.vector.tensor_reduce(tmp[:, :], cq[:, :, 1:QE], AX, ALU.min))
            step(nc.vector.tensor_scalar(tmp[:, :], tmp[:, :], 0.0, None, ALU.is_lt))
            step(nc.vector.tensor_tensor(hi[:, :], hi[:, :], lo[:, :], ALU.subtract))
            step(nc.vector.tensor_scalar(hi[:, :], hi[:, :], float(SLOTS), None, ALU.is_ge))
            step(nc.vector.tensor_tensor(hi[:, :], hi[:, :], tmp[:, :], ALU.max))
            step(nc.vector.tensor_reduce(badg[:, :], hi[:, :].rearrange("p (h k) -> p h k", h=2), AX, ALU.max))
            step(nc.vector.tensor_copy(bad[:, :].rearrange("p (h k) -> p h k", h=2), bc(badg[:, :], QPG)))
            step(nc.vector.tensor_tensor(lq, dq, bc(lo[:, :], QE), ALU.subtract))
            step(nc.vector.tensor_tensor(c3, m.lane[0:HG, :].unsqueeze(1).to_broadcast([HG, 2 * G, P]), l3, ALU.subtract))
            step(nc.vector.tensor_tensor(cq, cq, bc(bad[:, :], QE), ALU.mult))
            step(nc.vector.tensor_tensor(l3, l3, c3, ALU.add))
            step(nc.vector.tensor_scalar(tmp[:, :], lo[:, :], 1.0, None, ALU.add))
            step(nc.vector.tensor_tensor(tmp[:, :], tmp[:, :], bad[:, :], ALU.mult))
            step(nc.vector.tensor_tensor(tmp[:, :], lo[:, :], tmp[:, :], ALU.subtract))
            step(nc.vector.tensor_copy(base_i[:, :], tmp[:, :]))
            step(nc.vector.tensor_tensor(c3[:, :, 1:P], l3[:, :, 1:P], l3[:, :, 0:P - 1], ALU.not_equal))
            step(nc.vector.memset(c3[:, :, 0:1], 1.0))
            step(nc.vector.tensor_scalar(e3[:, :, 0:P - 1], l3[:, :, 0:P - 1], 1.0, None, ALU.add))
            step(nc.vector.tensor_tensor(e3[:, :, 0:P - 1], e3[:, :, 0:P - 1], c3[:, :, 1:P], ALU.mult))
            step(nc.vector.tensor_scalar(e3[:, :, 0:P - 1], e3[:, :, 0:P - 1], -1.0, None, ALU.add))
            step(nc.vector.tensor_copy(e3[:, :, P - 1:P], l3[:, :, P - 1:P]))
            nc.vector.tensor_scalar(change[:, :], change[:, :], RESET, None, ALU.mult).then_inc(sem["tables"], 1)
            v.wait_ge(sem["tables"], 1)
            v.sem_inc(sem["tables"], 1)
            i = 0
            for _, table in moves:
                for h in range(2):
                    for q in range(2):
                        v.wait_ge(sem["moved"], i + 1)
                        out = table[:, 0:NT].rearrange("p (h g k) -> p h k g", h=2, k=G)[:, h, q * 4:q * 4 + 4, :]
                        nc.vector.tensor_copy(out, ps[i % 4][:, :, 0:HG]).then_inc(sem["copied"], 1)
                        i += 1
            v.wait_ge(sem["copied"], i)
            step(nc.vector.tensor_scalar(lohi_i[:, :], m.src_idx[:, 0:NT], P - 1, None, ALU.bitwise_and))
            step(nc.vector.tensor_copy(m.src_lo[:, :], lohi_i[:, :]))
            step(nc.vector.tensor_scalar(lohi_i[:, :], m.src_idx[:, 0:NT], 7, None, ALU.logical_shift_right))
            step(nc.vector.tensor_copy(m.src_hi[:, :], lohi_i[:, :]))



def out_degrees(nc, z, m):
    NPT = z.node_tiles
    with Phase(nc) as ctx:
        def sb(name, shape, dt=F32):
            return ctx.enter_context(nc.sbuf_tensor(name, shape, dt))

        low, high = sb("low1", [P, 2, G, P], BF16), sb("high1", [P, 2, G, NPT], BF16)
        low_t, high_t = sb("low_t", [P, z.tiles], BF16), sb("high_t", [P, z.tiles], BF16)
        ps = [ctx.enter_context(nc.psum_tensor(f"ps_deg{i}", [P, NPT], F32)) for i in range(2)]
        hot_ready = [ctx.semaphore(f"hot_ready{i}") for i in range(2)]
        summed = [ctx.semaphore(f"summed{i}") for i in range(2)]
        added, cast = ctx.semaphore("hist_added"), ctx.semaphore("hist_cast")
        block = ctx.enter_context(nc.Block())

        @block.vector
        def _(v):
            nc.vector.tensor_copy(low_t[:, :], m.src_lo[:, :]).then_inc(cast, 1)
            nc.vector.tensor_copy(high_t[:, :], m.src_hi[:, :]).then_inc(cast, 1)
            nc.vector.memset(m.deg[:, :, :], 0.0).then_inc(added, 1)
            v.wait_ge(cast, 2)

            def run(f):
                if a := f(1):
                    v.wait_ge(summed[a.par], a.rnd + 1)
                    lanes = lambda n: m.lane_bf[:, 0:n].unsqueeze(1).to_broadcast([P, G, n])
                    nc.vector.tensor_tensor(low[:, a.par, :, :], lanes(P), bc(cols(low_t, a.no * G, G), P), ALU.is_equal)
                    nc.vector.tensor_tensor(high[:, a.par, :, :], lanes(NPT), bc(cols(high_t, a.no * G, G), NPT), ALU.is_equal).then_inc(hot_ready[a.par], 1)
                if g := f(0):
                    v.wait_ge(summed[g.par], g.rnd + 2)
                    v.wait_ge(added, g.no + 1)
                    nc.vector.tensor_tensor(m.deg[:, 0, :], m.deg[:, 0, :], ps[g.par][:, :], ALU.add).then_inc(added, 1)

            pipeline(v, z.groups, 1, run)
            v.wait_ge(added, z.groups + 1)

        @block.tensor
        def _(pe):
            for par in range(2):
                pe.sem_inc(summed[par], 1)

            def run(f):
                g = f(0)
                pe.wait_ge(hot_ready[g.par], g.rnd + 1)
                for k in range(G):
                    last = nc.tensor.matmul(ps[g.par][:, :], low[:, g.par, k, :], high[:, g.par, k, :], start=(k == 0), stop=(k == G - 1))
                last.then_inc(summed[g.par], 1)

            pipeline(pe, z.groups, 0, run)


def inverse_roots(nc, z, m, which):
    NPT = z.node_tiles
    a, b = which.start, which.stop
    with Phase(nc) as ctx:
        root, t = (ctx.enter_context(nc.sbuf_tensor(f"{n}{a}", [P, b - a, NPT], F32)) for n in ("root", "root_t"))
        count_t = ctx.enter_context(nc.sbuf_tensor(f"count_t{a}", [NPT, P], F32))
        ps = ctx.enter_context(nc.psum_tensor(f"count_ps{a}", [P, NPT], F32))
        counts, prepared, rooted, stepped, turned = (ctx.semaphore(f"{n}{a}") for n in ("counts_in", "deg_prepared", "deg_rooted", "deg_step", "deg_turned"))
        block = ctx.enter_context(nc.Block())
        in_degree = b > 2

        if in_degree:
            @block.sync
            def _(sp):
                sp.dma_start(m.counts[:, :], m.side[0:1, 0:z.padded]).then_inc(counts, 16)
                sp.wait_ge(counts, 16)
                sp.dma_start(count_t[:, :], m.counts[:, :].rearrange("o (t p) -> (o t) p", p=P)).then_inc(counts, 16)

            @block.tensor
            def _(pe):
                pe.wait_ge(counts, 32)
                nc.tensor.transpose(ps[:, :], count_t[:, :], m.ident[0:NPT, 0:NPT]).then_inc(turned, 1)

        @block.scalar
        def _(act):
            act.wait_ge(prepared, 1)
            nc.scalar.activation(root[:, :, :], m.deg[:, a:b, :], ACT.Sqrt).then_inc(rooted, 1)

        @block.vector
        def _(v):
            step = Chain(v, stepped, 0)
            for i in which:
                if i == 2:
                    v.wait_ge(turned, 1)
                    step(nc.vector.tensor_copy(m.deg[:, 2, :], ps[:, :]))
                step(nc.vector.tensor_scalar(m.deg[:, i, :], m.deg[:, i, :], 1.0, None, ALU.add if i == 1 else ALU.max))
            v.sem_inc(prepared, 1)
            v.wait_ge(rooted, 1)
            newton(nc, step, m.scale[:, a:b, :], m.deg[:, a:b, :], root[:, :, :], t[:, :, :])


def newton(nc, step, out, x, root, t):
    step(nc.vector.reciprocal(out, root))
    step(nc.vector.tensor_tensor(t, out, out, ALU.mult))
    step(nc.vector.tensor_tensor(t, t, x, ALU.mult))
    step(nc.vector.tensor_scalar(t, t, -0.5, 1.5, ALU.mult, ALU.add))
    step(nc.vector.tensor_tensor(out, out, t, ALU.mult))


NEWTON_STEPS = 5


def rows(table, c, width=D):
    return table[bass.ds(c * CH, CH), 0:width].rearrange("(k p) f -> p k f", p=P)


def scale_rows(nc, z, m):
    with Phase(nc) as ctx:
        xin = ctx.enter_context(nc.sbuf_tensor("sr_x", [P, 2, CT, D], F32))
        out = ctx.enter_context(nc.sbuf_tensor("sr_y", [P, 2, CT, D], F32))
        x_in = [ctx.semaphore(f"sr_x_in{i}") for i in range(2)]
        stored = [ctx.semaphore(f"sr_stored{i}") for i in range(2)]
        scaled = [ctx.semaphore(f"sr_scaled{i}") for i in range(2)]
        block = ctx.enter_context(nc.Block())

        @block.sync
        def _(sp):
            for c in range(z.chunks):
                if c >= 2:
                    sp.wait_ge(scaled[c % 2], c // 2)
                sp.dma_start(xin[:, c % 2, :, :], rows(m.x0, c)).then_inc(x_in[c % 2], 16)

        @block.vector
        def _(v):
            for c in range(z.chunks):
                v.wait_ge(x_in[c % 2], 16 * (c // 2 + 1))
                if c >= 2:
                    v.wait_ge(stored[c % 2], 16 * (c // 2))
                last = nc.vector.tensor_tensor(out[:, c % 2, :, :], xin[:, c % 2, :, :], bc(m.scale[:, 0, c * CT:(c + 1) * CT], D), ALU.mult)
                last.then_inc(scaled[c % 2], 1)

        @block.scalar
        def _(act):
            for c in range(z.chunks):
                act.wait_ge(scaled[c % 2], c // 2 + 1)
                act.dma_start(rows(m.table0, c), out[:, c % 2, :, :]).then_inc(stored[c % 2], 16)
            for i in range(2):
                act.wait_ge(stored[i], 16 * ((z.chunks + 1 - i) // 2))



class Windows:

    def __init__(self, nc, ctx, m, z, name, targets, apart=False):
        self.nc, self.m, self.z, self.name, self.targets, self.apart = nc, m, z, name, targets, apart
        self.n = G if apart else QPG
        self.added = [ctx.semaphore(f"{name}_added{i}") for i in range(len(targets))]
        self.hot_written = ctx.semaphore(f"{name}_hot_written")
        self.begun = ctx.semaphore(f"{name}_begun")

    def registers(self, v):
        self.bases = [[v.alloc_register(f"{self.name}_base{p}{k}") for k in range(QPG)] for p in range(2)]
        self.dst = v.alloc_register(f"{self.name}_dst")

    def clear(self):
        for (target, _, n, _), added in zip(self.targets, self.added):
            self.nc.vector.memset(target[0:n, :], 0.0).then_inc(added, 1)

    def free(self, eng, g):
        for added in self.added:
            eng.wait_ge(added, g.no * self.n + 1)

    def finish(self, v):
        for added in self.added:
            v.wait_ge(added, self.z.groups * self.n + 1)

    def one_hot(self, v, g, hot, slot, weights=None):
        nc, m = self.nc, self.m
        v.load(self.bases[g.par], m.base_row[0:1, bass.ds(g.no * QPG, QPG)])

        def write(width):
            if weights is None:
                last = nc.vector.tensor_tensor(hot[:, g.par, :, 0:width], m.lane[:, 0:width].unsqueeze(1).to_broadcast([P, G, width]),
                                               bc(cols(slot, g.no * G, G), width), ALU.is_equal)
            else:
                for k in range(G):
                    t = g.no * G + k
                    last = nc.vector.tensor_scalar(hot[:, g.par, k, 0:width], m.lane[:, 0:width], cols(slot, t, 1), cols(weights, t, 1),
                                                   ALU.is_equal, ALU.mult)
            return last

        with v.If_lt(self.bases[g.par][0], 0):
            write(P).then_inc(self.hot_written, 1)
        with v.Else():
            write(SLOTS).then_inc(self.hot_written, 1)

    def hot_ready(self, eng, g):
        eng.wait_ge(self.hot_written, g.no + 1)

    def column(self, pe, g, reg):
        pe.load(reg, self.m.base_row[0:1, bass.ds(g.no * QPG, 1)])

    def product(self, pe, g, reg, pairs, hot):
        nc = self.nc
        with pe.If_lt(reg, 0):
            for k in range(G):
                for out, left in pairs:
                    nc.tensor.matmul(out[:, k * P:(k + 1) * P], left(k), hot[:, g.par, k, :], start=True, stop=True)
        with pe.Else():
            for k in range(G):
                for out, left in pairs:
                    at = k * P if self.apart else k // QUAD * SLOTS
                    nc.tensor.matmul(out[:, at:at + SLOTS], left(k), hot[:, g.par, k, 0:SLOTS],
                                     start=self.apart or k % QUAD == 0, stop=self.apart or k % QUAD == QUAD - 1)

    def add(self, v, g):
        nc, z, m = self.nc, self.z, self.m
        v.sem_inc(self.begun, 1)
        with v.If_lt(self.bases[g.par][0], 0):
            self.free(v, g)
            v.sem_inc(self.begun, 1)
            with v.Fori(0, GE) as e:
                v.load(self.dst, m.dst_pad[bass.ds(g.no, 1), bass.ds(e, 1)])
                col = v.snap(self.dst, min_val=0, max_val=z.cols - 1)
                for target, source, n, op in self.targets:
                    nc.vector.tensor_tensor(target[0:n, bass.ds(col, 1)], target[0:n, bass.ds(col, 1)],
                                            source[0:n, bass.ds(e, 1)], op)
                v.drain()
            for added in self.added:
                v.drain().then_inc(added, self.n)
        with v.Else():
            for i in range(self.n):
                at, quad = (i * P, i // QUAD) if self.apart else (i * SLOTS, i)
                base = v.snap(self.bases[g.par][quad], min_val=0, max_val=z.cols - P)
                for (target, source, n, op), added in zip(self.targets, self.added):
                    v.wait_ge(added, g.no * self.n + i + 1)
                    nc.vector.tensor_tensor(target[0:n, bass.ds(base, SLOTS)], target[0:n, bass.ds(base, SLOTS)],
                                            source[0:n, at:at + SLOTS], op).then_inc(added, 1)


def gather(nc, pool, table, idx, out, g, landed):
    for k in range(G):
        pool.indirect_dma_start(out=out[:, g.par, k, :], out_offset=None, in_=table[:, :],
                                in_offset=bass.IndirectOffsetOnAxis(ap=idx[:, g.par, k:k + 1], axis=0)).then_inc(landed[g.par], 16)


def sum_over_edges(nc, z, m, table, weights, name, degrees=False):
    NPT = z.node_tiles
    with Phase(nc) as ctx:
        sb = lambda n, shape, dt=F32: ctx.enter_context(nc.sbuf_tensor(f"{name}_{n}", shape, dt))
        psum = lambda n, shape: ctx.enter_context(nc.psum_tensor(f"{name}_{n}", shape, F32))
        rows_, hot, idx = sb("rows", [P, 2, G, D]), sb("hot", [P, 2, G, P]), sb("idx", [P, 2, G], I32)
        ps = psum("ps", [P, GE])
        targets = [(m.acc, ps, P, ALU.add)]
        if degrees:
            low, high = sb("low", [P, 2, G, P]), sb("high", [P, 2, G, NPT])
            ps_count = psum("ps_count", [1, GE])
            ps_w = [psum(f"ps_w{i}", [P, NPT]) for i in range(2)]
            targets.append((m.side, ps_count, 1, ALU.add))
        two = lambda n: [ctx.semaphore(f"{name}_{n}{i}") for i in range(2)]
        idx_staged, rows_in, summed, hist_ready = two("idx_staged"), two("rows_in"), two("summed"), two("hist_ready")
        gather_begun, hist_added = ctx.semaphore(f"{name}_gather_begun"), ctx.semaphore(f"{name}_hist_added")
        windows = Windows(nc, ctx, m, z, name, targets)
        block = ctx.enter_context(nc.Block())

        @block.scalar
        def _(act):
            def run(f):
                g = f(0)
                act.wait_ge(summed[g.par], g.rnd + 1)
                nc.scalar.copy(idx[:, g.par, :], cols(m.src_idx, g.no * G, G)).then_inc(idx_staged[g.par], 1)

            pipeline(act, z.groups, 0, run)

        @block.gpsimd
        def _(pool):
            def run(f):
                g = f(0)
                pool.wait_ge(idx_staged[g.par], g.rnd + 1)
                pool.wait_ge(summed[g.par], g.rnd + 1)
                pool.sem_inc(gather_begun, 1)
                gather(nc, pool, table, idx, rows_, g, rows_in)

            pipeline(pool, z.groups, 0, run)

        @block.tensor
        def _(pe):
            reg = pe.alloc_register(f"{name}_pe_base")
            for par in range(2):
                pe.sem_inc(summed[par], 1)

            def run(f):
                g = f(0)
                pairs = [(ps, lambda k: rows_[:, g.par, k, :])]
                windows.column(pe, g, reg)
                if degrees:
                    pairs.append((ps_count, lambda k: m.ones[:, 0:1]))
                    pe.wait_ge(hist_ready[g.par], g.rnd + 1)
                    for k in range(G):
                        nc.tensor.matmul(ps_w[g.par][:, :], low[:, g.par, k, :], high[:, g.par, k, :], start=(k == 0), stop=(k == G - 1))
                windows.hot_ready(pe, g)
                pe.wait_ge(rows_in[g.par], (g.rnd + 1) * (16 * G))
                windows.free(pe, g)
                windows.product(pe, g, reg, pairs, hot)
                pe.drain().then_inc(summed[g.par], 1)

            pipeline(pe, z.groups, 0, run)

        @block.vector
        def _(v):
            windows.registers(v)
            windows.clear()
            v.sem_inc(hist_added, 1)

            def run(f):
                if a := f(1):
                    v.wait_ge(summed[a.par], a.rnd + 1)
                    windows.one_hot(v, a, hot, m.loc, weights)
                    if degrees:
                        for k in range(G):
                            t = a.no * G + k
                            nc.vector.tensor_scalar(low[:, a.par, k, :], m.lane[:, :], cols(m.src_lo, t, 1), None, ALU.is_equal)
                            last = nc.vector.tensor_scalar(high[:, a.par, k, :], m.lane[:, 0:NPT], cols(m.src_hi, t, 1), cols(m.w, t, 1),
                                                           ALU.is_equal, ALU.mult)
                        last.then_inc(hist_ready[a.par], 1)
                if g := f(0):
                    v.wait_ge(summed[g.par], g.rnd + 2)
                    windows.add(v, g)
                    if degrees:
                        v.wait_ge(hist_added, g.no + 1)
                        nc.vector.tensor_tensor(m.deg[:, 1, :], m.deg[:, 1, :], ps_w[g.par][:, :], ALU.add).then_inc(hist_added, 1)

            pipeline(v, z.groups, 1, run)
            windows.finish(v)
            if degrees:
                v.wait_ge(hist_added, z.groups + 1)



class NodePhase:

    def __init__(self, nc, ctx, name):
        self.nc, self.ctx, self.name = nc, ctx, name

    def sb(self, name, shape, dt=F32):
        return self.ctx.enter_context(self.nc.sbuf_tensor(f"{self.name}_{name}", shape, dt))

    def ps(self, name, shape):
        return self.ctx.enter_context(self.nc.psum_tensor(f"{self.name}_{name}", shape, F32))

    def sem(self, name):
        return self.ctx.semaphore(f"{self.name}_{name}")

    def sb2(self, name, shape, dt=F32):
        return self.sb(name, [shape[0], 2] + shape[1:], dt)

    def ps2(self, name, shape):
        return [self.ps(f"{name}{i}", shape) for i in range(2)]

    def sem2(self, name):
        return [self.sem(f"{name}{i}") for i in range(2)]


LN_STEPS = 2 * CT + 1 + NEWTON_STEPS + CT


def in_pairs(eng, chunks, run):
    if chunks // 2:
        with eng.Fori(0, chunks // 2) as b:
            run([Group(b * 2, 0, b), Group(b * 2 + 1, 1, b)])
    if chunks % 2:
        run([Group(chunks - 1, 0, chunks // 2)])


def rounds(chunks, par):
    return (chunks + 1 - par) // 2


class Norm:

    def __init__(self, nc, ph):
        self.nc = nc
        self.stats = ph.sb("stats", [P, 2, CT, 6])
        self.mv = ph.sb("meanvar", [P, 2, CT, 2])
        self.var, self.root, self.rstd, self.t = (ph.sb(n, [P, 2, CT]) for n in ("var", "rootv", "rstd", "rstd_t"))
        self.var_ready, self.root_ready = ph.sem2("var_ready"), ph.sem2("root_ready")
        self.stats_taken = ph.sem("stats_taken")

    def moments(self, v, step, g, y):
        nc, p = self.nc, g.par
        for k in range(CT):
            step.go(nc.vector.bn_stats(self.stats[:, p, k, :], y[:, p, k, :]))
        step.wait()
        v.sem_inc(self.stats_taken, 1)
        for k in range(CT):
            step.go(nc.vector.bn_aggr(self.mv[:, p, k, :], self.stats[:, p, k, :]))
        step.wait()
        step(nc.vector.tensor_scalar(self.var[:, p, :], self.mv[:, p, :, 1], EPS, None, ALU.add))
        v.sem_inc(self.var_ready[p], 1)

    def apply(self, v, step, g, y, out):
        nc, p = self.nc, g.par
        v.wait_ge(self.root_ready[p], g.rnd + 1)
        newton(nc, step, self.rstd[:, p, :], self.var[:, p, :], self.root[:, p, :], self.t[:, p, :])
        for k in range(CT):
            step.go(nc.vector.tensor_scalar(out[:, p, k, :], y[:, p, k, :], self.mv[:, p, k, 0:1], self.rstd[:, p, k:k + 1], ALU.subtract, ALU.mult))
        step.wait()

    def scalar(self, act, g):
        act.wait_ge(self.var_ready[g.par], g.rnd + 1)
        self.nc.scalar.activation(self.root[:, g.par, :], self.var[:, g.par, :], ACT.Sqrt).then_inc(self.root_ready[g.par], 1)


def layer0_nodes(nc, z, m, ins):
    with Phase(nc) as ctx:
        ph = NodePhase(nc, ctx, "n0")
        w_self, w_inter = ph.sb("w_self", [D, D]), ph.sb("w_inter", [D, D])
        x, acc_c, xt, hx = ph.sb2("x", [P, CT, D]), ph.sb2("acc_c", [D, CH]), ph.sb2("xt", [D, CH]), ph.sb2("hx", [D, CH])
        y, out, tab = ph.sb2("y", [P, CT, D]), ph.sb2("out", [P, CT, D]), ph.sb2("tab", [P, CT, D])
        ps_t, ps_a, ps_b = ph.ps2("ps_t", [D, CH]), ph.ps2("ps_a", [P, CT, D]), ph.ps2("ps_b", [P, CT, D])
        norm = Norm(nc, ph)
        w_in, storing = ph.sem("w_in"), ph.sem("storing")
        q = {n: ph.sem2(n) for n in ("x_in", "stored", "out_free", "turned", "acc_taken", "ready", "product", "step", "out_ready", "x_read")}
        block = ctx.enter_context(nc.Block())
        PER = 2 + CT + 1 + LN_STEPS + CT

        @block.sync
        def _(sp):
            sp.dma_start(w_self[:, :], ins["L0_gnn_W_self"]).then_inc(w_in, 16)
            sp.dma_start(w_inter[:, :], ins["L0_gnn_W_inter"]).then_inc(w_in, 16)

            def run(gs):
                for g in gs:
                    sp.wait_ge(q["x_read"][g.par], g.rnd + 1)
                    sp.dma_start(x[:, g.par, :, :], rows(m.x0, g.no)).then_inc(q["x_in"][g.par], 16)

            in_pairs(sp, z.chunks, run)

        @block.gpsimd
        def _(pool):
            for par in range(2):
                pool.sem_inc(q["out_free"][par], 1)

            def run(gs):
                for g in gs:
                    pool.wait_ge(q["out_ready"][g.par], g.rnd + 1)
                    pool.sem_inc(storing, 1)
                    pool.dma_start(rows(m.x1, g.no), out[:, g.par, :, :]).then_inc(q["stored"][g.par], 16)
                    pool.dma_start(rows(m.table1, g.no), tab[:, g.par, :, :]).then_inc(q["stored"][g.par], 16)
                for g in gs:
                    pool.wait_ge(q["stored"][g.par], g.rnd * 32 + 32)
                    pool.sem_inc(q["out_free"][g.par], 1)

            in_pairs(pool, z.chunks, run)

        @block.tensor
        def _(pe):
            for par in range(2):
                pe.sem_inc(q["product"][par], 1)
            pe.wait_ge(w_in, 32)

            def run(gs):
                for g in gs:
                    pe.wait_ge(q["x_in"][g.par], g.rnd * 16 + 16)
                    for k in range(CT):
                        last = nc.tensor.transpose(ps_t[g.par][:, k * P:(k + 1) * P], x[:, g.par, k, :], m.ident[:, :])
                    last.then_inc(q["turned"][g.par], 1)
                for g in gs:
                    p = g.par
                    pe.wait_ge(q["ready"][p], g.rnd + 1)
                    for k in range(CT):
                        at = slice(k * P, (k + 1) * P)
                        nc.tensor.matmul(ps_a[p][:, k, :], acc_c[:, p, at], w_self[:, :], start=True, stop=False)
                        nc.tensor.matmul(ps_a[p][:, k, :], hx[:, p, at], w_inter[:, :], start=False, stop=True)
                        last = nc.tensor.matmul(ps_b[p][:, k, :], xt[:, p, at], w_self[:, :], start=True, stop=True)
                    last.then_inc(q["product"][p], 1)

            in_pairs(pe, z.chunks, run)

        @block.scalar
        def _(act):
            def run(gs):
                for g in gs:
                    act.wait_ge(q["product"][g.par], g.rnd + 1)
                    nc.scalar.copy(acc_c[:, g.par, :], cols(m.acc, g.no * CH, CH)).then_inc(q["acc_taken"][g.par], 1)
                for g in gs:
                    norm.scalar(act, g)

            in_pairs(act, z.chunks, run)

        @block.vector
        def _(v):
            for par in range(2):
                v.sem_inc(q["x_read"][par], 1)

            def run(gs):
                steps = [Chain(v, q["step"][g.par], g.rnd * PER, PER) for g in gs]
                for g, step in zip(gs, steps):
                    p = g.par
                    v.wait_ge(q["turned"][p], g.rnd + 1)
                    v.wait_ge(q["product"][p], g.rnd + 1)
                    step(nc.vector.tensor_copy(xt[:, p, :], ps_t[p][:, :]))
                    v.wait_ge(q["acc_taken"][p], g.rnd + 1)
                    step(nc.vector.tensor_tensor(hx[:, p, :], acc_c[:, p, :], xt[:, p, :], ALU.mult))
                    v.sem_inc(q["ready"][p], 1)
                for g, step in zip(gs, steps):
                    p = g.par
                    v.wait_ge(q["product"][p], g.rnd + 2)
                    for k in range(CT):
                        step.go(nc.vector.scalar_tensor_tensor(y[:, p, k, :], ps_a[p][:, k, :], cols(m.scale[:, 2, :], g.no * CT + k, 1), x[:, p, k, :], ALU.mult, ALU.add))
                    step.wait()
                    v.sem_inc(q["x_read"][p], 1)
                    step(nc.vector.tensor_tensor(y[:, p, :, :], y[:, p, :, :], ps_b[p][:, :, :], ALU.add))
                    norm.moments(v, step, g, y)
                for g, step in zip(gs, steps):
                    p = g.par
                    v.wait_ge(q["out_free"][p], g.rnd + 1)
                    norm.apply(v, step, g, y, out)
                    for k in range(CT):
                        step.go(nc.vector.tensor_scalar(tab[:, p, k, :], out[:, p, k, :], cols(m.scale[:, 1, :], g.no * CT + k, 1), None, ALU.mult))
                    step.wait()
                    v.sem_inc(q["out_ready"][p], 1)
                    step.done()

            in_pairs(v, z.chunks, run)


def layer1_nodes(nc, z, m, ins):
    with Phase(nc) as ctx:
        ph = NodePhase(nc, ctx, "n1")
        w_raw, w_t, w2 = ph.sb("w_raw", [D, D]), ph.sb("w_t", [D, D]), ph.sb("w2", [D, D])
        att, bias = ph.sb("att", [D, 2 * HEADS]), ph.sb("bias", [P, D])
        x, tab_in = ph.sb2("x", [P, CT, D]), ph.sb2("tab_in", [P, CT, D])
        acc_s, xt, ht = ph.sb2("acc_s", [D, CH]), ph.sb2("xt", [D, CH]), ph.sb2("ht", [D, CH])
        y, out, tab = ph.sb2("y", [P, CT, D]), ph.sb2("out", [P, CT, D]), ph.sb2("tab", [P, CT, ROW2])
        ps_t, ps_a, ps_h = ph.ps2("ps_t", [D, CH]), ph.ps2("ps_a", [P, CT, D]), ph.ps2("ps_h", [D, CH])
        norm = Norm(nc, ph)
        w_in, att_zero, w_turned, w_copied, storing = (ph.sem(n) for n in ("w_in", "att_zero", "w_turned", "w_copied", "storing"))
        q = {n: ph.sem2(n) for n in ("rows_in", "stored", "out_free", "tab_turned", "acc_ready", "product", "x_read",
                                     "normed", "x2_turned", "x2_copied", "h_done", "ht_copied", "att_done", "table_ready", "step")}
        block = ctx.enter_context(nc.Block())
        PER = 1 + CT + 1 + LN_STEPS + 1 + 3
        att_of = lambda p: ps_h[p][:, 0:CT * 2 * HEADS].rearrange("p (k a) -> p k a", k=CT)

        @block.sync
        def _(sp):
            sp.dma_start(w_raw[:, :], ins["L1_gnn_W"]).then_inc(w_in, 16)
            sp.dma_start(w2[:, :], ins["L2_gnn_W"]).then_inc(w_in, 16)
            sp.dma_start(bias[:, :], ins["L1_gnn_b"].partition_broadcast(P)).then_inc(w_in, 16)
            sp.wait_ge(att_zero, 1)
            for h in range(HEADS):
                for i, name in enumerate(("L2_gnn_att_src", "L2_gnn_att_dst")):
                    sp.dma_start(att[h * HD:(h + 1) * HD, i * HEADS + h:i * HEADS + h + 1],
                                 ins[name][h:h + 1, :].rearrange("o c -> c o"), allow_slow_non_contiguous=True).then_inc(w_in, 16)

            def run(gs):
                for g in gs:
                    sp.wait_ge(q["x_read"][g.par], g.rnd + 1)
                    sp.dma_start(x[:, g.par, :, :], rows(m.x1, g.no)).then_inc(q["rows_in"][g.par], 16)
                    sp.dma_start(tab_in[:, g.par, :, :], rows(m.table1, g.no)).then_inc(q["rows_in"][g.par], 16)

            in_pairs(sp, z.chunks, run)

        @block.gpsimd
        def _(pool):
            for par in range(2):
                pool.sem_inc(q["out_free"][par], 1)

            def run(gs):
                for g in gs:
                    pool.wait_ge(q["table_ready"][g.par], g.rnd + 1)
                    pool.sem_inc(storing, 1)
                    pool.dma_start(rows(m.x2, g.no), out[:, g.par, :, :]).then_inc(q["stored"][g.par], 16)
                    pool.dma_start(rows(m.table2, g.no, ROW2), tab[:, g.par, :, :]).then_inc(q["stored"][g.par], 16)
                for g in gs:
                    pool.wait_ge(q["stored"][g.par], g.rnd * 32 + 32)
                    pool.sem_inc(q["out_free"][g.par], 1)

            in_pairs(pool, z.chunks, run)

        @block.tensor
        def _(pe):
            pe.wait_ge(w_in, 16 * (3 + 2 * HEADS))
            nc.tensor.transpose(ps_t[0][:, 0:D], w_raw[:, :], m.ident[:, :]).then_inc(w_turned, 1)
            pe.wait_ge(w_copied, 1)

            def run(gs):
                for g in gs:
                    pe.wait_ge(q["rows_in"][g.par], g.rnd * 32 + 32)
                    for k in range(CT):
                        last = nc.tensor.transpose(ps_t[g.par][:, k * P:(k + 1) * P], tab_in[:, g.par, k, :], m.ident[:, :])
                    last.then_inc(q["tab_turned"][g.par], 1)
                for g in gs:
                    p = g.par
                    pe.wait_ge(q["acc_ready"][p], g.rnd + 1)
                    for k in range(CT):
                        last = nc.tensor.matmul(ps_a[p][:, k, :], acc_s[:, p, k * P:(k + 1) * P], w_t[:, :], start=True, stop=True)
                    last.then_inc(q["product"][p], 1)
                for g in gs:
                    p = g.par
                    pe.wait_ge(q["normed"][p], g.rnd + 1)
                    for k in range(CT):
                        last = nc.tensor.transpose(ps_t[p][:, k * P:(k + 1) * P], out[:, p, k, :], m.ident[:, :])
                    last.then_inc(q["x2_turned"][p], 1)
                for g in gs:
                    p = g.par
                    pe.wait_ge(q["x2_copied"][p], g.rnd + 1)
                    nc.tensor.matmul(ps_h[p][:, :], w2[:, :], xt[:, p, :], start=True, stop=True).then_inc(q["h_done"][p], 1)
                    for k in range(CT):
                        nc.tensor.matmul(ps_a[p][:, k, :], xt[:, p, k * P:(k + 1) * P], w2[:, :], start=True, stop=True)
                for g in gs:
                    p = g.par
                    pe.wait_ge(q["ht_copied"][p], g.rnd + 1)
                    for k in range(CT):
                        last = nc.tensor.matmul(att_of(p)[:, k, :], ht[:, p, k * P:(k + 1) * P], att[:, :], start=True, stop=True)
                    last.then_inc(q["att_done"][p], 1)

            in_pairs(pe, z.chunks, run)

        @block.scalar
        def _(act):
            def run(gs):
                for g in gs:
                    norm.scalar(act, g)
                for g in gs:
                    act.wait_ge(q["h_done"][g.par], g.rnd + 1)
                    nc.scalar.copy(ht[:, g.par, :], ps_h[g.par][:, :]).then_inc(q["ht_copied"][g.par], 1)

            in_pairs(act, z.chunks, run)

        @block.vector
        def _(v):
            nc.vector.memset(att[:, :], 0.0).then_inc(att_zero, 1)
            for par in range(2):
                v.sem_inc(q["x_read"][par], 1)
            v.wait_ge(w_turned, 1)
            nc.vector.tensor_copy(w_t[:, :], ps_t[0][:, 0:D]).then_inc(w_copied, 1)

            def run(gs):
                steps = [Chain(v, q["step"][g.par], g.rnd * PER, PER) for g in gs]
                for g, step in zip(gs, steps):
                    p = g.par
                    v.wait_ge(q["tab_turned"][p], g.rnd + 1)
                    step(nc.vector.tensor_tensor(acc_s[:, p, :], cols(m.acc, g.no * CH, CH), ps_t[p][:, :], ALU.add))
                    v.sem_inc(q["acc_ready"][p], 1)
                for g, step in zip(gs, steps):
                    p = g.par
                    v.wait_ge(q["product"][p], g.rnd + 1)
                    for k in range(CT):
                        step.go(nc.vector.scalar_tensor_tensor(y[:, p, k, :], ps_a[p][:, k, :], cols(m.scale[:, 1, :], g.no * CT + k, 1), x[:, p, k, :], ALU.mult, ALU.add))
                    step.wait()
                    v.sem_inc(q["x_read"][p], 1)
                    step(nc.vector.tensor_tensor(y[:, p, :, :], y[:, p, :, :], bias[:, :].unsqueeze(1).to_broadcast([P, CT, D]), ALU.add))
                    norm.moments(v, step, g, y)
                for g, step in zip(gs, steps):
                    p = g.par
                    v.wait_ge(q["out_free"][p], g.rnd + 1)
                    norm.apply(v, step, g, y, out)
                    v.sem_inc(q["normed"][p], 1)
                for g, step in zip(gs, steps):
                    p = g.par
                    v.wait_ge(q["x2_turned"][p], g.rnd + 1)
                    step(nc.vector.tensor_copy(xt[:, p, :], ps_t[p][:, :]))
                    v.sem_inc(q["x2_copied"][p], 1)
                for g, step in zip(gs, steps):
                    p = g.par
                    v.wait_ge(q["att_done"][p], g.rnd + 1)
                    step.go(nc.vector.tensor_copy(tab[:, p, :, 0:D], ps_a[p][:, :, :]))
                    step.go(nc.vector.tensor_copy(tab[:, p, :, D:ROW2], att_of(p)[:, :, 0:HEADS]))
                    step(nc.vector.tensor_copy(m.att[:, bass.ds(g.no * CT, CT), :], att_of(p)))
                    v.sem_inc(q["table_ready"][p], 1)
                    step.done()

            in_pairs(v, z.chunks, run)


def lowest_source(nc, z, m):
    with Phase(nc) as ctx:
        part = ctx.enter_context(nc.sbuf_tensor("low_part", [P, 1], F32))
        per_lane, over = ctx.semaphore("low_per_lane"), ctx.semaphore("low_over")
        block = ctx.enter_context(nc.Block())

        @block.vector
        def _(v):
            nc.vector.tensor_reduce(part[:, :], m.att[:, :, 0:HEADS], mybir.AxisListType.XY, ALU.min, negate=True).then_inc(per_lane, 1)
            v.wait_ge(over, 1)

        @block.gpsimd
        def _(pool):
            pool.wait_ge(per_lane, 1)
            nc.gpsimd.partition_all_reduce(m.low[:, :], part[:, :], P, bass.bass_isa.ReduceOp.max).then_inc(over, 1)


def highest_source(nc, z, m):
    GH = G * HEADS
    with Phase(nc) as ctx:
        name = "e2"
        sb = lambda n, shape, dt=F32: ctx.enter_context(nc.sbuf_tensor(f"{name}_{n}", shape, dt))
        rows_, hot, idx = sb("rows", [P, 2, G, ROW2]), sb("hot", [P, 2, G, P]), sb("idx", [P, 2, G], I32)
        a_e, a_t, run_t, run_e = sb("a_e", [P, 2, GH]), sb("a_t", [GH, 2, P]), sb("run_t", [GH, 2, P]), sb("run_e", [P, 2, GH])
        resets = sb("resets", [GH, 2, P])
        ps = ctx.enter_context(nc.psum_tensor(f"{name}_ps", [HEADS, GE], F32))
        ps_a = [ctx.enter_context(nc.psum_tensor(f"{name}_ps_a{i}", [GH, P], F32)) for i in range(2)]
        ps_r = [ctx.enter_context(nc.psum_tensor(f"{name}_ps_r{i}", [P, GH], F32)) for i in range(2)]
        names = ("idx_staged", "rows_in", "resets_in", "stashed", "a_ready", "a_turned", "a_copied", "run_ready",
                 "run_turned", "run_copied", "summed")
        q = {n: [ctx.semaphore(f"{name}_{n}{i}") for i in range(2)] for n in names}
        gather_begun, turning = (ctx.semaphore(f"{name}_{n}") for n in ("gather_begun", "turning"))
        windows = Windows(nc, ctx, m, z, name, [(m.acc, ps, HEADS, ALU.max)], apart=True)
        block = ctx.enter_context(nc.Block())

        @block.gpsimd
        def _(pool):
            def run(f):
                g = f(0)
                pool.wait_ge(q["idx_staged"][g.par], g.rnd + 1)
                pool.wait_ge(q["a_ready"][g.par], g.rnd + 1)
                pool.wait_ge(q["stashed"][g.par], g.rnd * 16 + 16)
                pool.sem_inc(gather_begun, 1)
                gather(nc, pool, m.table2, idx, rows_, g, q["rows_in"])

            pipeline(pool, z.groups, 0, run)

        @block.sync
        def _(sp):
            for par in range(2):
                sp.sem_inc(q["stashed"][par], 16)

            def run(f):
                if a := f(1):
                    sp.wait_ge(q["run_ready"][a.par], a.rnd + 1)
                    sp.dma_start(resets[:, a.par, :], m.resets4[bass.ds(a.no, 1), :].rearrange("o (r e) -> (o r) e", e=P)).then_inc(q["resets_in"][a.par], 16)
                if g := f(0):
                    sp.wait_ge(q["rows_in"][g.par], (g.rnd + 1) * (16 * G))
                    sp.dma_start(m.stash[bass.ds(g.no * P, P), :], rows_[:, g.par, :, :].rearrange("p k f -> p (k f)")).then_inc(q["stashed"][g.par], 16)

            pipeline(sp, z.groups, 1, run)
            for par in range(2):
                sp.wait_ge(q["stashed"][par], 16 * (z.groups // 2 + 1))

        @block.scalar
        def _(act):
            def run(f):
                if a := f(1):
                    act.wait_ge(q["a_ready"][a.par], a.rnd + 1)
                    nc.scalar.copy(idx[:, a.par, :], cols(m.src_idx, a.no * G, G)).then_inc(q["idx_staged"][a.par], 1)
                if g := f(0):
                    act.wait_ge(q["a_turned"][g.par], g.rnd + 1)
                    nc.scalar.copy(a_t[:, g.par, :], ps_a[g.par][:, :]).then_inc(q["a_copied"][g.par], 1)
                    act.wait_ge(q["run_turned"][g.par], g.rnd + 1)
                    nc.scalar.copy(run_e[:, g.par, :], ps_r[g.par][:, :]).then_inc(q["run_copied"][g.par], 1)

            pipeline(act, z.groups, 1, run)

        @block.tensor
        def _(pe):
            reg = pe.alloc_register(f"{name}_pe_base")
            for par in range(2):
                pe.sem_inc(q["summed"][par], 1)

            def run(f):
                a, g = f(1), f(0)
                if a:
                    pe.wait_ge(q["a_ready"][a.par], a.rnd + 2)
                    nc.tensor.transpose(ps_a[a.par][:, :], a_e[:, a.par, :], m.ident[:, :]).then_inc(q["a_turned"][a.par], 1)
                if g:
                    windows.column(pe, g, reg)
                    pe.wait_ge(q["run_copied"][g.par], g.rnd + 1)
                    windows.hot_ready(pe, g)
                    windows.free(pe, g)
                    windows.product(pe, g, reg, [(ps, lambda k: run_e[:, g.par, k * HEADS:(k + 1) * HEADS])], hot)
                    pe.drain().then_inc(q["summed"][g.par], 1)
                if a:
                    pe.wait_ge(q["run_ready"][a.par], a.rnd + 2)
                    pe.sem_inc(turning, 1)
                    nc.tensor.transpose(ps_r[a.par][:, :], run_t[:, a.par, :], m.ident[0:GH, 0:GH]).then_inc(q["run_turned"][a.par], 1)

            pipeline(pe, z.groups, 1, run)

        @block.vector
        def _(v):
            windows.registers(v)
            windows.clear()
            for par in range(2):
                v.sem_inc(q["a_ready"][par], 1)
                v.sem_inc(q["run_ready"][par], 1)

            def run(f):
                if a := f(1):
                    v.wait_ge(q["rows_in"][a.par], (a.rnd + 1) * (16 * G))
                    nc.vector.tensor_scalar(a_e[:, a.par, :].rearrange("p (k h) -> p k h", h=HEADS), rows_[:, a.par, :, D:ROW2],
                                            m.low[:, 0:1], None, ALU.add).then_inc(q["a_ready"][a.par], 1)
                    v.wait_ge(q["summed"][a.par], a.rnd + 1)
                    windows.one_hot(v, a, hot, m.last)
                    v.wait_ge(q["a_copied"][a.par], a.rnd + 1)
                    v.wait_ge(q["resets_in"][a.par], a.rnd * 16 + 16)
                    nc.vector.tensor_tensor_scan(run_t[:, a.par, :], resets[:, a.par, :], a_t[:, a.par, :], 0.0, ALU.add, ALU.max).then_inc(q["run_ready"][a.par], 1)
                if g := f(0):
                    v.wait_ge(q["summed"][g.par], g.rnd + 2)
                    windows.add(v, g)

            pipeline(v, z.groups, 1, run)
            windows.finish(v)


def attention_nodes(nc, z, m):
    NCH, NPT = z.chunks, z.node_tiles
    with Phase(nc) as ctx:
        ph = NodePhase(nc, ctx, "na")
        top_c, top = ph.sb("top_c", [HEADS, CH]), ph.sb("top", [P, NPT, HEADS])
        e_self, t, dn = ph.sb("e_self", [P, NPT, HEADS]), ph.sb("t", [P, NPT, HEADS]), ph.sb("dn", [P, NPT, 2 * HEADS])
        ps = ph.ps("ps", [P, CT, HEADS])
        q = {n: ph.sem(n) for n in ("taken", "turned", "copied", "begun", "step", "e_ready", "exped", "dn_ready", "stored")}
        block = ctx.enter_context(nc.Block())

        @block.scalar
        def _(act):
            with act.Fori(0, NCH) as c:
                act.wait_ge(q["turned"], c + 1)
                nc.scalar.copy(top_c[:, :], m.acc[0:HEADS, bass.ds(c * CH, CH)]).then_inc(q["taken"], 1)
            act.wait_ge(q["e_ready"], 1)
            nc.scalar.activation(m.p_self[:, :, :], e_self[:, :, :], ACT.Exp).then_inc(q["exped"], 1)

        @block.tensor
        def _(pe):
            pe.sem_inc(q["turned"], 1)
            with pe.Fori(0, NCH) as c:
                pe.wait_ge(q["taken"], c + 1)
                pe.wait_ge(q["copied"], c + 1)
                pe.sem_inc(q["begun"], 1)
                for k in range(CT):
                    last = nc.tensor.transpose(ps[:, k, :], top_c[:, k * P:(k + 1) * P], m.ident[0:HEADS, 0:HEADS])
                last.then_inc(q["turned"], 1)

        @block.vector
        def _(v):
            step = Chain(v, q["step"], 0)
            v.sem_inc(q["copied"], 1)
            with v.Fori(0, NCH) as c:
                v.wait_ge(q["turned"], c + 2)
                nc.vector.tensor_copy(top[:, bass.ds(c * CT, CT), :], ps[:, :, :]).then_inc(q["copied"], 1)
            v.wait_ge(q["copied"], NCH + 1)
            a_src, a_dst = m.att[:, :, 0:HEADS], m.att[:, :, HEADS:]
            step(nc.vector.tensor_scalar(top[:, :, :], top[:, :, :], m.low[:, 0:1], None, ALU.subtract))
            step(nc.vector.tensor_tensor(top[:, :, :], top[:, :, :], a_src, ALU.max))
            step(nc.vector.tensor_tensor(top[:, :, :], top[:, :, :], a_dst, ALU.add))
            step(nc.vector.tensor_scalar(t[:, :, :], top[:, :, :], 0.2, None, ALU.mult))
            step(nc.vector.tensor_tensor(dn[:, :, HEADS:], top[:, :, :], t[:, :, :], ALU.max))
            step(nc.vector.tensor_copy(dn[:, :, 0:HEADS], a_dst))
            v.sem_inc(q["dn_ready"], 1)
            step(nc.vector.tensor_tensor(e_self[:, :, :], a_src, a_dst, ALU.add))
            step(nc.vector.tensor_scalar(t[:, :, :], e_self[:, :, :], 0.2, None, ALU.mult))
            step(nc.vector.tensor_tensor(e_self[:, :, :], e_self[:, :, :], t[:, :, :], ALU.max))
            step(nc.vector.tensor_tensor(e_self[:, :, :], e_self[:, :, :], dn[:, :, HEADS:], ALU.subtract))
            v.sem_inc(q["e_ready"], 1)
            v.wait_ge(q["exped"], 1)

        @block.sync
        def _(sp):
            sp.wait_ge(q["dn_ready"], 1)
            sp.dma_start(m.dst_terms[:, :].rearrange("(k p) f -> p k f", p=P), dn[:, :, :], allow_slow_non_contiguous=True).then_inc(q["stored"], 16)
            sp.wait_ge(q["stored"], 16)


def weighted_sum(nc, z, m):
    with Phase(nc) as ctx:
        name = "e3"
        sb = lambda n, shape, dt=F32: ctx.enter_context(nc.sbuf_tensor(f"{name}_{n}", shape, dt))
        rows_, hot, idx = sb("rows", [P, 2, G, ROW2]), sb("hot", [P, 2, G, P]), sb("idx", [P, 2, G], I32)
        terms, e, e2, prob, msg = (sb("terms", [P, 2, G, 2 * HEADS]), sb("e", [P, 2, G, HEADS]), sb("e2", [P, 2, G, HEADS]),
                                   sb("prob", [P, 2, G, HEADS]), sb("msg", [P, 2, G, D]))
        ps = ctx.enter_context(nc.psum_tensor(f"{name}_ps", [P, GE], F32))
        ps_p = ctx.enter_context(nc.psum_tensor(f"{name}_ps_p", [HEADS, GE], F32))
        names = ("idx_staged", "rows_in", "terms_in", "e_ready", "prob_ready", "msg_ready", "summed")
        q = {n: [ctx.semaphore(f"{name}_{n}{i}") for i in range(2)] for n in names}
        gather_begun, small = (ctx.semaphore(f"{name}_{n}") for n in ("gather_begun", "small"))
        windows = Windows(nc, ctx, m, z, name, [(m.acc, ps, P, ALU.add), (m.side, ps_p, HEADS, ALU.add)])
        block = ctx.enter_context(nc.Block())

        @block.gpsimd
        def _(pool):
            def run(f):
                g = f(0)
                pool.wait_ge(q["idx_staged"][g.par], g.rnd + 1)
                pool.wait_ge(q["e_ready"][g.par], g.rnd + 1)
                pool.sem_inc(gather_begun, 1)
                gather(nc, pool, m.dst_terms, idx, terms, g, q["terms_in"])

            pipeline(pool, z.groups, 0, run)

        @block.sync
        def _(sp):
            def run(f):
                g = f(0)
                sp.wait_ge(q["msg_ready"][g.par], g.rnd + 1)
                sp.dma_start(rows_[:, g.par, :, :].rearrange("p k f -> p (k f)"), m.stash[bass.ds(g.no * P, P), :]).then_inc(q["rows_in"][g.par], 16)

            pipeline(sp, z.groups, 0, run)

        @block.scalar
        def _(act):
            def run(f):
                if a := f(1):
                    act.wait_ge(q["e_ready"][a.par], a.rnd + 1)
                    nc.scalar.copy(idx[:, a.par, :], cols(m.dst_idx, a.no * G, G)).then_inc(q["idx_staged"][a.par], 1)
                if g := f(0):
                    act.wait_ge(q["e_ready"][g.par], g.rnd + 2)
                    nc.scalar.activation(prob[:, g.par, :, :], e[:, g.par, :, :], ACT.Exp).then_inc(q["prob_ready"][g.par], 1)

            pipeline(act, z.groups, 1, run)

        @block.tensor
        def _(pe):
            reg = pe.alloc_register(f"{name}_pe_base")
            for par in range(2):
                pe.sem_inc(q["summed"][par], 1)

            def run(f):
                g = f(0)
                windows.column(pe, g, reg)
                pe.wait_ge(q["msg_ready"][g.par], g.rnd + 2)
                windows.free(pe, g)
                windows.product(pe, g, reg, [(ps, lambda k: msg[:, g.par, k, :]), (ps_p, lambda k: prob[:, g.par, k, :])], hot)
                pe.drain().then_inc(q["summed"][g.par], 1)

            pipeline(pe, z.groups, 0, run)

        @block.vector
        def _(v):
            windows.registers(v)
            windows.clear()
            for par in range(2):
                v.sem_inc(q["e_ready"][par], 1)
                v.sem_inc(q["msg_ready"][par], 1)

            def messages(a):
                par = a.par
                step = Chain(v, small, a.no * 3, 3)
                v.wait_ge(q["summed"][par], a.rnd + 1)
                windows.one_hot(v, a, hot, m.loc)
                v.wait_ge(q["rows_in"][par], a.rnd * 16 + 16)
                v.wait_ge(q["terms_in"][par], (a.rnd + 1) * (16 * G))
                step(nc.vector.tensor_tensor(e2[:, par, :, :], rows_[:, par, :, D:ROW2], terms[:, par, :, 0:HEADS], ALU.add))
                step(nc.vector.tensor_scalar(e[:, par, :, :], e2[:, par, :, :], 0.2, None, ALU.mult))
                step(nc.vector.tensor_tensor(e2[:, par, :, :], e[:, par, :, :], e2[:, par, :, :], ALU.max))
                nc.vector.tensor_tensor(e[:, par, :, :], e2[:, par, :, :], terms[:, par, :, HEADS:], ALU.subtract).then_inc(q["e_ready"][par], 1)
                step.done()

            def weigh(a):
                par = a.par
                v.wait_ge(q["prob_ready"][par], a.rnd + 1)
                nc.vector.tensor_tensor(msg[:, par, :, :].rearrange("p k (h c) -> p k h c", h=HEADS), rows_[:, par, :, 0:D].rearrange("p k (h c) -> p k h c", h=HEADS),
                                        prob[:, par, :, :].unsqueeze(3).to_broadcast([P, G, HEADS, HD]), ALU.mult).then_inc(q["msg_ready"][par], 1)

            def run(f):
                if a := f(1):
                    messages(a)
                    weigh(a)
                if g := f(0):
                    v.wait_ge(q["summed"][g.par], g.rnd + 2)
                    windows.add(v, g)

            pipeline(v, z.groups, 1, run)
            windows.finish(v)


def layer2_nodes(nc, z, m, ins):
    with Phase(nc) as ctx:
        ph = NodePhase(nc, ctx, "n2")
        bias, lin1, conv1, sa, w_sa, b0 = (ph.sb("bias", [P, D]), ph.sb("lin1", [D, D]), ph.sb("conv1", [D, D]),
                                           ph.sb("sa", [2, 1]), ph.sb("w_sa", [2, D]), ph.sb("b0", [D, 1]))
        b_lin = ph.sb("b_lin", [D, 1])
        x, tab_in, acc_c, s_c = ph.sb2("x", [P, CT, D]), ph.sb2("tab_in", [P, CT, ROW2]), ph.sb2("acc_c", [D, CH]), ph.sb2("s_c", [HEADS, CH])
        den, y, out, xt, ht, tab = (ph.sb2("den", [P, CT, HEADS]), ph.sb2("y", [P, CT, D]), ph.sb2("out", [P, CT, D]),
                                    ph.sb2("xt", [D, CH]), ph.sb2("ht", [D, CH]), ph.sb2("tab", [P, CT, D]))
        ps_n, ps_t, ps_h = ph.ps2("ps_n", [P, CT, D]), ph.ps2("ps_t", [D, CH]), ph.ps2("ps_h", [D, CH])
        norm = Norm(nc, ph)
        w_in, b_done, b_ready, storing = (ph.sem(n) for n in ("w_in", "b_done", "b_ready", "storing"))
        q = {n: ph.sem2(n) for n in ("rows_in", "stored", "out_free", "taken", "turned", "x_read", "normed", "x3_turned", "x3_copied",
                                     "h_done", "h_copied", "h_kept", "xm_done", "xm_taken", "table_ready", "step")}
        block = ctx.enter_context(nc.Block())
        PER = 8 + LN_STEPS + 2
        heads = lambda a: a.rearrange("p k (h c) -> p k h c", h=HEADS)
        sums_of = lambda p: ps_t[p][:, 0:CT * HEADS].rearrange("p (k h) -> p k h", k=CT)

        @block.sync
        def _(sp):
            for dst, src in ((bias[:, :], ins["L2_gnn_bias"].partition_broadcast(P)), (lin1[:, :], ins["L3_gnn_lin1_w"][0, 2:2 + D, :]),
                             (w_sa[:, :], ins["L3_gnn_lin1_w"][0, 0:2, :]), (conv1[:, :], ins["L3_gnn_conv1_w"][0]),
                             (sa[:, :], ins["L3_gnn_state_attr"][0:1, :].rearrange("o s -> s o")),
                             (b_lin[:, :], ins["L3_gnn_lin1_b"][0:1, :].rearrange("o d -> d o"))):
                sp.dma_start(dst, src, allow_slow_non_contiguous=True).then_inc(w_in, 16)

            def run(gs):
                for g in gs:
                    sp.wait_ge(q["x_read"][g.par], g.rnd + 1)
                    sp.dma_start(x[:, g.par, :, :], rows(m.x2, g.no)).then_inc(q["rows_in"][g.par], 16)
                    sp.dma_start(tab_in[:, g.par, :, :], rows(m.table2, g.no, ROW2)).then_inc(q["rows_in"][g.par], 16)

            in_pairs(sp, z.chunks, run)

        @block.gpsimd
        def _(pool):
            for par in range(2):
                pool.sem_inc(q["out_free"][par], 1)

            def run(gs):
                for g in gs:
                    pool.wait_ge(q["table_ready"][g.par], g.rnd + 1)
                    pool.sem_inc(storing, 1)
                    pool.dma_start(rows(m.x3, g.no), out[:, g.par, :, :]).then_inc(q["stored"][g.par], 16)
                    pool.dma_start(rows(m.table3, g.no), tab[:, g.par, :, :]).then_inc(q["stored"][g.par], 16)
                for g in gs:
                    pool.wait_ge(q["stored"][g.par], g.rnd * 32 + 32)
                    pool.sem_inc(q["out_free"][g.par], 1)

            in_pairs(pool, z.chunks, run)

        @block.tensor
        def _(pe):
            for par in range(2):
                pe.sem_inc(q["turned"][par], 1)
                pe.sem_inc(q["xm_taken"][par], 1)
            pe.wait_ge(w_in, 16 * 6)
            nc.tensor.matmul(ps_h[0][:, 0:1], w_sa[:, :], sa[:, :], start=True, stop=True).then_inc(b_done, 1)
            pe.wait_ge(b_ready, 1)

            def run(gs):
                for g in gs:
                    p = g.par
                    pe.wait_ge(q["taken"][p], g.rnd + 1)
                    pe.wait_ge(q["xm_taken"][p], g.rnd + 1)
                    for k in range(CT):
                        at = slice(k * P, (k + 1) * P)
                        nc.tensor.transpose(ps_n[p][:, k, :], acc_c[:, p, at], m.ident[:, :])
                        last = nc.tensor.transpose(sums_of(p)[:, k, :], s_c[:, p, at], m.ident[0:HEADS, 0:HEADS])
                    last.then_inc(q["turned"][p], 1)
                for g in gs:
                    p = g.par
                    pe.wait_ge(q["normed"][p], g.rnd + 1)
                    for k in range(CT):
                        last = nc.tensor.transpose(ps_t[p][:, k * P:(k + 1) * P], out[:, p, k, :], m.ident[:, :])
                    last.then_inc(q["x3_turned"][p], 1)
                for g in gs:
                    p = g.par
                    pe.wait_ge(q["x3_copied"][p], g.rnd + 1)
                    pe.wait_ge(q["h_kept"][p], g.rnd + 1)
                    nc.tensor.matmul(ps_h[p][:, :], lin1[:, :], xt[:, p, :], start=True, stop=True).then_inc(q["h_done"][p], 1)
                for g in gs:
                    p = g.par
                    pe.wait_ge(q["h_copied"][p], g.rnd + 1)
                    for k in range(CT):
                        last = nc.tensor.matmul(ps_n[p][:, k, :], ht[:, p, k * P:(k + 1) * P], conv1[:, :], start=True, stop=True)
                    last.then_inc(q["xm_done"][p], 1)

            in_pairs(pe, z.chunks, run)

        @block.scalar
        def _(act):
            for par in range(2):
                act.sem_inc(q["h_kept"][par], 1)
            act.wait_ge(b_ready, 1)

            def run(gs):
                for g in gs:
                    p = g.par
                    act.wait_ge(q["turned"][p], g.rnd + 1)
                    nc.scalar.copy(acc_c[:, p, :], cols(m.acc, g.no * CH, CH))
                    nc.scalar.copy(s_c[:, p, :], m.side[0:HEADS, bass.ds(g.no * CH, CH)]).then_inc(q["taken"][p], 1)
                for g in gs:
                    norm.scalar(act, g)
                for g in gs:
                    p = g.par
                    act.wait_ge(q["h_done"][p], g.rnd + 1)
                    nc.scalar.activation(ht[:, p, :], ps_h[p][:, :], ACT.Identity, bias=b0[:, 0:1]).then_inc(q["h_copied"][p], 1)
                    nc.scalar.activation(cols(m.hidden, g.no * CH, CH), ps_h[p][:, :], ACT.Identity, bias=b0[:, 0:1]).then_inc(q["h_kept"][p], 1)

            in_pairs(act, z.chunks, run)

        @block.vector
        def _(v):
            for par in range(2):
                v.sem_inc(q["x_read"][par], 1)
            v.wait_ge(b_done, 1)
            nc.vector.tensor_tensor(b0[:, :], ps_h[0][:, 0:1], b_lin[:, :], ALU.add).then_inc(b_ready, 1)

            def run(gs):
                steps = [Chain(v, q["step"][g.par], g.rnd * PER, PER) for g in gs]
                for g, step in zip(gs, steps):
                    p = g.par
                    p_self = m.p_self[:, bass.ds(g.no * CT, CT), :]
                    yp, dp = y[:, p, :, :], den[:, p, :, :]
                    v.wait_ge(q["rows_in"][p], g.rnd * 32 + 32)
                    v.wait_ge(q["turned"][p], g.rnd + 2)
                    step(nc.vector.tensor_tensor(dp, sums_of(p), p_self, ALU.add))
                    step(nc.vector.tensor_scalar(dp, dp, 1e-16, None, ALU.add))
                    step.go(nc.vector.reciprocal(dp, dp))
                    step(nc.vector.tensor_tensor(heads(yp), heads(tab_in[:, p, :, 0:D]), p_self.unsqueeze(3).to_broadcast([P, CT, HEADS, HD]), ALU.mult))
                    step(nc.vector.tensor_tensor(yp, yp, ps_n[p][:, :, :], ALU.add))
                    step(nc.vector.tensor_tensor(heads(yp), heads(yp), dp.unsqueeze(3).to_broadcast([P, CT, HEADS, HD]), ALU.mult))
                    step(nc.vector.tensor_tensor(yp, yp, bias[:, :].unsqueeze(1).to_broadcast([P, CT, D]), ALU.add))
                    step(nc.vector.tensor_tensor(yp, yp, x[:, p, :, :], ALU.add))
                    v.sem_inc(q["x_read"][p], 1)
                    norm.moments(v, step, g, y)
                for g, step in zip(gs, steps):
                    p = g.par
                    v.wait_ge(q["out_free"][p], g.rnd + 1)
                    norm.apply(v, step, g, y, out)
                    v.sem_inc(q["normed"][p], 1)
                for g, step in zip(gs, steps):
                    p = g.par
                    v.wait_ge(q["x3_turned"][p], g.rnd + 1)
                    step(nc.vector.tensor_copy(xt[:, p, :], ps_t[p][:, :]))
                    v.sem_inc(q["x3_copied"][p], 1)
                for g, step in zip(gs, steps):
                    p = g.par
                    v.wait_ge(q["xm_done"][p], g.rnd + 1)
                    step(nc.vector.tensor_copy(tab[:, p, :, :], ps_n[p][:, :, :]))
                    v.sem_inc(q["xm_taken"][p], 1)
                    v.sem_inc(q["table_ready"][p], 1)
                    step.done()

            in_pairs(v, z.chunks, run)


def cutoffs(nc, z, m):
    NT = z.tiles
    with Phase(nc) as ctx:
        u, k = (ctx.enter_context(nc.sbuf_tensor(n, [P, NT], F32)) for n in ("cut_u", "cut_k"))
        half_pi = ctx.enter_context(nc.sbuf_tensor("half_pi", [P, 1], F32))
        step_s, r_ready, absed, sined = (ctx.semaphore(n) for n in ("cut_step", "cut_r", "cut_abs", "cut_sin"))
        block = ctx.enter_context(nc.Block())
        ROUND = 12582912.0
        two_pi_hi = float(np.float32(6.28125))
        two_pi_lo = float(2 * np.pi - 6.28125)

        @block.vector
        def _(v):
            step = Chain(v, step_s, 0)
            step(nc.vector.memset(half_pi[:, :], PI / 2))
            step(nc.vector.tensor_scalar(u[:, :], m.w[:, :], float(np.float32(PI / 10.0)), None, ALU.mult))
            step(nc.vector.tensor_scalar(k[:, :], u[:, :], 1.0 / (2 * PI), ROUND, ALU.mult, ALU.add))
            step(nc.vector.tensor_scalar(k[:, :], k[:, :], -ROUND, None, ALU.add))
            step(nc.vector.scalar_tensor_tensor(u[:, :], k[:, :], -two_pi_hi, u[:, :], ALU.mult, ALU.add))
            step(nc.vector.scalar_tensor_tensor(u[:, :], k[:, :], -two_pi_lo, u[:, :], ALU.mult, ALU.add))
            v.sem_inc(r_ready, 1)
            v.wait_ge(absed, 1)
            step(nc.vector.tensor_scalar(k[:, :], k[:, :], PI, None, ALU.min))
            v.sem_inc(r_ready, 1)
            v.wait_ge(sined, 1)
            step(nc.vector.tensor_scalar(m.w[:, :], u[:, :], 1.0, 0.5, ALU.add, ALU.mult))

        @block.scalar
        def _(act):
            act.wait_ge(r_ready, 1)
            nc.scalar.activation(k[:, :], u[:, :], ACT.Abs).then_inc(absed, 1)
            act.wait_ge(r_ready, 2)
            nc.scalar.activation(u[:, :], k[:, :], ACT.Sin, bias=half_pi[:, 0:1], scale=-1.0).then_inc(sined, 1)


LOG_SET = "natural_log_exp_and_others"


class Ssp:

    def __init__(self, nc, ph):
        self.nc = nc
        self.pos, self.neg, self.log = ph.sb("ssp_pos", [P, 2, CH]), ph.sb("ssp_neg", [P, 2, CH]), ph.sb("ssp_log", [P, 2, CH])

    def vector(self, out, par):
        return self.nc.vector.scalar_tensor_tensor(out, self.pos[:, par, :], -LN2, self.log[:, par, :], ALU.add, ALU.add)


def continuous_conv(nc, z, m, ins, layer):
    NG, K = z.groups, z.gauss
    name = f"c{layer}"
    with Phase(nc) as ctx:
        ph = NodePhase(nc, ctx, name)
        w1, w2, b1, b2 = ph.sb("w1", [K, D]), ph.sb("w2", [D, D]), ph.sb("b1", [D, 1]), ph.sb("b2", [P, D])
        rows_, hot, idx = ph.sb("rows", [P, 2, G, D]), ph.sb("hot", [P, 2, G, P]), ph.sb("idx", [P, 2, G], I32)
        attr, attr_t = ph.sb("attr", [P, 2, G, K]), ph.sb("attr_t", [K, GE])
        act_t, filt, msg = ph.sb("act_t", [D, 2, GE]), ph.sb("filt", [P, 2, CT, D]), ph.sb("msg", [P, 2, G, D])
        ssp = Ssp(nc, ph)
        ps_t = [ph.ps(f"ps_t{i}", [K, CH]) for i in range(2)]
        ps_1 = [ph.ps(f"ps_1{i}", [D, CH]) for i in range(2)]
        ps_2 = [ph.ps(f"ps_2{i}", [P, CT, D]) for i in range(2)]
        ps = ph.ps("ps", [P, GE])
        pair = {n: [ph.sem(f"{n}{i}") for i in range(2)] for n in (
            "idx_staged", "rows_in", "attr_in", "attr_read", "msg_ready", "summed")}
        half = {n: [ph.sem(f"{n}{i}") for i in range(2)] for n in (
            "turned", "turned_copied", "first_done", "first_read", "exp_done", "ssp_ready", "ssp_used", "filter_done", "filter_read", "msg_half")}
        one = {n: ph.sem(n) for n in ("w_in", "gather_begun", "turning", "attr_part")}
        windows = Windows(nc, ctx, m, z, name, [(m.acc, ps, P, ALU.add)])
        block = ctx.enter_context(nc.Block())

        def last_attr_dmas(g):
            left = max(0, min(GE, z.edges - g * GE))
            full, rest = left // G, left % G
            return ([(0, full, G)] if full else []) + ([(full, 1, rest)] if rest else [])

        @block.sync
        def _(sp):
            for dst, src in ((w1[:, :], ins["L3_gnn_mlp1_w"][layer]), (w2[:, :], ins["L3_gnn_mlp2_w"][layer]),
                             (b1[:, :], ins["L3_gnn_mlp1_b"][layer:layer + 1, :].rearrange("o d -> d o")),
                             (b2[:, :], ins["L3_gnn_mlp2_b"][layer].partition_broadcast(P))):
                sp.dma_start(dst, src, allow_slow_non_contiguous=True).then_inc(one["w_in"], 16)
            flat = lambda a: a.rearrange("p j f -> p (j f)")

            def load(f):
                g = f(0)
                sp.wait_ge(pair["attr_read"][g.par], g.rnd + 1)
                sp.dma_start(flat(attr[:, g.par, :, :]),
                             ins["edge_attr_50"][bass.ds(g.no * GE, GE), :].rearrange("(p j) f -> p (j f)", j=G)).then_inc(pair["attr_in"][g.par], 16)

            whole = (NG - 2) // 2 * 2
            pipeline(sp, whole, 0, load)
            attr_parts = 0
            for g in range(whole, NG):
                par = g % 2
                sp.wait_ge(pair["attr_read"][par], g // 2 + 1)
                parts = last_attr_dmas(g)
                for i, (p0, n, j) in enumerate(parts):
                    at = g * GE + p0 * G
                    load_part = sp.dma_start(flat(attr[p0:p0 + n, par, 0:j, :]),
                                             ins["edge_attr_50"][at:at + n * j, :].rearrange("(p j) f -> p (j f)", j=j))
                    if i < len(parts) - 1:
                        load_part.then_inc(one["attr_part"], 16)
                        attr_parts += 1
                        sp.wait_ge(one["attr_part"], 16 * attr_parts)
                    else:
                        load_part.then_inc(pair["attr_in"][par], 16)
                if not parts:
                    sp.sem_inc(pair["attr_in"][par], 16)

        @block.gpsimd
        def _(pool):
            def run(f):
                g = f(0)
                pool.wait_ge(pair["idx_staged"][g.par], g.rnd + 1)
                pool.wait_ge(pair["msg_ready"][g.par], g.rnd + 1)
                pool.sem_inc(one["gather_begun"], 1)
                gather(nc, pool, m.table3, idx, rows_, g, pair["rows_in"])

            pipeline(pool, NG, 0, run)

        @block.tensor
        def _(pe):
            reg = pe.alloc_register(f"{name}_pe_base")
            for par in range(2):
                pe.sem_inc(pair["attr_read"][par], 1)
                pe.sem_inc(pair["summed"][par], 1)
            pe.wait_ge(one["w_in"], 64)

            def run(f):
                if u := f(2):
                    for h in range(2):
                        pe.wait_ge(half["turned_copied"][0], u.no + 2)
                        pe.wait_ge(half["turned_copied"][1], u.no + 2)
                        pe.wait_ge(half["first_read"][h], u.no + 1)
                        nc.tensor.matmul(ps_1[h][:, :], w1[:, :], attr_t[:, h * CH:(h + 1) * CH], start=True, stop=True).then_inc(half["first_done"][h], 1)
                if a := f(1):
                    for h in range(2):
                        pe.wait_ge(half["ssp_used"][h], a.no + 2)
                        pe.wait_ge(half["filter_read"][h], a.no + 1)
                        for k in range(CT):
                            at = h * CH + k * P
                            last = nc.tensor.matmul(ps_2[h][:, k, :], act_t[:, a.par, at:at + P], w2[:, :], start=True, stop=True)
                        last.then_inc(half["filter_done"][h], 1)
                if t := f(3):
                    pe.wait_ge(pair["attr_in"][t.par], t.rnd * 16 + 16)
                    for h in range(2):
                        pe.wait_ge(half["turned_copied"][h], t.no + 1)
                        pe.sem_inc(one["turning"], 1)
                        for j in range(CT):
                            last = nc.tensor.transpose(ps_t[h][:, j * P:(j + 1) * P], attr[:, t.par, h * CT + j, :], m.ident[:, :])
                        last.then_inc(half["turned"][h], 1)
                if g := f(0):
                    windows.column(pe, g, reg)
                    pe.wait_ge(pair["msg_ready"][g.par], g.rnd + 2)
                    windows.free(pe, g)
                    windows.product(pe, g, reg, [(ps, lambda k: msg[:, g.par, k, :])], hot)
                    pe.drain().then_inc(pair["summed"][g.par], 1)
                if t:
                    pe.wait_ge(half["turned"][1], t.no + 1)
                    pe.sem_inc(pair["attr_read"][t.par], 1)

            pipeline(pe, NG, 3, run)

        @block.scalar
        def _(act):
            act.preload_act_table_set(LOG_SET)
            for h in range(2):
                act.sem_inc(half["turned_copied"][h], 1)
                act.sem_inc(half["first_read"][h], 1)
            act.wait_ge(one["w_in"], 64)

            def run(f):
                if u := f(2):
                    act.wait_ge(pair["msg_ready"][u.par], u.rnd + 1)
                    nc.scalar.copy(idx[:, u.par, :], cols(m.src_idx, u.no * G, G)).then_inc(pair["idx_staged"][u.par], 1)
                    for h in range(2):
                        act.wait_ge(half["first_done"][h], u.no + 1)
                        act.wait_ge(half["ssp_used"][h], u.no + 1)
                        nc.scalar.activation(ssp.pos[:, h, :], ps_1[h][:, :], ACT.Relu, bias=b1[:, 0:1])
                        nc.scalar.activation(ssp.neg[:, h, :], ps_1[h][:, :], ACT.Abs, bias=b1[:, 0:1]).then_inc(half["first_read"][h], 1)
                    for h in range(2):
                        act.wait_ge(half["first_read"][h], u.no + 2)
                        nc.scalar.activation(ssp.log[:, h, :], ssp.neg[:, h, :], ACT.Exp, scale=-1.0).then_inc(half["exp_done"][h], 1)
                    for h in range(2):
                        act.wait_ge(half["exp_done"][h], u.no + 1)
                        nc.scalar.activation(ssp.log[:, h, :], ssp.log[:, h, :], ACT.Ln, bias=1.0).then_inc(half["ssp_ready"][h], 1)
                if t := f(3):
                    for h in range(2):
                        act.wait_ge(half["turned"][h], t.no + 1)
                        out = attr_t[:, :].rearrange("f (p j) -> f j p", j=G)[:, h * CT:(h + 1) * CT, :]
                        nc.scalar.copy(out, ps_t[h][:, :].rearrange("f (j p) -> f j p", j=CT)).then_inc(half["turned_copied"][h], 1)

            pipeline(act, NG, 3, run)

        @block.vector
        def _(v):
            windows.registers(v)
            windows.clear()
            for h in range(2):
                v.sem_inc(half["filter_read"][h], 1)
                v.sem_inc(half["ssp_used"][h], 1)
                v.sem_inc(half["msg_half"][h], 1)
                v.sem_inc(pair["msg_ready"][h], 1)
            v.wait_ge(one["w_in"], 64)

            def run(f):
                if a := f(1):
                    v.wait_ge(pair["summed"][a.par], a.rnd + 1)
                    windows.one_hot(v, a, hot, m.loc, m.w)
                    v.wait_ge(pair["rows_in"][a.par], (a.rnd + 1) * (16 * G))
                    for h in range(2):
                        v.wait_ge(half["filter_done"][h], a.no + 1)
                        v.wait_ge(half["msg_half"][h], a.no + 1)
                        nc.vector.tensor_tensor(filt[:, h, :, :], ps_2[h][:, :, :], b2[:, :].unsqueeze(1).to_broadcast([P, CT, D]), ALU.add).then_inc(half["filter_read"][h], 1)
                    for h in range(2):
                        v.wait_ge(half["filter_read"][h], a.no + 2)
                        nc.vector.tensor_tensor(msg[:, a.par, h * CT:(h + 1) * CT, :], filt[:, h, :, :], rows_[:, a.par, h * CT:(h + 1) * CT, :], ALU.mult).then_inc(half["msg_half"][h], 1)
                    for h in range(2):
                        v.wait_ge(half["msg_half"][h], a.no + 2)
                    v.sem_inc(pair["msg_ready"][a.par], 1)
                if u := f(2):
                    for h in range(2):
                        v.wait_ge(half["ssp_ready"][h], u.no + 1)
                        ssp.vector(act_t[:, u.par, h * CH:(h + 1) * CH], h).then_inc(half["ssp_used"][h], 1)
                if g := f(0):
                    v.wait_ge(pair["summed"][g.par], g.rnd + 2)
                    windows.add(v, g)

            pipeline(v, NG, 3, run)
            windows.finish(v)


def conv_nodes(nc, z, m, ins, layer):
    NCH = z.chunks
    real = z.nodes - (NCH - 1) * CH
    with Phase(nc) as ctx:
        ph = NodePhase(nc, ctx, f"u{layer}")
        conv2, blin, b2, bb = ph.sb("conv2", [D, D]), ph.sb("blin", [D, D]), ph.sb("b2", [D, 1]), ph.sb("bb", [D, 1])
        act_c = ph.sb2("act_c", [D, CH])
        ssp = Ssp(nc, ph)
        ps_1, ps_2 = ph.ps2("ps_1", [D, CH]), ph.ps2("ps_2", [D, CH])
        w_in, summed = ph.sem("w_in"), ph.sem("summed")
        q = {n: ph.sem2(n) for n in ("first_done", "first_read", "exp_done", "ssp_ready", "act_ready", "second_done", "updated")}
        block = ctx.enter_context(nc.Block())

        @block.sync
        def _(sp):
            for dst, src in ((conv2[:, :], ins["L3_gnn_conv2_w"][layer]), (blin[:, :], ins["L3_gnn_blin_w"][layer]),
                             (b2[:, :], ins["L3_gnn_conv2_b"][layer:layer + 1, :].rearrange("o d -> d o")),
                             (bb[:, :], ins["L3_gnn_blin_b"][layer:layer + 1, :].rearrange("o d -> d o"))):
                sp.dma_start(dst, src, allow_slow_non_contiguous=True).then_inc(w_in, 16)

        @block.tensor
        def _(pe):
            pe.wait_ge(w_in, 64)

            def run(gs):
                for g in gs:
                    pe.wait_ge(q["first_read"][g.par], g.rnd + 1)
                    nc.tensor.matmul(ps_1[g.par][:, :], conv2[:, :], cols(m.acc, g.no * CH, CH), start=True, stop=True).then_inc(q["first_done"][g.par], 1)
                for g in gs:
                    pe.wait_ge(q["act_ready"][g.par], g.rnd + 1)
                    pe.wait_ge(q["updated"][g.par], g.rnd + 1)
                    nc.tensor.matmul(ps_2[g.par][:, :], blin[:, :], act_c[:, g.par, :], start=True, stop=True).then_inc(q["second_done"][g.par], 1)

            in_pairs(pe, NCH, run)

        @block.scalar
        def _(act):
            act.preload_act_table_set(LOG_SET)
            act.wait_ge(w_in, 64)
            for par in range(2):
                act.sem_inc(q["first_read"][par], 1)

            def run(gs):
                for g in gs:
                    p = g.par
                    act.wait_ge(q["first_done"][p], g.rnd + 1)
                    act.wait_ge(q["updated"][p], g.rnd + 1)
                    nc.scalar.activation(ssp.pos[:, p, :], ps_1[p][:, :], ACT.Relu, bias=b2[:, 0:1])
                    nc.scalar.activation(ssp.neg[:, p, :], ps_1[p][:, :], ACT.Abs, bias=b2[:, 0:1]).then_inc(q["first_read"][p], 1)
                for g in gs:
                    act.wait_ge(q["first_read"][g.par], g.rnd + 2)
                    nc.scalar.activation(ssp.log[:, g.par, :], ssp.neg[:, g.par, :], ACT.Exp, scale=-1.0).then_inc(q["exp_done"][g.par], 1)
                for g in gs:
                    act.wait_ge(q["exp_done"][g.par], g.rnd + 1)
                    nc.scalar.activation(ssp.log[:, g.par, :], ssp.log[:, g.par, :], ACT.Ln, bias=1.0).then_inc(q["ssp_ready"][g.par], 1)

            in_pairs(act, NCH, run)

        @block.vector
        def _(v):
            for par in range(2):
                v.sem_inc(q["updated"][par], 1)
            v.wait_ge(w_in, 64)

            def run(gs):
                for g in gs:
                    v.wait_ge(q["ssp_ready"][g.par], g.rnd + 1)
                    ssp.vector(act_c[:, g.par, :], g.par).then_inc(q["act_ready"][g.par], 1)
                for g in gs:
                    v.wait_ge(q["second_done"][g.par], g.rnd + 1)
                    h = cols(m.hidden, g.no * CH, CH)
                    nc.vector.scalar_tensor_tensor(h, ps_2[g.par][:, :], bb[:, 0:1], h, ALU.add, ALU.add).then_inc(q["updated"][g.par], 1)

            in_pairs(v, NCH, run)
            for par in range(2):
                v.wait_ge(q["updated"][par], rounds(NCH, par) + 1)
            parts = [(0, NCH - 1, CH)] if NCH > 1 else []
            parts.append((NCH - 1, 1, real))
            for c, n, width in parts:
                chunk = m.hidden[:, c * CH:c * CH + n * width].rearrange("p (c i) -> p c i", c=n)
                nc.vector.tensor_reduce(m.sums[:, c:c + n], chunk, AX, ALU.add).then_inc(summed, 1)
            v.wait_ge(summed, len(parts))


def next_messages(nc, z, m, ins):
    NCH = z.chunks
    with Phase(nc) as ctx:
        ph = NodePhase(nc, ctx, "nm")
        lin1, conv1, w_a, w_b, b_lin, b1 = (ph.sb("lin1", [D, D]), ph.sb("conv1", [D, D]), ph.sb("w_a", [D, 1]),
                                            ph.sb("w_b", [D, 1]), ph.sb("b_lin", [D, 1]), ph.sb("b1", [D, 1]))
        part, total, ht, tab = ph.sb("part", [P, 1]), ph.sb("total", [P, 1]), ph.sb2("ht", [D, CH]), ph.sb2("tab", [P, CT, D])
        ps_h, ps_x = ph.ps2("ps_h", [D, CH]), ph.ps2("ps_x", [P, CT, D])
        one = {n: ph.sem(n) for n in ("w_in", "part_ready", "totalled", "step", "b_ready")}
        q = {n: ph.sem2(n) for n in ("h_done", "h_copied", "h_kept", "xm_done", "table_ready", "stored")}
        block = ctx.enter_context(nc.Block())

        @block.sync
        def _(sp):
            for par in range(2):
                sp.sem_inc(q["stored"][par], 16)
            w = ins["L3_gnn_lin1_w"]
            for dst, src in ((lin1[:, :], w[1, 2:2 + D, :]), (conv1[:, :], ins["L3_gnn_conv1_w"][1]),
                             (w_a[:, :], w[1, 0:1, :].rearrange("o d -> d o")), (w_b[:, :], w[1, 1:2, :].rearrange("o d -> d o")),
                             (b_lin[:, :], ins["L3_gnn_lin1_b"][1:2, :].rearrange("o d -> d o"))):
                sp.dma_start(dst, src, allow_slow_non_contiguous=True).then_inc(one["w_in"], 16)

            def run(gs):
                for g in gs:
                    sp.wait_ge(q["table_ready"][g.par], g.rnd + 2)
                    sp.dma_start(rows(m.table3, g.no), tab[:, g.par, :, :]).then_inc(q["stored"][g.par], 16)

            in_pairs(sp, NCH, run)
            for par in range(2):
                sp.wait_ge(q["stored"][par], 16 * (rounds(NCH, par) + 1))

        @block.gpsimd
        def _(pool):
            pool.wait_ge(one["part_ready"], 1)
            nc.gpsimd.partition_all_reduce(total[:, :], part[:, :], P, bass.bass_isa.ReduceOp.add).then_inc(one["totalled"], 1)

        @block.tensor
        def _(pe):
            pe.wait_ge(one["w_in"], 80)

            def run(gs):
                for g in gs:
                    pe.wait_ge(q["h_kept"][g.par], g.rnd + 1)
                    nc.tensor.matmul(ps_h[g.par][:, :], lin1[:, :], cols(m.hidden, g.no * CH, CH), start=True, stop=True).then_inc(q["h_done"][g.par], 1)
                for g in gs:
                    p = g.par
                    pe.wait_ge(q["h_copied"][p], g.rnd + 1)
                    pe.wait_ge(q["table_ready"][p], g.rnd + 1)
                    for k in range(CT):
                        last = nc.tensor.matmul(ps_x[p][:, k, :], ht[:, p, k * P:(k + 1) * P], conv1[:, :], start=True, stop=True)
                    last.then_inc(q["xm_done"][p], 1)

            in_pairs(pe, NCH, run)

        @block.scalar
        def _(act):
            for par in range(2):
                act.sem_inc(q["h_kept"][par], 1)
            act.wait_ge(one["b_ready"], 1)

            def run(gs):
                for g in gs:
                    p = g.par
                    act.wait_ge(q["h_done"][p], g.rnd + 1)
                    act.wait_ge(q["xm_done"][p], g.rnd + 1)
                    nc.scalar.activation(ht[:, p, :], ps_h[p][:, :], ACT.Identity, bias=b1[:, 0:1]).then_inc(q["h_copied"][p], 1)
                    nc.scalar.activation(cols(m.hidden, g.no * CH, CH), ps_h[p][:, :], ACT.Identity, bias=b1[:, 0:1]).then_inc(q["h_kept"][p], 1)

            in_pairs(act, NCH, run)

        @block.vector
        def _(v):
            step = Chain(v, one["step"], 0)
            for par in range(2):
                v.sem_inc(q["xm_done"][par], 1)
                v.sem_inc(q["table_ready"][par], 1)
            nc.vector.tensor_reduce(part[:, :], m.sums[:, 0:NCH], AX, ALU.add).then_inc(one["part_ready"], 1)
            v.wait_ge(one["w_in"], 80)
            v.wait_ge(one["totalled"], 1)
            step(nc.vector.tensor_scalar(total[:, :], total[:, :], 1.0 / z.nodes, None, ALU.mult))
            step(nc.vector.tensor_tensor(w_a[:, :], w_a[:, :], w_b[:, :], ALU.add))
            step(nc.vector.tensor_tensor(w_a[:, :], w_a[:, :], total[:, :], ALU.mult))
            step(nc.vector.tensor_tensor(b1[:, :], w_a[:, :], b_lin[:, :], ALU.add))
            v.sem_inc(one["b_ready"], 1)

            def run(gs):
                for g in gs:
                    v.wait_ge(q["xm_done"][g.par], g.rnd + 2)
                    v.wait_ge(q["stored"][g.par], g.rnd * 16 + 16)
                    nc.vector.tensor_copy(tab[:, g.par, :, :], ps_x[g.par][:, :, :]).then_inc(q["table_ready"][g.par], 1)

            in_pairs(v, NCH, run)


def last_nodes(nc, z, m, ins, out_dram):
    NCH = z.chunks
    with Phase(nc) as ctx:
        ph = NodePhase(nc, ctx, "nl")
        w, bias = ph.sb("w", [D, D]), ph.sb("bias", [P, D])
        x, ht, y, out = ph.sb2("x", [P, CT, D]), ph.sb2("ht", [D, CH]), ph.sb2("y", [P, CT, D]), ph.sb2("out", [P, CT, D])
        ps = ph.ps2("ps", [P, CT, D])
        norm = Norm(nc, ph)
        w_in, storing = ph.sem("w_in"), ph.sem("storing")
        q = {n: ph.sem2(n) for n in ("x_in", "x_read", "taken", "product", "normed", "stored", "out_free", "step")}
        block = ctx.enter_context(nc.Block())
        PER = 3 + LN_STEPS

        @block.sync
        def _(sp):
            sp.dma_start(w[:, :], ins["L3_gnn_out_w"]).then_inc(w_in, 16)
            sp.dma_start(bias[:, :], ins["L3_gnn_out_b"].partition_broadcast(P)).then_inc(w_in, 16)

            def run(gs):
                for g in gs:
                    sp.wait_ge(q["x_read"][g.par], g.rnd + 1)
                    sp.dma_start(x[:, g.par, :, :], rows(m.x3, g.no)).then_inc(q["x_in"][g.par], 16)

            in_pairs(sp, NCH, run)

        @block.gpsimd
        def _(pool):
            for par in range(2):
                pool.sem_inc(q["out_free"][par], 1)

            def store(gs):
                for g in gs:
                    pool.wait_ge(q["normed"][g.par], g.rnd + 1)
                    pool.sem_inc(storing, 1)
                    pool.dma_start(rows(out_dram, g.no), out[:, g.par, :, :]).then_inc(q["stored"][g.par], 16)
                for g in gs:
                    pool.wait_ge(q["stored"][g.par], g.rnd * 16 + 16)
                    pool.sem_inc(q["out_free"][g.par], 1)

            whole = (NCH - 1) // 2 * 2
            if whole:
                with pool.Fori(0, whole // 2) as b:
                    store([Group(b * 2, 0, b), Group(b * 2 + 1, 1, b)])
            if whole < NCH - 1:
                store([Group(NCH - 2, 0, whole // 2)])
            par = (NCH - 1) % 2
            pool.wait_ge(q["normed"][par], rounds(NCH, par))
            n = rounds(NCH, par) - 1
            for k in range(CT):
                at = (NCH - 1) * CH + k * P
                real = min(P, z.nodes - at)
                if real > 0:
                    pool.dma_start(out_dram[at:at + real, :], out[0:real, par, k, :]).then_inc(q["stored"][par], 16)
                    n += 1
            pool.wait_ge(q["stored"][par], 16 * n)

        @block.tensor
        def _(pe):
            for par in range(2):
                pe.sem_inc(q["product"][par], 1)
            pe.wait_ge(w_in, 32)

            def run(gs):
                for g in gs:
                    p = g.par
                    pe.wait_ge(q["taken"][p], g.rnd + 1)
                    pe.wait_ge(q["x_read"][p], g.rnd + 1)
                    for k in range(CT):
                        last = nc.tensor.matmul(ps[p][:, k, :], ht[:, p, k * P:(k + 1) * P], w[:, :], start=True, stop=True)
                    last.then_inc(q["product"][p], 1)

            in_pairs(pe, NCH, run)

        @block.scalar
        def _(act):
            def run(gs):
                for g in gs:
                    act.wait_ge(q["product"][g.par], g.rnd + 1)
                    nc.scalar.copy(ht[:, g.par, :], cols(m.hidden, g.no * CH, CH)).then_inc(q["taken"][g.par], 1)
                for g in gs:
                    norm.scalar(act, g)

            in_pairs(act, NCH, run)

        @block.vector
        def _(v):
            for par in range(2):
                v.sem_inc(q["x_read"][par], 1)
            v.wait_ge(w_in, 32)

            def run(gs):
                steps = [Chain(v, q["step"][g.par], g.rnd * PER, PER) for g in gs]
                for g, step in zip(gs, steps):
                    p = g.par
                    v.wait_ge(q["product"][p], g.rnd + 2)
                    step(nc.vector.tensor_tensor(y[:, p, :, :], ps[p][:, :, :], bias[:, :].unsqueeze(1).to_broadcast([P, CT, D]), ALU.add))
                    step(nc.vector.tensor_scalar(y[:, p, :, :], y[:, p, :, :], 0.0, None, ALU.max))
                    v.wait_ge(q["x_in"][p], g.rnd * 16 + 16)
                    step(nc.vector.tensor_tensor(y[:, p, :, :], y[:, p, :, :], x[:, p, :, :], ALU.add))
                    v.sem_inc(q["x_read"][p], 1)
                    norm.moments(v, step, g, y)
                for g, step in zip(gs, steps):
                    p = g.par
                    v.wait_ge(q["out_free"][p], g.rnd + 1)
                    norm.apply(v, step, g, y, out)
                    v.sem_inc(q["normed"][p], 1)
                    step.done()

            in_pairs(v, NCH, run)


def build(nc, z, ins, out, layers):
    class M:
        pass

    m = M()
    with ExitStack() as ctx:
        def sb(name, shape, dt=F32):
            return ctx.enter_context(nc.sbuf_tensor(name, shape, dt))

        NT, NP = z.tiles, z.padded
        m.ident, m.lane = sb("ident", [P, P]), sb("lane", [P, P])
        m.lane_bf, m.ones = sb("lane_bf", [P, P], BF16), sb("ones", [P, P])
        m.src_idx, m.dst_idx = sb("src_idx", [P, NT], I32), sb("dst_idx", [P, NT], I32)
        m.loc, m.last, m.w = sb("loc", [P, NT]), sb("last", [P, NT]), sb("w", [P, NT])
        m.base_row = sb("base_row", [1, z.groups * QPG], I32)
        m.acc = sb("acc", [P, z.cols])
        m.side = m.hidden = sb("side", [P, max(z.cols, 5 * 2 * GE)])
        m.deg, m.scale = sb("deg", [P, 3, z.node_tiles]), sb("scale", [P, 3, z.node_tiles])

        m.x0, m.x1, m.x2, m.x3 = (nc.dram_tensor(f"x{i}", [NP, D], F32) for i in range(4))
        m.table0, m.table1, m.table3 = (nc.dram_tensor(f"table{i}", [NP, D], F32) for i in (0, 1, 3))
        m.dst_pad = nc.dram_tensor("dst_pad", [z.groups, GE], I32)
        m.bases = nc.dram_tensor("bases", [z.groups, QPG], I32)
        m.counts = nc.dram_tensor("counts", [1, NP], F32)

        m.resets4 = nc.dram_tensor("resets4", [z.groups, HEADS * GE], F32)
        m.table2 = nc.dram_tensor("table2", [NP, ROW2], F32)
        m.dst_terms = nc.dram_tensor("dst_terms", [NP, 2 * HEADS], F32)
        m.stash = nc.dram_tensor("stash", [z.groups * P, G * ROW2], F32)
        m.att, m.p_self = sb("att", [P, z.node_tiles, 2 * HEADS]), sb("p_self", [P, z.node_tiles, HEADS])
        m.low, m.sums = sb("low", [P, 1]), sb("sums", [P, z.chunks])

        with ExitStack() as early:
            m.src_lo, m.src_hi = (early.enter_context(nc.sbuf_tensor(n, [P, NT], F32)) for n in ("src_lo", "src_hi"))
            prepare(nc, z, m, ins)
            out_degrees(nc, z, m)
            inverse_roots(nc, z, m, range(0, 1))
            scale_rows(nc, z, m)
            sum_over_edges(nc, z, m, m.table0, None, "e0", degrees=True)
        inverse_roots(nc, z, m, range(1, 3))
        layer0_nodes(nc, z, m, ins)
        if layers == 1:
            return dump(nc, z, m.x1, out)
        sum_over_edges(nc, z, m, m.table1, m.w, "e1")
        layer1_nodes(nc, z, m, ins)
        if layers == 2:
            return dump(nc, z, m.x2, out)
        lowest_source(nc, z, m)
        highest_source(nc, z, m)
        attention_nodes(nc, z, m)
        weighted_sum(nc, z, m)
        layer2_nodes(nc, z, m, ins)
        if layers == 3:
            return dump(nc, z, m.x3, out)
        cutoffs(nc, z, m)
        continuous_conv(nc, z, m, ins, 0)
        conv_nodes(nc, z, m, ins, 0)
        next_messages(nc, z, m, ins)
        continuous_conv(nc, z, m, ins, 1)
        conv_nodes(nc, z, m, ins, 1)
        last_nodes(nc, z, m, ins, out)


def dump(nc, z, x, out):
    with nc.semaphore("dumped") as s, nc.Block() as block:
        @block.sync
        def _(sp):
            sp.dma_start(out, x[0:z.nodes, :]).then_inc(s, 16)
            sp.wait_ge(s, 16)


LAYERS = 4


def kernel(**inputs):
    import concourse.bacc as bacc
    from concourse.bass_utils import run_bass_kernel_spmd as run

    z = Sizes(inputs["x"].shape[0], inputs["src"].shape[0], inputs["edge_attr_50"].shape[1])
    nc = bacc.Bacc("TRN2", target_bir_lowering=False, num_devices=1)
    arrays, ins = {}, {}
    for name, a in inputs.items():
        a = np.ascontiguousarray(a)
        arrays[f"in_{name}"] = a
        ins[name] = nc.dram_tensor(f"in_{name}", a.shape, mybir.dt.from_np(a.dtype), kind="ExternalInput").ap()
    out = nc.dram_tensor("out", [z.nodes, D], F32, kind="ExternalOutput").ap()
    build(nc, z, ins, out, LAYERS)
    return run(nc, [arrays], core_ids=[0]).results[0]["out"]
```
